# Optimizing a Trainium2 kernel written in Bass

```python
import numpy as np
import jax
import jax.numpy as jnp

def _softmax(x, axis=-1):
    return jax.nn.softmax(x, axis=axis)

def _gelu(x):
    return jax.nn.gelu(x, approximate=True)

def _silu(x):
    return jax.nn.silu(x)

def _sigmoid(x):
    return jax.nn.sigmoid(x)

def _layernorm(x, axis=-1, eps=1e-05):
    m = jnp.mean(x, axis=axis, keepdims=True)
    v = jnp.var(x, axis=axis, keepdims=True)
    return (x - m) / jnp.sqrt(v + eps)

def _scatter_add(tgt, idx, src, axis=0):
    return tgt.at[idx].add(src)

def _segment_sum(src, seg, n):
    return jax.ops.segment_sum(src, seg, n)
kernel_name = 'mk_adaln_d1_jaxref_r4_fb3e24'

def setup_inputs(seed: int=0):
    np.random.seed(seed)
    _w = jnp.asarray

    def _L0_attn_setup():
        import jax, jax.numpy as jnp
        import numpy as np
        HIDDEN = 512
        N_HEADS = 16
        HEAD_DIM = HIDDEN // N_HEADS
        ROTARY_DIM = 32
        ROPE_BASE = 10000.0
        NEG_INF = -10000.0

        def _rope_cos_sin(seqlen, dtype):
            inv_freq = 1.0 / ROPE_BASE ** (jnp.arange(0, ROTARY_DIM, 2, dtype=jnp.float32) / ROTARY_DIM)
            t = jnp.arange(seqlen, dtype=jnp.float32)
            freqs = jnp.outer(t, inv_freq)
            return (jnp.cos(freqs).astype(dtype), jnp.sin(freqs).astype(dtype))

        def _apply_rotary(u, cos, sin):
            u_rot, u_pass = (u[..., :ROTARY_DIM], u[..., ROTARY_DIM:])
            u1, u2 = (u_rot[..., :ROTARY_DIM // 2], u_rot[..., ROTARY_DIM // 2:])
            c = cos[None, :, None, :]
            s = sin[None, :, None, :]
            rot = jnp.concatenate([u1 * c - u2 * s, u1 * s + u2 * c], axis=-1)
            return jnp.concatenate([rot, u_pass], axis=-1)
        key = jax.random.key(seed)
        k1, k2, k3 = jax.random.split(key, 3)
        x = jax.random.normal(k1, (2, 512, HIDDEN), dtype=jnp.float32)
        Wqkv_w = jax.random.normal(k2, (3 * HIDDEN, HIDDEN), dtype=jnp.float32) * (1.0 / np.sqrt(HIDDEN))
        Wqkv_b = jax.random.normal(k3, (3 * HIDDEN,), dtype=jnp.float32) * 0.01
        return {'x': x, 'Wqkv_w': Wqkv_w, 'Wqkv_b': Wqkv_b}
    _L0_attn_in = _L0_attn_setup()

    def _L0_ffn_setup():
        import jax, jax.numpy as jnp
        import numpy as np
        HIDDEN = 512
        NUM_EXPERTS = 32
        TOP_K = 4
        MOE_INTER = 192
        GROUP = 2
        NUM_CHUNK = NUM_EXPERTS // GROUP
        CHUNK_INTER = 128
        SMALL_SCALE = 0.05

        def _routing(x2d, gate_w):
            logits = x2d @ gate_w.T
            rw = jax.nn.softmax(logits.astype(jnp.float32), axis=-1)
            scores = jax.nn.sigmoid(logits.astype(jnp.float32))
            _, sel = jax.lax.top_k(scores, TOP_K)
            w = jnp.take_along_axis(rw, sel, axis=-1)
            w = w / w.sum(axis=-1, keepdims=True)
            return (w.astype(x2d.dtype), sel)

        def _moe(x2d, Wg, Wu, Wd, cw):
            g = jnp.einsum('th,ehi->eti', x2d, Wg)
            u = jnp.einsum('th,ehi->eti', x2d, Wu)
            a = jax.nn.silu(g) * u * cw.T[:, :, None]
            return jnp.einsum('eti,eih->th', a, Wd)
        key = jax.random.key(seed)
        ks = jax.random.split(key, 8)
        s = 0.02
        B, S = (2, 512)
        return {'hidden_states': jax.random.normal(ks[0], (B, S, HIDDEN), jnp.float32), 'gate_w': jax.random.normal(ks[1], (NUM_EXPERTS, HIDDEN), jnp.float32) * s, 'Wg': jax.random.normal(ks[2], (NUM_EXPERTS, HIDDEN, MOE_INTER), jnp.float32) * s, 'Wu': jax.random.normal(ks[3], (NUM_EXPERTS, HIDDEN, MOE_INTER), jnp.float32) * s, 'Wd': jax.random.normal(ks[4], (NUM_EXPERTS, MOE_INTER, HIDDEN), jnp.float32) * s, 'cWg': jax.random.normal(ks[5], (NUM_CHUNK, HIDDEN, CHUNK_INTER), jnp.float32) * s, 'cWu': jax.random.normal(ks[6], (NUM_CHUNK, HIDDEN, CHUNK_INTER), jnp.float32) * s, 'cWd': jax.random.normal(ks[7], (NUM_CHUNK, CHUNK_INTER, HIDDEN), jnp.float32) * s}
    _L0_ffn_in = _L0_ffn_setup()
    _L0_c = _w((lambda *s: np.random.randn(*s).astype(np.float32) * 0.05)(1, 512))
    _L0_wmod = _w((lambda *s: np.random.randn(*s).astype(np.float32) * 0.05)(512, 6 * 512) * 512 ** (-0.5))
    _d = {'L0_attn_x': _L0_attn_in['x'], 'L0_attn_Wqkv_w': _L0_attn_in['Wqkv_w'], 'L0_attn_Wqkv_b': _L0_attn_in['Wqkv_b'], 'L0_ffn_gate_w': _L0_ffn_in['gate_w'], 'L0_ffn_Wg': _L0_ffn_in['Wg'], 'L0_ffn_Wu': _L0_ffn_in['Wu'], 'L0_ffn_Wd': _L0_ffn_in['Wd'], 'L0_ffn_cWg': _L0_ffn_in['cWg'], 'L0_ffn_cWu': _L0_ffn_in['cWu'], 'L0_ffn_cWd': _L0_ffn_in['cWd'], 'L0_c': _L0_c, 'L0_wmod': _L0_wmod}
    _x0 = _d['L0_attn_x']
    _d['L0_attn_x'] = jax.random.normal(jax.random.fold_in(jax.random.key(seed), 1), (1, 2048, 512), dtype=_x0.dtype)
    del _x0
    return _d

def reference(L0_attn_x, L0_attn_Wqkv_w, L0_attn_Wqkv_b, L0_ffn_gate_w, L0_ffn_Wg, L0_ffn_Wu, L0_ffn_Wd, L0_ffn_cWg, L0_ffn_cWu, L0_ffn_cWd, L0_c, L0_wmod):

    def _L0_attn_ref(x, Wqkv_w, Wqkv_b):
        import jax, jax.numpy as jnp
        import numpy as np
        HIDDEN = 512
        N_HEADS = 16
        HEAD_DIM = HIDDEN // N_HEADS
        ROTARY_DIM = 32
        ROPE_BASE = 10000.0
        NEG_INF = -10000.0

        def _rope_cos_sin(seqlen, dtype):
            inv_freq = 1.0 / ROPE_BASE ** (jnp.arange(0, ROTARY_DIM, 2, dtype=jnp.float32) / ROTARY_DIM)
            t = jnp.arange(seqlen, dtype=jnp.float32)
            freqs = jnp.outer(t, inv_freq)
            return (jnp.cos(freqs).astype(dtype), jnp.sin(freqs).astype(dtype))

        def _apply_rotary(u, cos, sin):
            u_rot, u_pass = (u[..., :ROTARY_DIM], u[..., ROTARY_DIM:])
            u1, u2 = (u_rot[..., :ROTARY_DIM // 2], u_rot[..., ROTARY_DIM // 2:])
            c = cos[None, :, None, :]
            s = sin[None, :, None, :]
            rot = jnp.concatenate([u1 * c - u2 * s, u1 * s + u2 * c], axis=-1)
            return jnp.concatenate([rot, u_pass], axis=-1)
        B, S, _ = x.shape
        qkv = jnp.einsum('bse,oe->bso', x, Wqkv_w) + Wqkv_b
        qkv = qkv.reshape(B, S, 3, N_HEADS, HEAD_DIM)
        cos, sin = _rope_cos_sin(S, x.dtype)
        q = _apply_rotary(qkv[:, :, 0], cos, sin)
        k = _apply_rotary(qkv[:, :, 1], cos, sin)
        v = qkv[:, :, 2]
        scale = 1.0 / np.sqrt(HEAD_DIM)
        scores = jnp.einsum('bthd,bshd->bhts', q, k * scale)
        causal_mask = jnp.triu(jnp.full((S, S), NEG_INF, dtype=scores.dtype), 1)
        scores = scores + causal_mask
        attn = jax.nn.softmax(scores, axis=-1)
        out = jnp.einsum('bhts,bshd->bthd', attn, v)
        return out.reshape(B, S, N_HEADS * HEAD_DIM)

    def _L0_ffn_ref(hidden_states, gate_w, Wg, Wu, Wd, cWg, cWu, cWd):
        import jax, jax.numpy as jnp
        import numpy as np
        HIDDEN = 512
        NUM_EXPERTS = 32
        TOP_K = 4
        MOE_INTER = 192
        GROUP = 2
        NUM_CHUNK = NUM_EXPERTS // GROUP
        CHUNK_INTER = 128
        SMALL_SCALE = 0.05

        def _routing(x2d, gate_w):
            logits = x2d @ gate_w.T
            rw = jax.nn.softmax(logits.astype(jnp.float32), axis=-1)
            scores = jax.nn.sigmoid(logits.astype(jnp.float32))
            _, sel = jax.lax.top_k(scores, TOP_K)
            w = jnp.take_along_axis(rw, sel, axis=-1)
            w = w / w.sum(axis=-1, keepdims=True)
            return (w.astype(x2d.dtype), sel)

        def _moe(x2d, Wg, Wu, Wd, cw):
            g = jnp.einsum('th,ehi->eti', x2d, Wg)
            u = jnp.einsum('th,ehi->eti', x2d, Wu)
            a = jax.nn.silu(g) * u * cw.T[:, :, None]
            return jnp.einsum('eti,eih->th', a, Wd)
        B, S, H = hidden_states.shape
        T = B * S
        x = hidden_states.reshape(T, H)
        w, sel = _routing(x, gate_w)
        rows = jnp.arange(T)[:, None]
        cw_large = jnp.zeros((T, NUM_EXPERTS), x.dtype).at[rows, sel].add(w)
        cw_small = jnp.zeros((T, NUM_CHUNK), x.dtype).at[rows, sel // GROUP].add(w)
        large = _moe(x, Wg, Wu, Wd, cw_large)
        small = _moe(x, cWg, cWu, cWd, cw_small)
        return (large + SMALL_SCALE * small).reshape(B, S, H)
    x = L0_attn_x
    mod = (_silu(L0_c) @ L0_wmod).reshape(L0_c.shape[0], 6, 1, -1)
    sa, ca, ga, sb, cb, gb = (mod[:, 0], mod[:, 1], mod[:, 2], mod[:, 3], mod[:, 4], mod[:, 5])
    ga = (2 * (ga >= 0) - 1) * jnp.maximum(jnp.abs(ga), 0.25)
    gb = (2 * (gb >= 0) - 1) * jnp.maximum(jnp.abs(gb), 0.25)
    h = _layernorm(x, axis=-1) * (1 + ca) + sa
    x = x + ga * _L0_attn_ref(h, L0_attn_Wqkv_w, L0_attn_Wqkv_b)
    h = _layernorm(x, axis=-1) * (1 + cb) + sb
    x = x + gb * _L0_ffn_ref(h, L0_ffn_gate_w, L0_ffn_Wg, L0_ffn_Wu, L0_ffn_Wd, L0_ffn_cWg, L0_ffn_cWu, L0_ffn_cWd)
    return x

_drawn_inputs = setup_inputs


def setup_inputs(seed=0):
    import zlib

    import numpy as np

    out = dict(_drawn_inputs(seed))
    spreads = {}
    factors = {'L0_attn_Wqkv_b': 8.0,
     'L0_ffn_gate_w': 8.0,
     'L0_ffn_Wg': 8.0,
     'L0_ffn_Wu': 8.0,
     'L0_ffn_Wd': 8.0,
     'L0_ffn_cWg': 8.0,
     'L0_ffn_cWu': 8.0,
     'L0_ffn_cWd': 8.0}
    for name, (base, spread) in spreads.items():
        noise = np.random.default_rng([zlib.crc32(name.encode()), seed]).standard_normal(out[name].shape)
        drawn = base * np.exp(spread * noise) if base else spread * noise
        out[name] = jnp.asarray(drawn.astype(out[name].dtype))
    for name, factor in factors.items():
        out[name] = (out[name] * factor).astype(out[name].dtype)
    return out
```

```python
from contextlib import ExitStack

import numpy as np
import concourse.bass as bass
from concourse import mybir

F32 = mybir.dt.float32
F32R = mybir.dt.float32r
F16 = mybir.dt.float16
I32 = mybir.dt.int32
U32 = mybir.dt.uint32
ALU = mybir.AluOpType
ACT = mybir.ActivationFunctionType
AX = mybir.AxisListType

P = 128
T, D = 2048, 512
H, DH = 16, 32
KT = D // P
TT = T // P
CH = 512
NCH = T // CH
EPS = 1e-5
WSLOTS = 4
SWAP = [(i + DH // 2) % DH for i in range(DH)]


def wait_apart(eng, sem, value, passed):
    value = eng.to_reg(value)
    eng.wait_ge(passed, 1)
    eng.wait_ge(sem, value)


def modulation_and_projection(nc, d, keep):
    with ExitStack() as ctx:
        sb = lambda name, shape, dt=F32: ctx.enter_context(nc.sbuf_tensor(name, shape, dt))
        sem = lambda name: ctx.enter_context(nc.semaphore(name))
        pb = lambda name: ctx.enter_context(nc.psum_tensor(name, [P, CH], F32))

        wmod = sb("wmod_sb", [P, WSLOTS, KT, D])
        c_col = sb("c_col", [P, KT])
        silu_c = sb("silu_c", [P, KT])
        silu_cb = sb("silu_cb", [P, KT, P])
        floor_t = sb("floor_t", [P, 2, D])
        w_qkv = sb("w_qkv", [P, KT, 3 * D])
        b_qk = sb("b_qk", [P, 8])
        b_v = sb("b_v", [P, D])
        cos_t = sb("cos_t", [P, T])
        sin_t = sb("sin_t", [P, T])
        x_n = sb("x_n", [P, 4, D])
        stats = sb("stats", [P, 4, 6])
        meanvar = sb("meanvar", [P, 4, 2])
        std = sb("std", [P, 4])
        rstd = sb("rstd", [P, 4])
        h_t = sb("h_t", [P, 2, KT, CH])
        biased = sb("biased", [P, 2, CH])
        swapped = sb("swapped", [P, 2, CH])
        by_cos = sb("by_cos", [P, 2, CH])
        rotated = sb("rotated", [P, 2, CH])
        part_hi = sb("part_hi", [P, 2, CH], F32R)
        part_lo = sb("part_lo", [P, 2, CH], F32R)
        eps_col = sb("eps_col", [P, 1])
        tp = [pb(f"tp{i}") for i in range(2)]
        pj = [pb(f"pj{i}") for i in range(4)]
        pm = [pb(f"pm{i}") for i in range(2)]
        ident, mod_col, gate_row, v_all, x_all = (keep[n] for n in ("ident", "mod_col", "gate_row", "v_all", "x_all"))

        s_small = sem("small_loaded")
        s_wmod = [sem(f"wmod{g}_loaded") for g in range(6)]
        s_w = sem("w_loaded")
        s_tab = sem("tables_loaded")
        s_x0 = sem("x_first_loaded")
        s_x = sem("x_rest_loaded")
        s_const = sem("constants_set")
        s_silu = sem("silu_done")
        s_sb = sem("silu_spread")
        s_mod = sem("mod_done")
        s_modc = sem("mod_copied")
        s_flo = sem("gate_floor")
        s_st = sem("stats_done")
        s_mv = sem("meanvar_done")
        s_std = sem("std_done")
        s_rs = sem("rstd_done")
        s_xn = sem("x_n_done")
        s_tp = sem("transposed")
        s_ht = sem("h_t_done")
        s_pj = sem("projected")
        s_bi = sem("biased_done")
        s_v = sem("v_done")
        s_sw = sem("swapped_done")
        s_sw2 = sem("sin_done")
        s_cos = sem("cos_done")
        s_rot = sem("rotated_done")
        s_hi = sem("hi_done")
        s_lo = sem("lo_done")
        s_store = [sem(f"parts{i}_stored") for i in range(2)]

        GROUPS = [0, 1, 3, 4, 2, 5]
        JOBS = 8

        block = ctx.enter_context(nc.Block())

        @block.sync
        def _(sp):
            sp.dma_start(c_col[:, :], d["c_col"]).then_inc(s_small, 16)
            sp.dma_start(b_qk[:, :], d["b_qk"]).then_inc(s_small, 16)
            sp.dma_start(b_v[:, :], d["b_v"].partition_broadcast(P)).then_inc(s_small, 16)
            wm = d["wmod"].rearrange("(k p) (g n) -> g p k n", p=P, n=D)
            xs = d["x"].rearrange("(c t p) n -> c p t n", p=P, t=4)
            sp.dma_start(x_all[:, 0:4], xs[0]).then_inc(s_x0, 16)
            for i, g in enumerate(GROUPS[:2]):
                sp.dma_start(wmod[:, i], wm[g]).then_inc(s_wmod[g], 16)
            w_view = d["w_t"].rearrange("(k p) n -> p k n", p=P)
            for n in range(3):
                sp.dma_start(w_qkv[:, :, n * D:(n + 1) * D], w_view[:, :, n * D:(n + 1) * D]).then_inc(s_w, 16)
            for r in range(4):
                sp.dma_start(cos_t[DH * r:DH * r + DH, :], d["cos"]).then_inc(s_tab, 16)
                sp.dma_start(sin_t[DH * r:DH * r + DH, :], d["sin"]).then_inc(s_tab, 16)
            for c in range(1, NCH):
                sp.dma_start(x_all[:, 4 * c:4 * c + 4], xs[c]).then_inc(s_x, 16)
            for i, g in enumerate(GROUPS[2:], 2):
                if i >= WSLOTS:
                    sp.wait_ge(s_mod, i - WSLOTS + 1)
                sp.dma_start(wmod[:, i % WSLOTS], wm[g]).then_inc(s_wmod[g], 16)
            with sp.Fori(0, NCH) as c:
                for j in range(JOBS):
                    s, o = divmod(j, KT)
                    rows = slice(o * P, (o + 1) * P)
                    sp.wait_ge(s_hi, c * JOBS + j + 1)
                    sp.dma_start(d["qk_parts"][0, s, rows, bass.ds(c * CH, CH)], part_hi[:, j % 2].bitcast(F32)).then_inc(s_store[j % 2], 16)
                    sp.wait_ge(s_lo, c * JOBS + j + 1)
                    sp.dma_start(d["qk_parts"][1, s, rows, bass.ds(c * CH, CH)], part_lo[:, j % 2].bitcast(F32)).then_inc(s_store[j % 2], 16)
            for b in range(2):
                sp.wait_ge(s_store[b], NCH * JOBS * 16)

        @block.gpsimd
        def _(pool):
            nc.gpsimd.memset(ident[:, :], 0.0).then_inc(s_const, 1)
            pool.wait_ge(s_const, 1)
            nc.gpsimd.affine_select(out=ident[:, :], in_=ident[:, :], compare_op=ALU.not_equal, fill=1.0,
                                    base=0, pattern=[[-1, P]], channel_multiplier=1).then_inc(s_const, 1)
            nc.gpsimd.memset(v_all[:, :, :, DH:DH + 1], 1.0).then_inc(s_const, 1)
            nc.gpsimd.memset(eps_col[:, :], EPS).then_inc(s_const, 1)
            pool.wait_ge(s_silu, 1)
            nc.gpsimd.tensor_copy(silu_cb[:, :, :], silu_c[:, :].unsqueeze(2).to_broadcast([P, KT, P])).then_inc(s_sb, 1)
            pool.wait_ge(s_tab, 16 * 8)
            with pool.Fori(0, NCH) as c:
                for j in range(JOBS):
                    wait_apart(pool, s_bi, c * JOBS + j + 1, s_tab)
                    if j >= 2:
                        pool.wait_ge(s_rot, c * JOBS + j - 1)
                    nc.gpsimd.tensor_tensor(by_cos[:, j % 2], biased[:, j % 2], cos_t[:, bass.ds(c * CH, CH)],
                                            ALU.mult).then_inc(s_cos, 1)
                pool.wait_ge(s_rot, c * JOBS + JOBS)

        @block.scalar
        def _(act):
            act.wait_ge(s_small, 48)
            nc.scalar.activation(silu_c[:, :], c_col[:, :], ACT.Silu).then_inc(s_silu, 1)
            act.wait_ge(s_const, 4)

            with act.Fori(0, NCH // 2) as pair:
                for b in range(2):
                    c = pair * 2 + b
                    act.wait_ge(s_mv, c + 1)
                    nc.scalar.activation(std[:, :], meanvar[:, :, 1], ACT.Sqrt, bias=eps_col[:, :]).then_inc(s_std, 1)
                    for k in range(KT):
                        act.wait_ge(s_tp, c * KT + k + 1)
                        if k == 0:
                            act.wait_ge(s_modc, 2)
                        nc.scalar.activation(h_t[:, b, k], tp[k % 2][:, :], ACT.Identity, bias=mod_col[:, 0, k:k + 1],
                                             scale=mod_col[:, 1, k:k + 1]).then_inc(s_ht, 1)
                    for j in range(JOBS):
                        act.wait_ge(s_pj, c * 12 + j + 1)
                        if j >= 2:
                            act.wait_ge(s_cos, c * JOBS + j - 1)
                            act.wait_ge(s_sw, c * JOBS + j - 1)
                        nc.scalar.activation(biased[:, j % 2], pj[j % 4][:, :], ACT.Identity,
                                             bias=b_qk[:, j:j + 1]).then_inc(s_bi, 1)
                        act.wait_ge(s_rot, c * JOBS + j + 1)
                        if j >= 2:
                            act.wait_ge(s_store[j % 2], (c * (JOBS // 2) + j // 2) * 32)
                        nc.scalar.activation(part_hi[:, j % 2], rotated[:, j % 2], ACT.Copy).then_inc(s_hi, 1)
                    for p in range(2):
                        act.wait_ge(s_store[p], (c + 1) * (JOBS * 16))

        @block.vector
        def _(dve):
            def gate(i, g):
                dve.wait_ge(s_mod, 5 + i)
                nc.vector.tensor_scalar(floor_t[:, 0], pm[i][:, :], -1.0, 0.25, ALU.mult, ALU.max).then_inc(s_flo, 1)
                nc.vector.tensor_scalar(floor_t[:, 1], pm[i][:, :], 0.25, None, ALU.max).then_inc(s_flo, 1)
                dve.wait_ge(s_flo, 6 * i + 2)
                nc.vector.tensor_tensor(floor_t[:, 1], floor_t[:, 1], floor_t[:, 0], ALU.max).then_inc(s_flo, 1)
                dve.wait_ge(s_flo, 6 * i + 3)
                nc.vector.tensor_scalar(floor_t[:, 0], pm[i][:, :], 0.0, 2.0, ALU.is_ge, ALU.mult).then_inc(s_flo, 1)
                dve.wait_ge(s_flo, 6 * i + 4)
                nc.vector.tensor_scalar(floor_t[:, 0], floor_t[:, 0], -1.0, None, ALU.add).then_inc(s_flo, 1)
                dve.wait_ge(s_flo, 6 * i + 5)
                nc.vector.tensor_tensor(gate_row[:, i], floor_t[:, 0], floor_t[:, 1], ALU.mult).then_inc(s_flo, 1)
                dve.wait_ge(s_flo, 6 * i + 6)

            def ln(c, b):
                if b == 1:
                    dve.wait_ge(s_x, (NCH - 1) * 16)
                for t in range(4):
                    nc.vector.bn_stats(stats[:, t], x_all[:, bass.ds(c * 4 + t, 1)].rearrange("p o n -> p (o n)")).then_inc(s_st, 1)
                for t in range(4):
                    wait_apart(dve, s_st, c * 4 + t + 1, s_x0)
                    last = nc.vector.bn_aggr(meanvar[:, t], stats[:, t])
                last.then_inc(s_mv, 1)
                dve.wait_ge(s_std, c + 1)
                nc.vector.reciprocal(rstd[:, :], std[:, :]).then_inc(s_rs, 1)
                dve.wait_ge(s_rs, c + 1)
                for t in range(4):
                    last = nc.vector.tensor_scalar(x_n[:, t], x_all[:, bass.ds(c * 4 + t, 1)].rearrange("p o n -> p (o n)"), meanvar[:, t, 0:1], rstd[:, t:t + 1],
                                                   ALU.subtract, ALU.mult)
                    last.then_inc(s_xn, 1)

            for i, g in enumerate(GROUPS[:4]):
                dve.wait_ge(s_mod, i + 1)
                nc.vector.tensor_scalar(mod_col[:, i], pm[i % 2][:, 0:KT], 1.0 if i % 2 else 0.0, None,
                                        ALU.add).then_inc(s_modc, 1)

            dve.wait_ge(s_x0, 16)
            with dve.Fori(0, NCH // 2) as pair:
                for b in range(2):
                    c = pair * 2 + b
                    ln(c, b)
                    for j in range(JOBS):
                        n = c * JOBS + j
                        wait_apart(dve, s_bi, n + 1, s_x0)
                        if j >= 2:
                            dve.wait_ge(s_rot, n - 1)
                        nc.vector.stream_shuffle(swapped[:, j % 2], biased[:, j % 2], SWAP).then_inc(s_sw, 1)
                        dve.wait_ge(s_sw, n + 1)
                        nc.vector.tensor_tensor(swapped[:, j % 2], swapped[:, j % 2], sin_t[:, bass.ds(c * CH, CH)],
                                                ALU.mult).then_inc(s_sw2, 1)
                        dve.wait_ge(s_sw2, n + 1)
                        dve.wait_ge(s_cos, n + 1)
                        if j >= 2:
                            dve.wait_ge(s_lo, n - 1)
                            dve.wait_ge(s_hi, n - 1)
                        nc.vector.tensor_tensor(rotated[:, j % 2], by_cos[:, j % 2], swapped[:, j % 2],
                                                ALU.add).then_inc(s_rot, 1)
                        dve.wait_ge(s_hi, n + 1)
                        if j >= 2:
                            dve.wait_ge(s_store[j % 2], (c * (JOBS // 2) + j // 2) * 32)
                        nc.vector.tensor_tensor(part_lo[:, j % 2], rotated[:, j % 2], part_hi[:, j % 2],
                                                ALU.subtract).then_inc(s_lo, 1)
                    for t in range(4):
                        dve.wait_ge(s_pj, c * 12 + JOBS + t + 1)
                        nc.vector.tensor_tensor(v_all[:, bass.ds(c * 4 + t, 1), :, 0:DH].rearrange("p o h w -> p (o h) w"),
                                                pj[t % 4][:, :].rearrange("p (h w) -> p h w", w=DH),
                                                b_v[:, :].rearrange("p (h w) -> p h w", w=DH), ALU.add).then_inc(s_v, 1)
            gate(0, 2)
            gate(1, 5)

        @block.tensor
        def _(pe):
            pe.wait_ge(s_silu, 1)
            pe.wait_ge(s_const, 4)
            for i, g in enumerate(GROUPS[:4]):
                pe.wait_ge(s_wmod[g], 16)
                if i >= 2:
                    pe.wait_ge(s_modc, i - 1)
                for m in range(KT):
                    for k in range(KT):
                        last = nc.tensor.matmul(pm[i % 2][:, m:m + 1], wmod[:, i % WSLOTS, k, m * P:(m + 1) * P],
                                                silu_c[:, k:k + 1], start=(k == 0), stop=(k == KT - 1))
                last.then_inc(s_mod, 1)
            pe.wait_ge(s_sb, 1)
            pe.wait_ge(s_modc, 4)
            for i, g in enumerate(GROUPS[4:]):
                pe.wait_ge(s_wmod[g], 16)
                for k in range(KT):
                    last = nc.tensor.matmul(pm[i][:, :], silu_cb[:, k], wmod[:, (i + 4) % WSLOTS, k], start=(k == 0),
                                            stop=(k == KT - 1))
                last.then_inc(s_mod, 1)
            pe.wait_ge(s_w, 48)
            with pe.Fori(0, NCH // 2) as pair:
                for b in range(2):
                    c = pair * 2 + b
                    for k in range(KT):
                        pe.wait_ge(s_xn, c * 4 + 4)
                        if k >= 2:
                            pe.wait_ge(s_ht, c * KT + k - 1)
                        for t in range(4):
                            last = nc.tensor.transpose(tp[k % 2][:, t * P:(t + 1) * P], x_n[:, t, k * P:(k + 1) * P],
                                                       ident[:, :])
                        last.then_inc(s_tp, 1)
                    pe.wait_ge(s_ht, (c + 1) * KT)
                    for j in range(JOBS + 4):
                        if j >= 4:
                            pe.wait_ge(s_bi, c * JOBS + j - 3)
                        for k in range(KT):
                            if j < JOBS:
                                last = nc.tensor.matmul(pj[j % 4][:, :], w_qkv[:, k, j * P:(j + 1) * P], h_t[:, b, k],
                                                        start=(k == 0), stop=(k == KT - 1))
                            else:
                                t = j - JOBS
                                last = nc.tensor.matmul(pj[j % 4][:, :], h_t[:, b, k, t * P:(t + 1) * P],
                                                        w_qkv[:, k, 2 * D:3 * D], start=(k == 0), stop=(k == KT - 1))
                        last.then_inc(s_pj, 1)
                    pe.wait_ge(s_v, (c + 1) * 4)



PAIRS = H // 2
BLK = 2 * NCH
QK_ROWS = 3 * DH
MASK = -56576.0


def block_pairs():
    return [(h, c, kt) for h in range(2) for c in range(NCH) for kt in range(0, 4 * c + 4, 2)]


def first_query(c, kt):
    return 0 if c == 0 and kt == 1 else max(0, (kt - 4 * c) * P)


def pv_until(k):
    return 40 * (k // NCH) + 2 * (k % NCH + 1) * (k % NCH + 2)


def max_units():
    return [(i, c, CH if c < i // 4 else (i % 4 + 1) * P) for i in range(TT) for c in range(i // 4 + 1)]


SLOTS = block_pairs()
UNITS = max_units()
LAST_OF_CHUNK = [n for n, (i, c, _) in enumerate(UNITS) if i % 4 == 3 and c == i // 4]
UNIT_FROM = 6


def units_of(slot):
    span = len(SLOTS) - UNIT_FROM - 2
    return [n for n in range(len(UNITS)) if UNIT_FROM + n * span // len(UNITS) == slot]


def attention(nc, d, keep):
    with ExitStack() as ctx:
        sb = lambda name, shape, dt=F32: ctx.enter_context(nc.sbuf_tensor(name, shape, dt))
        sem = lambda name: ctx.enter_context(nc.semaphore(name))
        pb = lambda name, shape: ctx.enter_context(nc.psum_tensor(name, shape, F32))
        ident, v_all, x_all, gate_row = (keep[n] for n in ("ident", "v_all", "x_all", "gate_row"))

        rows = QK_ROWS + 2
        q_st = [[sb(f"q_st{b}{h}", [rows, T], F32R) for h in range(2)] for b in range(2)]
        k_st = [[sb(f"k_st{b}{h}", [rows, T], F32R) for h in range(2)] for b in range(2)]
        v_h = [sb(f"v_h{h}", [P, TT, DH + 1]) for h in range(2)]
        probs = sb("probs", [P, 4, CH])
        o_t = sb("o_t", [P, 2, CH])
        ident16 = sb("ident16", [P, P], F16)
        mask16 = sb("mask16", [P, P], F16)
        fold = sb("fold", [P, DH + 1])
        max_part = sb("max_part", [P, 2, TT, NCH])
        max_q = sb("max_q", [P, 2, 4])
        neg_hi = sb("neg_hi", [P, 2, 4], F32R)
        neg_cols = sb("neg_cols", [P, 2, 2, 4])
        neg_rows = sb("neg_rows", [16, 2, P], F32R)
        rden = sb("rden", [P, 4])
        out_h = sb("out_h", [P, 4, DH])
        s_bank = pb("s_bank", [P, 2, CH])
        m_bank = pb("m_bank", [P, 2, 2, CH])
        o_bank = pb("o_bank", [P, CH])
        misc = pb("misc", [P, CH])

        s_cst = sem("constants_set2")
        s_zero = sem("o_bank_zeroed")
        s_ld = [[sem(f"stack{b}{h}_loaded") for h in range(2)] for b in range(2)]
        s_vh = sem("v_head_copied")
        s_max = sem("max_scores_done")
        s_red = sem("max_reduced")
        s_mq = sem("max_of_chunk_done")
        s_nh = sem("neg_hi_done")
        s_nc = sem("neg_cols_done")
        s_mt = sem("neg_rows_transposed")
        s_mr = sem("neg_rows_copied")
        s_mrow = [sem(f"neg_rows{c}_placed") for c in range(NCH)]
        s_s = sem("scores_done")
        s_exp = sem("exp_done")
        s_mask = sem("probs_masked")
        s_pv = sem("pv_done")
        s_oe = sem("o_t_copied")
        s_comb = sem("o_folded")
        s_rd = sem("denominator_done")
        s_norm = sem("normalized")
        s_og = sem("output_gated")
        s_x2 = sem("x_added")

        block = ctx.enter_context(nc.Block())
        MASKED = [n for n, (h, c, kt) in enumerate(SLOTS) if kt >= 4 * c]

        @block.sync
        def _(sp):
            parts = d["qk_parts"]

            def load(pair, b, h):
                order = [(0, 0), (0, 1), (1, 0)] if h == 0 else [(0, 1), (0, 0), (1, 0)]
                for r, (qp, kp) in enumerate(order):
                    src = bass.ds((pair * 2 + h) * DH, DH)
                    sp.dma_start(q_st[b][h][r * DH:(r + 1) * DH, :].bitcast(F32), parts[qp, 0, src, :]).then_inc(s_ld[b][h], 16)
                    sp.dma_start(k_st[b][h][r * DH:(r + 1) * DH, :].bitcast(F32), parts[kp, 1, src, :]).then_inc(s_ld[b][h], 16)

            def place_max(pair, b, cq):
                sp.wait_ge(s_mr, pair * NCH + cq + 1)
                for h in range(2):
                    for part in range(2):
                        r = h * 8 + part * 4
                        sp.dma_start(q_st[b][h][QK_ROWS + part:QK_ROWS + part + 1, cq * CH:(cq + 1) * CH].bitcast(F32),
                                     neg_rows[r:r + 4, cq % 2, :].bitcast(F32)).then_inc(s_mrow[cq], 16)

            def step(it, s, more):
                st = 2 * it + s
                place_max(st + 1, 1 - s, 0)
                place_max(st + 1, 1 - s, 1)
                if more:
                    sp.wait_ge(s_pv, st * 80 + pv_until(3))
                    load(st + 2, s, 0)
                place_max(st + 1, 1 - s, 2)
                place_max(st + 1, 1 - s, 3)
                if more:
                    sp.wait_ge(s_pv, st * 80 + pv_until(7))
                    load(st + 2, s, 1)

            for b in range(2):
                for h in range(2):
                    load(b, b, h)
            for cq in range(NCH):
                place_max(0, 0, cq)
            with sp.Fori(0, PAIRS // 2 - 1) as it:
                for s in range(2):
                    step(it, s, True)
            step(PAIRS // 2 - 1, 0, False)
            for c in range(NCH):
                sp.wait_ge(s_mrow[c], PAIRS * 64)

        @block.gpsimd
        def _(pool):
            def copy_v(head, h):
                nc.gpsimd.tensor_copy(v_h[h][:, :, :], v_all[:, :, bass.ds(head, 1), :].rearrange("p t o w -> p t (o w)")
                                      ).then_inc(s_vh, 1)

            nc.gpsimd.memset(ident16[:, :], 0.0).then_inc(s_cst, 1)
            nc.gpsimd.memset(mask16[:, :], 0.0).then_inc(s_cst, 1)
            nc.gpsimd.memset(fold[:, :], 0.0).then_inc(s_cst, 1)
            pool.wait_ge(s_cst, 3)
            nc.gpsimd.affine_select(out=ident16[:, :], in_=ident16[:, :], compare_op=ALU.not_equal, fill=1.0,
                                    base=0, pattern=[[-1, P]], channel_multiplier=1).then_inc(s_cst, 1)
            nc.gpsimd.affine_select(out=mask16[:, :], in_=mask16[:, :], compare_op=ALU.is_ge, fill=MASK,
                                    base=0, pattern=[[-1, P]], channel_multiplier=1).then_inc(s_cst, 1)
            nc.gpsimd.affine_select(out=fold[:, :], in_=fold[:, :], compare_op=ALU.not_equal, fill=1.0,
                                    base=0, pattern=[[-1, DH + 1]], channel_multiplier=1).then_inc(s_cst, 1)
            pool.wait_ge(s_cst, 6)
            nc.gpsimd.affine_select(out=fold[:, :], in_=fold[:, :], compare_op=ALU.not_equal, fill=1.0,
                                    base=-P // 2, pattern=[[-1, DH + 1]], channel_multiplier=1).then_inc(s_cst, 1)
            pool.wait_ge(s_cst, 7)
            for h in range(2):
                copy_v(h, h)

            def step(it, s, more):
                st = 2 * it + s
                for n in MASKED:
                    h, c, kt = SLOTS[n]
                    for j in range(2):
                        blk = 2 * n + j
                        wait_apart(pool, s_exp, st * 80 + blk + 1, s_cst)
                        q0 = first_query(c, kt + j)
                        w = (kt + j - 4 * c) * P + P - q0
                        tile = probs[:, blk % 4, q0:q0 + w]
                        nc.gpsimd.affine_select(out=tile, in_=tile, compare_op=ALU.is_ge, fill=0.0,
                                                base=P - w, pattern=[[1, w]], channel_multiplier=-1).then_inc(s_mask, 1)
                    if kt == 4 * c + 2 and c == NCH - 1 and more:
                        wait_apart(pool, s_pv, st * 80 + pv_until(4 * h + 3), s_cst)
                        copy_v(2 * (st + 1) + h, h)

            with pool.Fori(0, PAIRS // 2 - 1) as it:
                for s in range(2):
                    step(it, s, True)
            step(PAIRS // 2 - 1, 0, True)
            step(PAIRS // 2 - 1, 1, False)

        @block.scalar
        def _(act):
            def copy_o(st, k):
                act.wait_ge(s_pv, st * 80 + pv_until(k))
                if k >= 2:
                    act.wait_ge(s_comb, 8 * st + k - 1)
                nc.scalar.activation(o_t[:, k % 2], o_bank[:, :], ACT.Copy).then_inc(s_oe, 1)

            def step(it, s):
                st = 2 * it + s
                ended = None
                for n, (h, c, kt) in enumerate(SLOTS):
                    for j in range(2):
                        blk = 2 * n + j
                        act.wait_ge(s_s, st * 80 + blk + 1)
                        if blk >= 4:
                            act.wait_ge(s_pv, st * 80 + blk - 3)
                        q0 = first_query(c, kt + j)
                        nc.scalar.activation(probs[:, blk % 4, q0:], s_bank[:, blk % 2, q0:], ACT.Exp,
                                             scale=DH ** -0.5).then_inc(s_exp, 1)
                    if ended is not None:
                        copy_o(st, ended)
                    ended = 4 * h + c if kt == 4 * c + 2 else None
                copy_o(st, ended)
                act.wait_ge(s_comb, 8 * st + 8)

            act.wait_ge(s_zero, 1)
            with act.Fori(0, PAIRS // 2 - 1) as it:
                for s in range(2):
                    step(it, s)
            for s in range(2):
                step(PAIRS // 2 - 1, s)

        @block.vector
        def _(dve):
            def reduce_unit(pair, u):
                i, c, w = UNITS[u]
                dve.wait_ge(s_max, pair * len(UNITS) + u + 1)
                nc.vector.tensor_reduce(max_part[:, :, i, c], m_bank[:, u % 2, :, 0:w], AX.X, ALU.max).then_inc(s_red, 1)

            def max_of_chunk(pair, cq):
                m = pair * NCH + cq
                dve.wait_ge(s_red, pair * len(UNITS) + LAST_OF_CHUNK[cq] + 1)
                nc.vector.tensor_reduce(max_q[:, :, :], max_part[:, :, 4 * cq:4 * cq + 4, 0:cq + 1], AX.X,
                                        ALU.max).then_inc(s_mq, 1)
                dve.wait_ge(s_mq, m + 1)
                nc.vector.tensor_scalar(neg_hi[:, :, :], max_q[:, :, :], -1.0, None, ALU.mult).then_inc(s_nh, 1)
                dve.wait_ge(s_nh, m + 1)
                nc.vector.tensor_copy(neg_cols[:, :, 0], neg_hi[:, :, :]).then_inc(s_nc, 1)
                nc.vector.scalar_tensor_tensor(neg_cols[:, :, 1], max_q[:, :, :], -1.0, neg_hi[:, :, :], ALU.mult,
                                               ALU.subtract).then_inc(s_nc, 1)

            def copy_rows(pair, cq):
                dve.wait_ge(s_mt, pair * NCH + cq + 1)
                if cq >= 2:
                    dve.wait_ge(s_mrow[cq - 2], (pair + 1) * 64)
                nc.vector.tensor_copy(neg_rows[:, cq % 2], misc[0:16, 0:P]).then_inc(s_mr, 1)

            def normalize(st, k, head):
                h, c = divmod(k, 4)
                dve.wait_ge(s_comb, 8 * st + k + 1)
                o = misc[:, 0:4 * (DH + 1)].rearrange("p (i w) -> p i w", i=4)
                nc.vector.reciprocal(rden[:, :], o[:, :, DH]).then_inc(s_rd, 1)
                dve.wait_ge(s_rd, 8 * st + k + 1)
                nc.vector.tensor_tensor(out_h[:, :, :], o[:, :, 0:DH], rden[:, :].unsqueeze(2).to_broadcast([P, 4, DH]),
                                        ALU.mult).then_inc(s_norm, 1)
                dve.wait_ge(s_norm, 8 * st + k + 1)
                cols = bass.ds(head * DH, DH)
                nc.vector.tensor_tensor(out_h[:, :, :], out_h[:, :, :], gate_row[:, 0:1, cols].to_broadcast([P, 4, DH]),
                                        ALU.mult).then_inc(s_og, 1)
                dve.wait_ge(s_og, 8 * st + k + 1)
                nc.vector.tensor_tensor(x_all[:, 4 * c:4 * c + 4, cols], x_all[:, 4 * c:4 * c + 4, cols], out_h[:, :, :],
                                        ALU.add).then_inc(s_x2, 1)
                dve.wait_ge(s_x2, 8 * st + k + 1)

            nc.vector.memset(o_bank[:, :], 0.0).then_inc(s_zero, 1)
            for b in range(2):
                for h in range(2):
                    nc.vector.memset(k_st[b][h][QK_ROWS:QK_ROWS + 2, :].bitcast(F32), 1.0).then_inc(s_zero, 1)
            for u in range(len(UNITS)):
                reduce_unit(0, u)
                if u in LAST_OF_CHUNK:
                    max_of_chunk(0, LAST_OF_CHUNK.index(u))
                    copy_rows(0, LAST_OF_CHUNK.index(u))

            def step(it, s, more):
                st = 2 * it + s
                for what, arg in timeline(more):
                    if what == "unit":
                        reduce_unit(st + 1, arg)
                        if arg in LAST_OF_CHUNK:
                            max_of_chunk(st + 1, LAST_OF_CHUNK.index(arg))
                    elif what == "rows":
                        copy_rows(st + 1, arg)
                    elif what == "fold":
                        normalize(st, arg, 2 * st + arg // 4)
                if more:
                    dve.wait_ge(s_mrow[2], (st + 2) * 64)
                    dve.wait_ge(s_mrow[3], (st + 2) * 64)

            with dve.Fori(0, PAIRS // 2 - 1) as it:
                for s in range(2):
                    step(it, s, True)
            step(PAIRS // 2 - 1, 0, True)
            step(PAIRS // 2 - 1, 1, False)

        @block.tensor
        def _(pe):
            def unit(pair, b, u):
                i, c, w = UNITS[u]
                if u >= 2:
                    pe.wait_ge(s_red, pair * len(UNITS) + u - 1)
                last = None
                diagonal = c == i // 4
                for h in range(2):
                    r = slice(h * DH, (h + 1) * DH)
                    last = nc.tensor.matmul(m_bank[:, u % 2, h, 0:w], q_st[b][h][r, i * P:(i + 1) * P],
                                            k_st[b][h][r, c * CH:c * CH + w], start=True, stop=True)
                if diagonal:
                    for h in range(2):
                        last = nc.tensor.matmul(m_bank[:, u % 2, h, w - P:w], ident16[:, :], mask16[:, :],
                                                start=False, stop=True, skip_group_check=True)
                last.then_inc(s_max, 1)

            def rows(pair, cq):
                pe.wait_ge(s_nc, 2 * (pair * NCH + cq) + 2)
                nc.tensor.transpose(misc[0:16, 0:P], neg_cols[:, :, :, :].rearrange("p h s i -> p (h s i)"),
                                    ident[:, :]).then_inc(s_mt, 1)

            def scores(st, s, n):
                h, c, kt = SLOTS[n]
                for j in range(2):
                    blk = 2 * n + j
                    if blk >= 2:
                        pe.wait_ge(s_exp, st * 80 + blk - 1)
                    q0 = first_query(c, kt + j)
                    nc.tensor.matmul(s_bank[:, blk % 2, q0:], k_st[s][h][:, (kt + j) * P:(kt + j + 1) * P],
                                     q_st[s][h][:, c * CH + q0:(c + 1) * CH], start=True, stop=True).then_inc(s_s, 1)

            def pv(st, n):
                h, c, kt = SLOTS[n]
                k = 4 * h + c
                masked = len([m for m in MASKED if m <= n])
                if kt >= 4 * c:
                    pe.wait_ge(s_mask, st * 2 * len(MASKED) + 2 * masked)
                else:
                    pe.wait_ge(s_exp, st * 80 + 2 * n + 2)
                if kt == 0:
                    if c == 0:
                        pe.wait_ge(s_vh, 2 * st + h + 1)
                    if k:
                        pe.wait_ge(s_oe, 8 * st + k)
                for j in range(2):
                    q0 = first_query(c, kt + j)
                    last = nc.tensor.matmul(o_bank[64 * j:64 * j + DH + 1, q0:], v_h[h][:, kt + j, :],
                                            probs[:, (2 * n + j) % 4, q0:], start=(kt == 0), stop=(kt == 4 * c + 2))
                    last.then_inc(s_pv, 1)

            def fold_o(st, k):
                pe.wait_ge(s_oe, 8 * st + k + 1)
                for i in range(4):
                    last = nc.tensor.matmul(misc[:, i * (DH + 1):(i + 1) * (DH + 1)], o_t[:, k % 2, i * P:(i + 1) * P],
                                            fold[:, :], start=True, stop=True)
                last.then_inc(s_comb, 1)

            pe.wait_ge(s_cst, 7)
            pe.wait_ge(s_zero, 5)
            for h in range(2):
                pe.wait_ge(s_ld[0][h], 96)
            for u in range(len(UNITS)):
                unit(0, 0, u)
                if u in LAST_OF_CHUNK:
                    cq = LAST_OF_CHUNK.index(u)
                    if cq:
                        pe.wait_ge(s_mr, cq)
                    rows(0, cq)
            pe.wait_ge(s_mr, NCH)

            def step(it, s, more):
                st = 2 * it + s
                free = None
                for what, arg in timeline(more):
                    if what == "scores":
                        h, c, kt = SLOTS[arg]
                        if h == 0 and kt == 0:
                            pe.wait_ge(s_mrow[c], (st + 1) * 64)
                        scores(st, s, arg)
                    elif what == "pv":
                        pv(st, arg)
                    elif what == "unit":
                        if arg == 0:
                            for h in range(2):
                                pe.wait_ge(s_ld[1 - s][h], (it + 1 + s) * 96)
                        unit(st + 1, 1 - s, arg)
                    elif what == "rows":
                        if free:
                            pe.wait_ge(*free)
                        rows(st + 1, arg)
                        free = (s_mr, (st + 1) * NCH + arg + 1)
                    elif what == "fold":
                        if free:
                            pe.wait_ge(*free)
                        fold_o(st, arg)
                        free = (s_norm, 8 * st + arg + 1)
                pe.wait_ge(*free)

            with pe.Fori(0, PAIRS // 2 - 1) as it:
                for s in range(2):
                    step(it, s, True)
            step(PAIRS // 2 - 1, 0, True)
            step(PAIRS // 2 - 1, 1, False)


def timeline(more):
    out, due, rows = [], [], []
    for n in range(len(SLOTS) + 1):
        if n < len(SLOTS):
            out.append(("scores", n))
        if more:
            for u in units_of(n):
                out.append(("unit", u))
                if u in LAST_OF_CHUNK:
                    rows.append((n + 1, LAST_OF_CHUNK.index(u)))
        for at, cq in [r for r in rows if r[0] == n]:
            out.append(("rows", cq))
        if n:
            out.append(("pv", n - 1))
            h, c, kt = SLOTS[n - 1]
            for at, k in [x for x in due if x[0] == n]:
                out.append(("fold", k))
            if kt == 4 * c + 2:
                due.append((n + 1, 4 * h + c))
    out.append(("fold", 2 * NCH - 1))
    return out


E_N, TOP = 32, 4
SLOT_TILE = 320
SUBS = [(0, P), (P, P), (2 * P, SLOT_TILE - 2 * P)]
REGION = -(-T // SLOT_TILE) * SLOT_TILE
N_MORE = REGION // SLOT_TILE - 1
NO_SLOT = E_N * REGION
ROWS = T * TOP
SATURATED = 16.6355


def route(nc, d, keep):
    with ExitStack() as ctx:
        sb = lambda name, shape, dt=F32: ctx.enter_context(nc.sbuf_tensor(name, shape, dt))
        sem = lambda name: ctx.enter_context(nc.semaphore(name))
        pb = lambda name, shape: ctx.enter_context(nc.psum_tensor(name, shape, F32))
        ident, mod_col, x_all, weights, tile_list, n_tiles = (
            keep[n] for n in ("ident", "mod_col", "x_all", "weights", "tile_list", "n_tiles"))

        gate_w = sb("gate_w", [P, KT, E_N])
        stats = sb("stats2", [P, 4, 6])
        meanvar = sb("meanvar2", [P, 4, 2])
        std = sb("std2", [P, 4])
        rstd = sb("rstd2", [P, 4])
        eps_col = sb("eps_col2", [P, 1])
        x_n = sb("x_n2", [P, 2, 4, D])
        h_t = sb("h_t2", [P, 2, KT, CH])
        logits = sb("logits", [P, 4, E_N])
        capped = sb("capped", [P, 4, E_N])
        top_v = sb("top_v", [P, 4, 8])
        top_i = sb("top_i", [P, 4, 8], U32)
        top_f = sb("top_f", [P, 4, 8])
        expert_no = sb("expert_no", [P, E_N])
        region_of = sb("region_of", [P, E_N])
        onehot = sb("onehot", [P, TOP, 4, E_N])
        picked = sb("picked", [P, TOP, 4, E_N])
        row_max = sb("row_max", [P, 4])
        top_logit = sb("top_logit", [P, TOP, 4])
        top_exp = sb("top_exp", [P, TOP, 4])
        top_sum = sb("top_sum", [P, 4])
        top_rec = sb("top_rec", [P, 4])
        mask_h = sb("mask_h", [P, 4, E_N], F16)
        count_h = sb("count_h", [P, 5, E_N], F16)
        before = sb("before", [P, P], F16)
        ones_h = sb("ones_h", [P, P], F16)
        slot_f = sb("slot_f", [P, 4, E_N])
        slot_k = sb("slot_k", [P, TOP, 4])
        slot_i = sb("slot_i", [P, NCH, TOP, 4], I32)
        row_no = sb("row_no", [P, TOP, TT], I32)
        blank = sb("blank", [P, 5 * P], I32)
        zero_rows = sb("zero_rows", [P // 4, D])
        flags = sb("flags", [P, N_MORE, E_N])
        flag_sum = sb("flag_sum", [P, N_MORE * E_N])
        ones_f = sb("ones_f", [P, N_MORE * E_N])
        start_v = sb("start_v", [P, N_MORE, E_N])
        chosen = sb("chosen", [P, N_MORE * E_N])
        prod = sb("prod", [P, N_MORE * E_N])
        number_1 = sb("number_1", [P, 1])
        more_f = sb("more_f", [P, 2])
        more_i = sb("more_i", [P, 3], I32)
        first_i = sb("first_i", [P, 3], I32)
        tp = [pb(f"tp2_{i}", [P, CH]) for i in range(2)]
        lg = [pb(f"lg{i}", [P, 4, E_N]) for i in range(2)]
        pos = [pb(f"pos{i}", [P, 4, E_N]) for i in range(2)]
        tot = pb("tot", [P, E_N])

        s_gw = sem("gate_w_loaded")
        s_cst = sem("constants_set3")
        s_cst2 = sem("constants_set4")
        s_blank = sem("slot_list_blank")
        s_blankz = sem("zero_rows_stored")
        s_st = sem("stats_done2")
        s_mv = sem("meanvar_done2")
        s_std = sem("std_done2")
        s_rs = sem("rstd_done2")
        s_xn = sem("x_n_done2")
        s_xns = [sem(f"x_n_stored{i}") for i in range(2)]
        s_tp = sem("transposed2")
        s_ht = sem("h_t_done2")
        s_lg = sem("logits_done")
        s_d = sem("routing_step")
        s_e = sem("top_exp_done")
        s_mask = sem("mask_done")
        s_pos = sem("ranks_done")
        s_slot = sem("slots_done")
        s_scat = sem("slots_placed")
        chain = sem("vector_chain")
        s_zc = sem("count_zeroed")
        s_tot = sem("counts_done")
        s_list = sem("tile_list_done")
        s_lstore = sem("tile_list_stored")
        s_lload = sem("tile_list_loaded")

        block = ctx.enter_context(nc.Block())

        @block.sync
        def _(sp):
            sp.dma_start(gate_w[:, :, :], d["gate_t"].rearrange("(k p) e -> p k e", p=P)).then_inc(s_gw, 16)
            sp.wait_ge(s_cst, 5)
            n = P * 5
            full = E_N * REGION // n
            sp.dma_start(d["slots"][0:full * n, :].rearrange("(p f) o -> p (f o)", f=n), blank[0:full, :]).then_inc(s_blank, 16)
            rest = NO_SLOT + SLOT_TILE - full * n
            sp.dma_start(d["slots"][full * n:full * n + rest, :].rearrange("(p f) o -> p (f o)", p=1),
                         blank[0:1, 0:rest]).then_inc(s_blank, 16)
            sp.dma_start(d["x_norm"][T:T + P // 4, :], zero_rows[:, :]).then_inc(s_blankz, 16)
            for c in range(NCH):
                b = c % 2
                sp.wait_ge(s_xn, c * 4 + 4)
                sp.dma_start(d["x_norm"][c * CH:(c + 1) * CH, :].rearrange("(t p) n -> p t n", p=P),
                             x_n[:, b]).then_inc(s_xns[b], 16)
            sp.wait_ge(s_list, 2)
            sp.dma_start(d["tiles"][0:E_N, :], first_i[0:E_N, :]).then_inc(s_lstore, 16)
            sp.dma_start(d["tiles"][E_N:2 * E_N, :], more_i[0:E_N, :]).then_inc(s_lstore, 16)
            sp.wait_ge(s_lstore, 32)
            sp.dma_start(tile_list[0:1, :], d["tiles"].rearrange("(o a) b -> o (a b)", o=1)).then_inc(s_lload, 16)
            sp.wait_ge(s_lload, 16)
            sp.wait_ge(s_blankz, 16)
            for b in range(2):
                sp.wait_ge(s_xns[b], 16 * NCH // 2)

        @block.gpsimd
        def _(pool):
            nc.gpsimd.iota(blank[:, :], [[0, 5], [1, P]], base=ROWS, channel_multiplier=0).then_inc(s_cst, 1)
            nc.gpsimd.memset(zero_rows[:, :], 0.0).then_inc(s_cst, 1)
            nc.gpsimd.memset(ones_h[:, :], 1.0).then_inc(s_cst, 1)
            nc.gpsimd.memset(eps_col[:, :], EPS).then_inc(s_cst, 1)
            nc.gpsimd.memset(ones_f[:, :], 1.0).then_inc(s_cst, 1)
            pool.wait_ge(s_cst, 5)
            nc.gpsimd.affine_select(out=before[:, :], in_=ones_h[:, :], compare_op=ALU.is_gt, fill=0.0,
                                    base=0, pattern=[[1, P]], channel_multiplier=-1).then_inc(s_cst2, 1)
            nc.gpsimd.iota(expert_no[:, :], [[1, E_N]], base=0, channel_multiplier=0,
                           allow_small_or_imprecise_dtypes=True).then_inc(s_cst2, 1)
            nc.gpsimd.iota(region_of[:, :], [[REGION, E_N]], base=0, channel_multiplier=0,
                           allow_small_or_imprecise_dtypes=True).then_inc(s_cst2, 1)
            nc.gpsimd.iota(row_no[:, :, :], [[1, TOP], [TOP * P, TT]], base=0, channel_multiplier=TOP).then_inc(s_cst2, 1)
            nc.gpsimd.iota(start_v[:, :, :], [[SLOT_TILE, N_MORE], [REGION, E_N]], base=SLOT_TILE - NO_SLOT,
                           channel_multiplier=0, allow_small_or_imprecise_dtypes=True).then_inc(s_cst2, 1)
            nc.gpsimd.iota(number_1[:, :], [[0, 1]], base=1, channel_multiplier=1,
                           allow_small_or_imprecise_dtypes=True).then_inc(s_cst2, 1)
            nc.gpsimd.iota(first_i[:, 0:1], [[0, 1]], base=0, channel_multiplier=1).then_inc(s_cst2, 1)
            nc.gpsimd.iota(first_i[:, 1:2], [[0, 1]], base=0, channel_multiplier=REGION).then_inc(s_cst2, 1)
            pool.wait_ge(s_blank, 32)
            for c in range(NCH):
                b = c % 2
                pool.wait_ge(s_slot, c + 1)
                for t in range(4):
                    for k in range(TOP):
                        nc.gpsimd.indirect_dma_start(
                            out=d["slots"], out_offset=bass.IndirectOffsetOnAxis(ap=slot_i[:, c, k, t:t + 1], axis=0),
                            in_=row_no[:, k, 4 * c + t:4 * c + t + 1], in_offset=None).then_inc(s_scat, 16)
            pool.wait_ge(s_scat, 16 * TOP * TT)

        @block.scalar
        def _(act):
            for c in range(NCH):
                b = c % 2
                act.wait_ge(s_mv, c + 1)
                nc.scalar.activation(std[:, :], meanvar[:, :, 1], ACT.Sqrt, bias=eps_col[:, :]).then_inc(s_std, 1)
                for k in range(KT):
                    act.wait_ge(s_tp, c * KT + k + 1)
                    nc.scalar.activation(h_t[:, b, k], tp[k % 2][:, :], ACT.Identity, bias=mod_col[:, 2, k:k + 1],
                                         scale=mod_col[:, 3, k:k + 1]).then_inc(s_ht, 1)
                act.wait_ge(s_d, c * 2 + 1)
                nc.scalar.activation(top_exp[:, :, :], top_logit[:, :, :], ACT.Exp).then_inc(s_e, 1)

        @block.vector
        def _(dve):
            spread_e = lambda ap: ap.unsqueeze(1).to_broadcast([P, 4, E_N])

            def normalize(c, b):
                for t in range(4):
                    nc.vector.bn_stats(stats[:, t], x_all[:, c * 4 + t]
                                       ).then_inc(s_st, 1)
                for t in range(4):
                    dve.wait_ge(s_st, c * 4 + t + 1)
                    last = nc.vector.bn_aggr(meanvar[:, t], stats[:, t])
                last.then_inc(s_mv, 1)
                dve.wait_ge(s_std, c + 1)
                nc.vector.reciprocal(rstd[:, :], std[:, :]).then_inc(s_rs, 1)
                dve.wait_ge(s_rs, c + 1)
                for t in range(4):
                    nc.vector.tensor_scalar(x_n[:, b, t], x_all[:, c * 4 + t],
                                            meanvar[:, t, 0:1], rstd[:, t:t + 1],
                                            ALU.subtract, ALU.mult).then_inc(s_xn, 1)

            def choose(c, b):
                steps = [0]

                def link(ins):
                    steps[0] += 1
                    ins.then_inc(chain, 1)
                    dve.wait_ge(chain, c * LINKS + steps[0])

                dve.wait_ge(s_lg, c + 1)
                link(nc.vector.tensor_copy(logits[:, :, :], lg[b][:, :, :]))
                link(nc.vector.tensor_scalar(capped[:, :, :], logits[:, :, :], SATURATED, None, ALU.min))
                for t in range(4):
                    link(nc.vector.max(top_v[:, t], capped[:, t]))
                    link(nc.vector.max_index(top_i[:, t], top_v[:, t], capped[:, t]))
                link(nc.vector.tensor_copy(top_f[:, :, :], top_i[:, :, :]))
                for k in range(TOP):
                    link(nc.vector.tensor_tensor(onehot[:, k], top_f[:, :, k].unsqueeze(2).to_broadcast([P, 4, E_N]),
                                                 spread_e(expert_no[:, :]), ALU.is_equal))
                with nc.allow_low_precision("ones and zeros"):
                    link(nc.vector.tensor_reduce(mask_h[:, :, :], onehot[:, :, :, :].rearrange("p k t e -> p t e k"),
                                                 AX.X, ALU.add))
                for t in range(3):
                    link(nc.vector.tensor_tensor(count_h[:, t + 1], count_h[:, t], mask_h[:, t], ALU.add))
                nc.vector.tensor_tensor(count_h[:, 4], count_h[:, 3], mask_h[:, 3], ALU.add).then_inc(s_mask, 1)
                dve.wait_ge(s_mask, c + 1)
                link(nc.vector.tensor_reduce(row_max[:, :], logits[:, :, :], AX.X, ALU.max))
                for k in range(TOP):
                    link(nc.vector.tensor_tensor(picked[:, k], onehot[:, k], logits[:, :, :], ALU.mult))
                link(nc.vector.tensor_reduce(top_logit[:, :, :], picked[:, :, :, :], AX.X, ALU.add))
                nc.vector.tensor_tensor(top_logit[:, :, :], top_logit[:, :, :],
                                        row_max[:, :].unsqueeze(1).to_broadcast([P, TOP, 4]), ALU.subtract
                                        ).then_inc(s_d, 1)
                dve.wait_ge(s_d, 2 * c + 1)
                dve.wait_ge(s_pos, c + 1)
                link(nc.vector.tensor_tensor(slot_f[:, :, :], pos[b][:, :, :], spread_e(region_of[:, :]), ALU.add))
                for k in range(TOP):
                    link(nc.vector.tensor_tensor(picked[:, k], onehot[:, k], slot_f[:, :, :], ALU.mult))
                link(nc.vector.tensor_reduce(slot_k[:, :, :], picked[:, :, :, :], AX.X, ALU.add))
                nc.vector.tensor_copy(slot_i[:, c], slot_k[:, :, :]).then_inc(s_slot, 1)
                dve.wait_ge(s_slot, c + 1)
                dve.wait_ge(s_e, c + 1)
                link(nc.vector.tensor_reduce(top_sum[:, :], top_exp[:, :, :].rearrange("p k t -> p t k"), AX.X, ALU.add))
                link(nc.vector.reciprocal(top_rec[:, :], top_sum[:, :]))
                link(nc.vector.tensor_tensor(weights[:, :, 4 * c:4 * c + 4], top_exp[:, :, :],
                                             top_rec[:, :].unsqueeze(1).to_broadcast([P, TOP, 4]), ALU.mult))
                nc.vector.tensor_copy(count_h[:, 0], count_h[:, 4]).then_inc(s_d, 1)
                dve.wait_ge(s_d, 2 * c + 2)
                assert steps[0] == LINKS

            LINKS = 34
            with nc.allow_low_precision("a count of zero"):
                nc.vector.memset(count_h[:, 0], 0.0).then_inc(s_zc, 1)
            dve.wait_ge(s_zc, 1)
            dve.wait_ge(s_gw, 16)
            dve.wait_ge(s_cst2, 8)
            for c in range(NCH):
                b = c % 2
                if c >= 2:
                    dve.wait_ge(s_xns[b], 16 * (c // 2))
                normalize(c, b)
                choose(c, b)

            last = [NCH * LINKS]

            def link(ins):
                last[0] += 1
                ins.then_inc(chain, 1)
                dve.wait_ge(chain, last[0])

            dve.wait_ge(s_tot, 1)
            for r in range(N_MORE):
                link(nc.vector.tensor_scalar(flags[:, r], tot[:, :], float((r + 1) * SLOT_TILE), None, ALU.is_gt))
            flat = flags[:, :, :].rearrange("p r e -> p (r e)")
            link(nc.vector.tensor_tensor_scan(flag_sum[:, :], ones_f[:, :], flat, 0.0, ALU.mult, ALU.add))
            link(nc.vector.tensor_scalar(chosen[:, :], flag_sum[:, :], number_1[:, 0:1], None, ALU.is_equal))
            link(nc.vector.tensor_tensor(chosen[:, :], chosen[:, :], flat, ALU.mult))
            link(nc.vector.tensor_tensor(prod[:, :], chosen[:, :], start_v[:, :, :].rearrange("p r e -> p (r e)"), ALU.mult))
            link(nc.vector.tensor_reduce(more_f[:, 1:2], prod[:, :], AX.X, ALU.add))
            link(nc.vector.tensor_tensor(flags[:, :, :], chosen[:, :].rearrange("p (r e) -> p r e", e=E_N),
                                         expert_no[:, :].unsqueeze(1).to_broadcast([P, N_MORE, E_N]), ALU.mult))
            link(nc.vector.tensor_reduce(more_f[:, 0:1], flags[:, :, :], AX.XY, ALU.add))
            link(nc.vector.tensor_scalar(more_i[:, 1:2], more_f[:, 1:2], float(NO_SLOT), None, ALU.add))
            link(nc.vector.tensor_copy(more_i[:, 0:1], more_f[:, 0:1]))
            link(nc.vector.tensor_scalar(more_i[:, 2:3], more_i[:, 0:1], 1, None, ALU.logical_shift_right))
            nc.vector.tensor_scalar(first_i[:, 2:3], first_i[:, 0:1], 1, None, ALU.logical_shift_right).then_inc(s_list, 1)
            link(nc.vector.tensor_scalar(n_tiles[:, 0:1], flag_sum[:, N_MORE * E_N - 1:], float(E_N + 1), None, ALU.add))
            link(nc.vector.tensor_scalar(n_tiles[:, 0:1], n_tiles[:, 0:1], 1, None, ALU.logical_shift_right))
            nc.vector.tensor_scalar(n_tiles[:, 0:1], n_tiles[:, 0:1], 1, None, ALU.logical_shift_left).then_inc(s_list, 1)
            dve.wait_ge(s_list, 2)

        @block.tensor
        def _(pe):
            pe.wait_ge(s_gw, 16)
            pe.wait_ge(s_cst2, 8)
            for c in range(NCH):
                b = c % 2
                pe.wait_ge(s_xn, c * 4 + 4)
                for k in range(KT):
                    if k >= 2:
                        pe.wait_ge(s_ht, c * KT + k - 1)
                    for t in range(4):
                        last = nc.tensor.transpose(tp[k % 2][:, t * P:(t + 1) * P], x_n[:, b, t, k * P:(k + 1) * P],
                                                   ident[:, :])
                    last.then_inc(s_tp, 1)
                pe.wait_ge(s_ht, (c + 1) * KT)
                for t in range(4):
                    for k in range(KT):
                        last = nc.tensor.matmul(lg[b][:, t], h_t[:, b, k, t * P:(t + 1) * P], gate_w[:, k],
                                                start=(k == 0), stop=(k == KT - 1))
                last.then_inc(s_lg, 1)
                pe.wait_ge(s_mask, c + 1)
                nc.tensor.matmul(pos[b][:, :, :], before[:, :], mask_h[:, :, :], start=True, stop=False)
                nc.tensor.matmul(pos[b][:, :, :], ones_h[:, :], count_h[:, 0:4], start=False, stop=True).then_inc(s_pos, 1)
            pe.wait_ge(s_d, 2 * NCH)
            nc.tensor.matmul(tot[:, :], ones_h[:, :], count_h[:, 4], start=True, stop=True).then_inc(s_tot, 1)


I_BIG, I_SMALL = 192, 128
SMALL_SCALE = 0.05
GU_COLS = 2 * I_BIG
JOBS_GU = [("big", 0, P), ("big", P, P), ("big", 2 * P, P), ("small", 0, P), ("small", P, P)]


def experts(nc, d, keep):
    with ExitStack() as ctx:
        sb = lambda name, shape, dt=F32: ctx.enter_context(nc.sbuf_tensor(name, shape, dt))
        sem = lambda name: ctx.enter_context(nc.semaphore(name))
        pb = lambda name, shape: ctx.enter_context(nc.psum_tensor(name, shape, F32))
        ident, mod_col, tile_list, n_tiles = (keep[n] for n in ("ident", "mod_col", "tile_list", "n_tiles"))

        w_gu = [sb(f"w_gu{b}", [P, KT, GU_COLS]) for b in range(2)]
        w_gu_s = [sb(f"w_gu_s{b}", [P, KT, 2 * I_SMALL]) for b in range(2)]
        w_d = [sb(f"w_d{b}", [P, 3, D]) for b in range(2)]
        rows_i = [sb(f"rows_i{b}", [P, 3], I32) for b in range(2)]
        toks_i = [sb(f"toks_i{b}", [P, 3], I32) for b in range(2)]
        x_g = [sb(f"x_g{b}", [P, 3, D]) for b in range(2)]
        x_t = sb("x_t", [P, 2, KT, SLOT_TILE])
        gated = sb("gated", [P, 2, SLOT_TILE])
        act_t = sb("act_t", [P, 2, 3, SLOT_TILE])
        y_sb = [sb(f"y_sb{b}", [P, 3, D]) for b in range(2)]
        tp = pb("tp3", [P, SLOT_TILE])
        gu = [pb(f"gu{j}", [P, SLOT_TILE]) for j in range(5)]
        yb = [pb(f"y{j}", [P, D]) for j in range(2)]

        s_rows = [sem(f"rows{b}_loaded") for b in range(2)]
        s_wgu = [sem(f"w_gu{b}_loaded") for b in range(2)]
        s_wd = [sem(f"w_d{b}_loaded") for b in range(2)]
        s_tok = sem("tokens_done")
        s_xg = [sem(f"x_gathered{b}") for b in range(2)]
        s_tp = sem("x_transposed")
        s_xt = sem("x_t_done")
        s_gu = sem("gate_up_done")
        s_silu = sem("silu_done2")
        s_act = sem("act_done")
        s_y = sem("y_done")
        s_yc = sem("y_copied")
        s_ys = [sem(f"y_stored{b}") for b in range(2)]
        one = sem("always_one")

        block = ctx.enter_context(nc.Block())
        N_MAX = 2 * E_N

        def bound(eng):
            return eng.value_load(n_tiles[0:1, 0:1], min_val=E_N, max_val=N_MAX - 3)

        def entry(eng, g, what, top):
            return eng.value_load(tile_list[0:1, bass.ds(g * 3 + what, 1)], min_val=0, max_val=top)

        @block.sync
        def _(sp):
            def load_rows(g, b):
                start = entry(sp, g, 1, NO_SLOT)
                for j, (s0, n) in enumerate(SUBS):
                    sp.dma_start(rows_i[b][0:n, j:j + 1], d["slots"][bass.ds(start + s0, n), :]).then_inc(s_rows[b], 16)

            def load_weights(g, b):
                e = entry(sp, g, 0, E_N - 1)
                c = entry(sp, g, 2, E_N // 2 - 1)
                sp.dma_start(w_gu[b][:, :, :], d["w_gu"][bass.ds(e, 1)].rearrange("o (k p) n -> p (o k) n", p=P)).then_inc(s_wgu[b], 16)
                sp.dma_start(w_gu_s[b][:, :, :], d["w_gu_s"][bass.ds(c, 1)].rearrange("o (k p) n -> p (o k) n", p=P)).then_inc(s_wgu[b], 16)
                sp.dma_start(w_d[b][:, 0, :], d["w_d"][bass.ds(e, 1), 0:P].rearrange("o p n -> p (o n)")).then_inc(s_wd[b], 16)
                sp.dma_start(w_d[b][0:I_BIG - P, 1, :], d["w_d"][bass.ds(e, 1), P:I_BIG].rearrange("o p n -> p (o n)")).then_inc(s_wd[b], 16)
                sp.dma_start(w_d[b][:, 2, :], d["w_d_s"][bass.ds(c, 1)].rearrange("o p n -> p (o n)")).then_inc(s_wd[b], 16)

            n = bound(sp)
            load_rows(0, 0)
            load_rows(1, 1)
            load_weights(0, 0)
            load_weights(1, 1)
            with sp.Fori(0, n, 2) as g0:
                for b in range(2):
                    g = g0 + b
                    sp.wait_ge(s_y, g * 3 + 3)
                    load_weights(g + 2, b)
                    sp.wait_ge(s_ys[b], (g0 * 24) + 48)
                    load_rows(g + 2, b)
            weights_asked, lists_asked, stored = (sp.to_reg(v) for v in (n * 16 + 32, n * 24 + 48, n * 24))
            for b in range(2):
                wait_apart(sp, s_wgu[b], weights_asked, s_rows[0])
                sp.wait_ge(s_wd[b], lists_asked)
                sp.wait_ge(s_rows[b], lists_asked)
                sp.wait_ge(s_ys[b], stored)

        @block.gpsimd
        def _(pool):
            def gather(g, b, half):
                wait_apart(pool, s_tok, g + 1, one)
                for j, (s0, n) in enumerate(SUBS):
                    nc.gpsimd.indirect_dma_start(
                        out=x_g[b][0:n, j, :], out_offset=None, in_=d["x_norm"],
                        in_offset=bass.IndirectOffsetOnAxis(ap=toks_i[b][0:n, j:j + 1], axis=0)).then_inc(s_xg[b], 16)

            pool.sem_inc(one, 1)
            n = bound(pool)
            gather(0, 0, 0)
            with pool.Fori(0, n, 2) as g0:
                for b in range(2):
                    g = g0 + b
                    gather(g + 1, 1 - b, 0)
                    for j, (s0, m) in enumerate(SUBS):
                        wait_apart(pool, s_yc, g * 3 + j + 1, one)
                        nc.gpsimd.indirect_dma_start(
                            out=d["y_rows"], out_offset=bass.IndirectOffsetOnAxis(ap=rows_i[b][0:m, j:j + 1], axis=0),
                            in_=y_sb[b][0:m, j, :], in_offset=None).then_inc(s_ys[b], 16)

        @block.scalar
        def _(act):
            def transposed(g, b):
                for k in range(KT):
                    act.wait_ge(s_tp, g * KT + k + 1)
                    nc.scalar.activation(x_t[:, b, k], tp[:, :], ACT.Identity, bias=mod_col[:, 2, k:k + 1],
                                         scale=mod_col[:, 3, k:k + 1]).then_inc(s_xt, 1)

            n = bound(act)
            transposed(0, 0)
            with act.Fori(0, n, 2) as g0:
                for b in range(2):
                    g = g0 + b
                    for j in range(3):
                        act.wait_ge(s_gu, g * 5 + (1, 3, 4)[j])
                        rows = slice(0, 64) if j == 1 else slice(0, P)
                        if j == 2:
                            act.wait_ge(s_act, g * 3 + 1)
                        nc.scalar.activation(gated[rows, j % 2], gu[(0, 2, 3)[j]][rows, :], ACT.Silu).then_inc(s_silu, 1)
                    for i, (s0, m) in enumerate(SUBS):
                        if i == 1:
                            transposed(g + 1, 1 - b)
                        act.wait_ge(s_y, g * 3 + i + 1)
                        nc.scalar.activation(y_sb[b][0:m, i, :], yb[i % 2][0:m, :], ACT.Copy).then_inc(s_yc, 1)

        @block.vector
        def _(dve):
            def tokens(g, b, half):
                dve.wait_ge(s_rows[b], half * 48 + 48)
                for j, (s0, n) in enumerate(SUBS):
                    last = nc.vector.tensor_scalar(toks_i[b][0:n, j:j + 1], rows_i[b][0:n, j:j + 1], 2, None,
                                                   ALU.logical_shift_right)
                last.then_inc(s_tok, 1)

            n = bound(dve)
            tokens(0, 0, 0)
            tokens(1, 1, 0)
            with dve.Fori(0, n, 2) as g0:
                for b in range(2):
                    g = g0 + b
                    for j in range(3):
                        rows = slice(0, 64) if j == 1 else slice(0, P)
                        dve.wait_ge(s_silu, g * 3 + j + 1)
                        dve.wait_ge(s_gu, g * 5 + (2, 3, 5)[j])
                        if j == 2:
                            nc.vector.scalar_tensor_tensor(act_t[:, b, 2], gated[:, 0], SMALL_SCALE, gu[4][:, :], ALU.mult,
                                                           ALU.mult).then_inc(s_act, 1)
                        else:
                            up = gu[1][:, :] if j == 0 else gu[2][64:P, :]
                            nc.vector.tensor_tensor(act_t[rows, b, j], gated[rows, j % 2], up, ALU.mult).then_inc(s_act, 1)
                    dve.wait_ge(s_rows[b], g0 * 24 + 96)
                    for j, (s0, m) in enumerate(SUBS):
                        last = nc.vector.tensor_scalar(toks_i[b][0:m, j:j + 1], rows_i[b][0:m, j:j + 1], 2, None,
                                                       ALU.logical_shift_right)
                    last.then_inc(s_tok, 1)

        @block.tensor
        def _(pe):
            def transpose_x(g, b, k):
                if k:
                    pe.wait_ge(s_xt, g * KT + k)
                for j, (s0, n) in enumerate(SUBS):
                    last = nc.tensor.transpose(tp[:, s0:s0 + n], x_g[b][0:n, j, k * P:(k + 1) * P], ident[0:n, 0:n])
                last.then_inc(s_tp, 1)

            n = bound(pe)
            pe.wait_ge(s_xg[0], 48)
            for k in range(KT):
                transpose_x(0, 0, k)
            with pe.Fori(0, n, 2) as g0:
                for b in range(2):
                    g = g0 + b
                    pe.wait_ge(s_xt, g * KT + KT)
                    pe.wait_ge(s_wgu[b], g0 * 16 + 32)
                    for j, (which, c0, cols) in enumerate(JOBS_GU):
                        w = w_gu[b] if which == "big" else w_gu_s[b]
                        for k in range(KT):
                            last = nc.tensor.matmul(gu[j][:, :], w[:, k, c0:c0 + cols], x_t[:, b, k],
                                                    start=(k == 0), stop=(k == KT - 1))
                        last.then_inc(s_gu, 1)
                    pe.wait_ge(s_wd[b], g0 * 24 + 48)
                    pe.wait_ge(s_xg[1 - b], (g0 + 2 * b) * 24 + 48)
                    for i, (s0, m) in enumerate(SUBS):
                        for k in ((0,), (1, 2), (3,))[i]:
                            transpose_x(g + 1, 1 - b, k)
                        if i == 0:
                            pe.wait_ge(s_act, g * 3 + 3)
                        if i == 2:
                            pe.wait_ge(s_yc, g * 3 + 1)
                        for j, inner in enumerate((P, I_BIG - P, P)):
                            last = nc.tensor.matmul(yb[i % 2][0:m, :], act_t[0:inner, b, j, s0:s0 + m],
                                                    w_d[b][0:inner, j, :], start=(j == 0), stop=(j == 2))
                        last.then_inc(s_y, 1)


def combine(nc, d, keep):
    with ExitStack() as ctx:
        sb = lambda name, shape, dt=F32: ctx.enter_context(nc.sbuf_tensor(name, shape, dt))
        sem = lambda name: ctx.enter_context(nc.semaphore(name))
        x_all, gate_row, weights = (keep[n] for n in ("x_all", "gate_row", "weights"))
        BUFS = 4
        y_in = [sb(f"y_in{b}", [P, TOP, D]) for b in range(BUFS)]
        acc = [sb(f"acc{b}", [P, D]) for b in range(2)]
        res = [sb(f"res{b}", [P, D]) for b in range(2)]
        s_in = [sem(f"y_in{b}_loaded") for b in range(BUFS)]
        s_w0 = sem("first_weighed")
        s_acc = sem("weighed")
        s_gate = sem("gated_done")
        s_res = sem("result_done")
        s_out = [sem(f"out{b}_stored") for b in range(2)]
        block = ctx.enter_context(nc.Block())
        y_view = d["y_rows"][0:ROWS, :].rearrange("(t p k) n -> t p k n", p=P, k=TOP)

        @block.sync
        def _(sp):
            for t in range(TT):
                if t >= BUFS:
                    sp.wait_ge(s_acc, 3 * (t - BUFS) + 3)
                sp.dma_start(y_in[t % BUFS][:, :, :], y_view[t]).then_inc(s_in[t % BUFS], 16)

        @block.scalar
        def _(act):
            for t in range(TT):
                act.wait_ge(s_in[t % BUFS], 16 * (t // BUFS) + 16)
                if t >= 2:
                    act.wait_ge(s_gate, t - 1)
                nc.scalar.activation(acc[t % 2][:, :], y_in[t % BUFS][:, 0, :], ACT.Copy,
                                     scale=weights[:, 0, t:t + 1]).then_inc(s_w0, 1)
                if t:
                    act.wait_ge(s_res, t)
                    act.dma_start(d["out"][(t - 1) * P:t * P, :], res[(t - 1) % 2][:, :]).then_inc(s_out[(t - 1) % 2], 16)
            act.wait_ge(s_res, TT)
            act.dma_start(d["out"][(TT - 1) * P:TT * P, :], res[(TT - 1) % 2][:, :]).then_inc(s_out[(TT - 1) % 2], 16)
            for b in range(2):
                act.wait_ge(s_out[b], 16 * TT // 2)

        @block.vector
        def _(dve):
            def finish(t):
                dve.wait_ge(s_gate, t + 1)
                if t >= 2:
                    dve.wait_ge(s_out[t % 2], 16 * (t // 2))
                nc.vector.tensor_tensor(res[t % 2][:, :], acc[t % 2][:, :], x_all[:, t], ALU.add).then_inc(s_res, 1)

            for t in range(TT):
                dve.wait_ge(s_w0, t + 1)
                dve.wait_ge(s_in[t % BUFS], 16 * (t // BUFS) + 16)
                for k in range(1, TOP):
                    if k > 1:
                        dve.wait_ge(s_acc, 3 * t + k - 1)
                    nc.vector.scalar_tensor_tensor(acc[t % 2][:, :], y_in[t % BUFS][:, k], weights[:, k, t:t + 1],
                                                   acc[t % 2][:, :], ALU.mult, ALU.add).then_inc(s_acc, 1)
                if t:
                    finish(t - 1)
            finish(TT - 1)

        @block.gpsimd
        def _(pool):
            for t in range(TT):
                pool.wait_ge(s_acc, 3 * t + 3)
                nc.gpsimd.tensor_tensor(acc[t % 2][:, :], acc[t % 2][:, :], gate_row[:, 1], ALU.mult).then_inc(s_gate, 1)


def adaln_moe_kernel(nc, d):
    scratch = lambda name, shape, dt=F32: nc.dram_tensor(name, shape, dt, kind="Internal").ap()
    d = dict(d)
    d["qk_parts"] = scratch("qk_parts", (2, 2, D, T))
    d["slots"] = scratch("slots", (NO_SLOT + SLOT_TILE, 1), I32)
    d["x_norm"] = scratch("x_norm", (T + P // 4, D))
    d["tiles"] = scratch("tiles", (2 * E_N, 3), I32)
    d["y_rows"] = scratch("y_rows", (ROWS + P, D))
    with ExitStack() as ctx:
        sb = lambda name, shape, dt=F32: ctx.enter_context(nc.sbuf_tensor(name, shape, dt))
        keep = {
            "ident": sb("ident", [P, P]),
            "mod_col": sb("mod_col", [P, 4, KT]),
            "gate_row": sb("gate_row", [P, 2, D]),
            "x_all": sb("x_all", [P, TT, D]),
            "weights": sb("weights", [P, TOP, TT]),
            "tile_list": sb("tile_list", [1, 6 * E_N], I32),
            "n_tiles": sb("n_tiles", [P, 1], I32),
        }
        with nc.sbuf_tensor("v_all", [P, TT, H, DH + 1], F32) as v_all:
            keep["v_all"] = v_all
            modulation_and_projection(nc, d, keep)
            attention(nc, d, keep)
        route(nc, d, keep)
        experts(nc, d, keep)
        combine(nc, d, keep)


def rotary_tables():
    inv = (np.float32(1.0) / np.float32(10000.0) ** (np.arange(0, DH, 2, dtype=np.float32) / np.float32(DH)))
    angle = np.outer(np.arange(T, dtype=np.float32), inv.astype(np.float32)).astype(np.float32).T
    cos, sin = np.cos(angle).astype(np.float32), np.sin(angle).astype(np.float32)
    return np.concatenate([cos, cos]), np.concatenate([-sin, sin])


def kernel(**inputs):
    import concourse.bacc as bacc
    from concourse.bass_utils import run_bass_kernel_spmd

    a = {n: np.asarray(v) for n, v in inputs.items()}
    cos, sin = rotary_tables()
    bias = a["L0_attn_Wqkv_b"]
    gate_up = lambda g, u: [g[..., :P], u[..., :P]] + ([g[..., P:], u[..., P:]] if g.shape[-1] > P else [])
    arrays = {
        "x": a["L0_attn_x"].reshape(T, D),
        "w_t": a["L0_attn_Wqkv_w"].T,
        "b_qk": bias[:2 * D].reshape(8, P).T,
        "b_v": bias[2 * D:],
        "wmod": a["L0_wmod"],
        "c_col": a["L0_c"].reshape(KT, P).T,
        "cos": cos,
        "sin": sin,
        "gate_t": a["L0_ffn_gate_w"].T,
        "w_gu": np.concatenate(gate_up(a["L0_ffn_Wg"], a["L0_ffn_Wu"]), axis=-1),
        "w_d": a["L0_ffn_Wd"],
        "w_gu_s": np.concatenate(gate_up(a["L0_ffn_cWg"], a["L0_ffn_cWu"]), axis=-1),
        "w_d_s": a["L0_ffn_cWd"],
    }
    arrays = {n: np.ascontiguousarray(v) for n, v in arrays.items()}
    nc = bacc.Bacc("TRN2", target_bir_lowering=False, num_devices=1)
    d = {n: nc.dram_tensor(f"in_{n}", v.shape, mybir.dt.from_np(v.dtype), kind="ExternalInput").ap() for n, v in arrays.items()}
    d["out"] = nc.dram_tensor("out", (T, D), F32, kind="ExternalOutput").ap()
    adaln_moe_kernel(nc, d)
    r = run_bass_kernel_spmd(nc, [{f"in_{n}": v for n, v in arrays.items()}], core_ids=[0])
    return r.results[0]["out"].reshape(1, T, D)
```

```python
from contextlib import ExitStack

import numpy as np
import concourse.bass as bass
from concourse import mybir

F32 = mybir.dt.float32
F32R = mybir.dt.float32r
F16 = mybir.dt.float16
I32 = mybir.dt.int32
U32 = mybir.dt.uint32
ALU = mybir.AluOpType
ACT = mybir.ActivationFunctionType
AX = mybir.AxisListType

P = 128
T, D = 2048, 512
H, DH = 16, 32
KT = D // P
TT = T // P
CH = 512
NCH = T // CH
EPS = 1e-5
WSLOTS = 4
SWAP = [(i + DH // 2) % DH for i in range(DH)]


def wait_apart(eng, sem, value, passed):
    value = eng.to_reg(value)
    eng.wait_ge(passed, 1)
    eng.wait_ge(sem, value)


def modulation_and_projection(nc, d, keep):
    with ExitStack() as ctx:
        sb = lambda name, shape, dt=F32: ctx.enter_context(nc.sbuf_tensor(name, shape, dt))
        sem = lambda name: ctx.enter_context(nc.semaphore(name))
        pb = lambda name: ctx.enter_context(nc.psum_tensor(name, [P, CH], F32))

        wmod = sb("wmod_sb", [P, WSLOTS, KT, D])
        c_col = sb("c_col", [P, KT])
        silu_c = sb("silu_c", [P, KT])
        silu_cb = sb("silu_cb", [P, KT, P])
        floor_t = sb("floor_t", [P, 2, D])
        w_qkv = sb("w_qkv", [P, KT, 3 * D])
        b_qk = sb("b_qk", [P, 8])
        b_v = sb("b_v", [P, D])
        cos_t = sb("cos_t", [P, T])
        sin_t = sb("sin_t", [P, T])
        x_n = sb("x_n", [P, 4, D])
        stats = sb("stats", [P, 4, 6])
        meanvar = sb("meanvar", [P, 4, 2])
        std = sb("std", [P, 4])
        rstd = sb("rstd", [P, 4])
        h_t = sb("h_t", [P, 2, KT, CH])
        biased = sb("biased", [P, 2, CH])
        swapped = sb("swapped", [P, 2, CH])
        by_cos = sb("by_cos", [P, 2, CH])
        rotated = sb("rotated", [P, 2, CH])
        part_hi = sb("part_hi", [P, 2, CH], F32R)
        part_lo = sb("part_lo", [P, 2, CH], F32R)
        eps_col = sb("eps_col", [P, 1])
        tp = [pb(f"tp{i}") for i in range(2)]
        pj = [pb(f"pj{i}") for i in range(4)]
        pm = [pb(f"pm{i}") for i in range(2)]
        ident, mod_col, gate_row, v_all, x_all = (keep[n] for n in ("ident", "mod_col", "gate_row", "v_all", "x_all"))

        s_small = sem("small_loaded")
        s_wmod = [sem(f"wmod{g}_loaded") for g in range(6)]
        s_w = sem("w_loaded")
        s_tab = sem("tables_loaded")
        s_x0 = sem("x_first_loaded")
        s_x = sem("x_rest_loaded")
        s_const = sem("constants_set")
        s_silu = sem("silu_done")
        s_sb = sem("silu_spread")
        s_mod = sem("mod_done")
        s_modc = sem("mod_copied")
        s_flo = sem("gate_floor")
        s_st = sem("stats_done")
        s_mv = sem("meanvar_done")
        s_std = sem("std_done")
        s_rs = sem("rstd_done")
        s_xn = sem("x_n_done")
        s_tp = sem("transposed")
        s_ht = sem("h_t_done")
        s_pj = sem("projected")
        s_bi = sem("biased_done")
        s_v = sem("v_done")
        s_sw = sem("swapped_done")
        s_sw2 = sem("sin_done")
        s_cos = sem("cos_done")
        s_rot = sem("rotated_done")
        s_hi = sem("hi_done")
        s_lo = sem("lo_done")
        s_store = [sem(f"parts{i}_stored") for i in range(2)]

        GROUPS = [0, 1, 3, 4, 2, 5]
        JOBS = 8

        block = ctx.enter_context(nc.Block())

        @block.sync
        def _(sp):
            sp.dma_start(c_col[:, :], d["c_col"]).then_inc(s_small, 16)
            sp.dma_start(b_qk[:, :], d["b_qk"]).then_inc(s_small, 16)
            sp.dma_start(b_v[:, :], d["b_v"].partition_broadcast(P)).then_inc(s_small, 16)
            wm = d["wmod"].rearrange("(k p) (g n) -> g p k n", p=P, n=D)
            xs = d["x"].rearrange("(c t p) n -> c p t n", p=P, t=4)
            sp.dma_start(x_all[:, 0:4], xs[0]).then_inc(s_x0, 16)
            for i, g in enumerate(GROUPS[:2]):
                sp.dma_start(wmod[:, i], wm[g]).then_inc(s_wmod[g], 16)
            w_view = d["w_t"].rearrange("(k p) n -> p k n", p=P)
            for n in range(3):
                sp.dma_start(w_qkv[:, :, n * D:(n + 1) * D], w_view[:, :, n * D:(n + 1) * D]).then_inc(s_w, 16)
            for r in range(4):
                sp.dma_start(cos_t[DH * r:DH * r + DH, :], d["cos"]).then_inc(s_tab, 16)
                sp.dma_start(sin_t[DH * r:DH * r + DH, :], d["sin"]).then_inc(s_tab, 16)
            for c in range(1, NCH):
                sp.dma_start(x_all[:, 4 * c:4 * c + 4], xs[c]).then_inc(s_x, 16)
            for i, g in enumerate(GROUPS[2:], 2):
                if i >= WSLOTS:
                    sp.wait_ge(s_mod, i - WSLOTS + 1)
                sp.dma_start(wmod[:, i % WSLOTS], wm[g]).then_inc(s_wmod[g], 16)
            with sp.Fori(0, NCH) as c:
                for j in range(JOBS):
                    s, o = divmod(j, KT)
                    rows = slice(o * P, (o + 1) * P)
                    sp.wait_ge(s_hi, c * JOBS + j + 1)
                    sp.dma_start(d["qk_parts"][0, s, rows, bass.ds(c * CH, CH)], part_hi[:, j % 2].bitcast(F32)).then_inc(s_store[j % 2], 16)
                    sp.wait_ge(s_lo, c * JOBS + j + 1)
                    sp.dma_start(d["qk_parts"][1, s, rows, bass.ds(c * CH, CH)], part_lo[:, j % 2].bitcast(F32)).then_inc(s_store[j % 2], 16)
            for b in range(2):
                sp.wait_ge(s_store[b], NCH * JOBS * 16)

        @block.gpsimd
        def _(pool):
            nc.gpsimd.memset(ident[:, :], 0.0).then_inc(s_const, 1)
            pool.wait_ge(s_const, 1)
            nc.gpsimd.affine_select(out=ident[:, :], in_=ident[:, :], compare_op=ALU.not_equal, fill=1.0,
                                    base=0, pattern=[[-1, P]], channel_multiplier=1).then_inc(s_const, 1)
            nc.gpsimd.memset(v_all[:, :, :, DH:DH + 1], 1.0).then_inc(s_const, 1)
            nc.gpsimd.memset(eps_col[:, :], EPS).then_inc(s_const, 1)
            pool.wait_ge(s_silu, 1)
            nc.gpsimd.tensor_copy(silu_cb[:, :, :], silu_c[:, :].unsqueeze(2).to_broadcast([P, KT, P])).then_inc(s_sb, 1)
            pool.wait_ge(s_tab, 16 * 8)
            with pool.Fori(0, NCH) as c:
                for j in range(JOBS):
                    wait_apart(pool, s_bi, c * JOBS + j + 1, s_tab)
                    if j >= 2:
                        pool.wait_ge(s_rot, c * JOBS + j - 1)
                    nc.gpsimd.tensor_tensor(by_cos[:, j % 2], biased[:, j % 2], cos_t[:, bass.ds(c * CH, CH)],
                                            ALU.mult).then_inc(s_cos, 1)
                pool.wait_ge(s_rot, c * JOBS + JOBS)

        @block.scalar
        def _(act):
            act.wait_ge(s_small, 48)
            nc.scalar.activation(silu_c[:, :], c_col[:, :], ACT.Silu).then_inc(s_silu, 1)
            act.wait_ge(s_const, 4)

            with act.Fori(0, NCH // 2) as pair:
                for b in range(2):
                    c = pair * 2 + b
                    act.wait_ge(s_mv, c + 1)
                    nc.scalar.activation(std[:, :], meanvar[:, :, 1], ACT.Sqrt, bias=eps_col[:, :]).then_inc(s_std, 1)
                    for k in range(KT):
                        act.wait_ge(s_tp, c * KT + k + 1)
                        if k == 0:
                            act.wait_ge(s_modc, 2)
                        nc.scalar.activation(h_t[:, b, k], tp[k % 2][:, :], ACT.Identity, bias=mod_col[:, 0, k:k + 1],
                                             scale=mod_col[:, 1, k:k + 1]).then_inc(s_ht, 1)
                    for j in range(JOBS):
                        act.wait_ge(s_pj, c * 12 + j + 1)
                        if j >= 2:
                            act.wait_ge(s_cos, c * JOBS + j - 1)
                            act.wait_ge(s_sw, c * JOBS + j - 1)
                        nc.scalar.activation(biased[:, j % 2], pj[j % 4][:, :], ACT.Identity,
                                             bias=b_qk[:, j:j + 1]).then_inc(s_bi, 1)
                        act.wait_ge(s_rot, c * JOBS + j + 1)
                        if j >= 2:
                            act.wait_ge(s_store[j % 2], (c * (JOBS // 2) + j // 2) * 32)
                        nc.scalar.activation(part_hi[:, j % 2], rotated[:, j % 2], ACT.Copy).then_inc(s_hi, 1)
                    for p in range(2):
                        act.wait_ge(s_store[p], (c + 1) * (JOBS * 16))

        @block.vector
        def _(dve):
            def gate(i, g):
                dve.wait_ge(s_mod, 5 + i)
                nc.vector.tensor_scalar(floor_t[:, 0], pm[i][:, :], -1.0, 0.25, ALU.mult, ALU.max).then_inc(s_flo, 1)
                nc.vector.tensor_scalar(floor_t[:, 1], pm[i][:, :], 0.25, None, ALU.max).then_inc(s_flo, 1)
                dve.wait_ge(s_flo, 6 * i + 2)
                nc.vector.tensor_tensor(floor_t[:, 1], floor_t[:, 1], floor_t[:, 0], ALU.max).then_inc(s_flo, 1)
                dve.wait_ge(s_flo, 6 * i + 3)
                nc.vector.tensor_scalar(floor_t[:, 0], pm[i][:, :], 0.0, 2.0, ALU.is_ge, ALU.mult).then_inc(s_flo, 1)
                dve.wait_ge(s_flo, 6 * i + 4)
                nc.vector.tensor_scalar(floor_t[:, 0], floor_t[:, 0], -1.0, None, ALU.add).then_inc(s_flo, 1)
                dve.wait_ge(s_flo, 6 * i + 5)
                nc.vector.tensor_tensor(gate_row[:, i], floor_t[:, 0], floor_t[:, 1], ALU.mult).then_inc(s_flo, 1)
                dve.wait_ge(s_flo, 6 * i + 6)

            def ln(c, b):
                if b == 1:
                    dve.wait_ge(s_x, (NCH - 1) * 16)
                for t in range(4):
                    nc.vector.bn_stats(stats[:, t], x_all[:, bass.ds(c * 4 + t, 1)].rearrange("p o n -> p (o n)")).then_inc(s_st, 1)
                for t in range(4):
                    wait_apart(dve, s_st, c * 4 + t + 1, s_x0)
                    last = nc.vector.bn_aggr(meanvar[:, t], stats[:, t])
                last.then_inc(s_mv, 1)
                dve.wait_ge(s_std, c + 1)
                nc.vector.reciprocal(rstd[:, :], std[:, :]).then_inc(s_rs, 1)
                dve.wait_ge(s_rs, c + 1)
                for t in range(4):
                    last = nc.vector.tensor_scalar(x_n[:, t], x_all[:, bass.ds(c * 4 + t, 1)].rearrange("p o n -> p (o n)"), meanvar[:, t, 0:1], rstd[:, t:t + 1],
                                                   ALU.subtract, ALU.mult)
                    last.then_inc(s_xn, 1)

            for i, g in enumerate(GROUPS[:4]):
                dve.wait_ge(s_mod, i + 1)
                nc.vector.tensor_scalar(mod_col[:, i], pm[i % 2][:, 0:KT], 1.0 if i % 2 else 0.0, None,
                                        ALU.add).then_inc(s_modc, 1)

            dve.wait_ge(s_x0, 16)
            with dve.Fori(0, NCH // 2) as pair:
                for b in range(2):
                    c = pair * 2 + b
                    ln(c, b)
                    for j in range(JOBS):
                        n = c * JOBS + j
                        wait_apart(dve, s_bi, n + 1, s_x0)
                        if j >= 2:
                            dve.wait_ge(s_rot, n - 1)
                        nc.vector.stream_shuffle(swapped[:, j % 2], biased[:, j % 2], SWAP).then_inc(s_sw, 1)
                        dve.wait_ge(s_sw, n + 1)
                        nc.vector.tensor_tensor(swapped[:, j % 2], swapped[:, j % 2], sin_t[:, bass.ds(c * CH, CH)],
                                                ALU.mult).then_inc(s_sw2, 1)
                        dve.wait_ge(s_sw2, n + 1)
                        dve.wait_ge(s_cos, n + 1)
                        if j >= 2:
                            dve.wait_ge(s_lo, n - 1)
                            dve.wait_ge(s_hi, n - 1)
                        nc.vector.tensor_tensor(rotated[:, j % 2], by_cos[:, j % 2], swapped[:, j % 2],
                                                ALU.add).then_inc(s_rot, 1)
                        dve.wait_ge(s_hi, n + 1)
                        if j >= 2:
                            dve.wait_ge(s_store[j % 2], (c * (JOBS // 2) + j // 2) * 32)
                        nc.vector.tensor_tensor(part_lo[:, j % 2], rotated[:, j % 2], part_hi[:, j % 2],
                                                ALU.subtract).then_inc(s_lo, 1)
                    for t in range(4):
                        dve.wait_ge(s_pj, c * 12 + JOBS + t + 1)
                        nc.vector.tensor_tensor(v_all[:, bass.ds(c * 4 + t, 1), :, 0:DH].rearrange("p o h w -> p (o h) w"),
                                                pj[t % 4][:, :].rearrange("p (h w) -> p h w", w=DH),
                                                b_v[:, :].rearrange("p (h w) -> p h w", w=DH), ALU.add).then_inc(s_v, 1)
            gate(0, 2)
            gate(1, 5)

        @block.tensor
        def _(pe):
            pe.wait_ge(s_silu, 1)
            pe.wait_ge(s_const, 4)
            for i, g in enumerate(GROUPS[:4]):
                pe.wait_ge(s_wmod[g], 16)
                if i >= 2:
                    pe.wait_ge(s_modc, i - 1)
                for m in range(KT):
                    for k in range(KT):
                        last = nc.tensor.matmul(pm[i % 2][:, m:m + 1], wmod[:, i % WSLOTS, k, m * P:(m + 1) * P],
                                                silu_c[:, k:k + 1], start=(k == 0), stop=(k == KT - 1))
                last.then_inc(s_mod, 1)
            pe.wait_ge(s_sb, 1)
            pe.wait_ge(s_modc, 4)
            for i, g in enumerate(GROUPS[4:]):
                pe.wait_ge(s_wmod[g], 16)
                for k in range(KT):
                    last = nc.tensor.matmul(pm[i][:, :], silu_cb[:, k], wmod[:, (i + 4) % WSLOTS, k], start=(k == 0),
                                            stop=(k == KT - 1))
                last.then_inc(s_mod, 1)
            pe.wait_ge(s_w, 48)
            with pe.Fori(0, NCH // 2) as pair:
                for b in range(2):
                    c = pair * 2 + b
                    for k in range(KT):
                        pe.wait_ge(s_xn, c * 4 + 4)
                        if k >= 2:
                            pe.wait_ge(s_ht, c * KT + k - 1)
                        for t in range(4):
                            last = nc.tensor.transpose(tp[k % 2][:, t * P:(t + 1) * P], x_n[:, t, k * P:(k + 1) * P],
                                                       ident[:, :])
                        last.then_inc(s_tp, 1)
                    pe.wait_ge(s_ht, (c + 1) * KT)
                    for j in range(JOBS + 4):
                        if j >= 4:
                            pe.wait_ge(s_bi, c * JOBS + j - 3)
                        for k in range(KT):
                            if j < JOBS:
                                last = nc.tensor.matmul(pj[j % 4][:, :], w_qkv[:, k, j * P:(j + 1) * P], h_t[:, b, k],
                                                        start=(k == 0), stop=(k == KT - 1))
                            else:
                                t = j - JOBS
                                last = nc.tensor.matmul(pj[j % 4][:, :], h_t[:, b, k, t * P:(t + 1) * P],
                                                        w_qkv[:, k, 2 * D:3 * D], start=(k == 0), stop=(k == KT - 1))
                        last.then_inc(s_pj, 1)
                    pe.wait_ge(s_v, (c + 1) * 4)



PAIRS = H // 2
BLK = 2 * NCH
QK_ROWS = 3 * DH
MASK = -56576.0


def block_pairs():
    return [(h, c, kt) for h in range(2) for c in range(NCH) for kt in range(0, 4 * c + 4, 2)]


def first_query(c, kt):
    return 0 if c == 0 and kt == 1 else max(0, (kt - 4 * c) * P)


def pv_until(k):
    return 40 * (k // NCH) + 2 * (k % NCH + 1) * (k % NCH + 2)


def max_units():
    return [(i, c, CH if c < i // 4 else (i % 4 + 1) * P) for i in range(TT) for c in range(i // 4 + 1)]


SLOTS = block_pairs()
UNITS = max_units()
LAST_OF_CHUNK = [n for n, (i, c, _) in enumerate(UNITS) if i % 4 == 3 and c == i // 4]
UNIT_FROM = 6


def units_of(slot):
    span = len(SLOTS) - UNIT_FROM - 2
    return [n for n in range(len(UNITS)) if UNIT_FROM + n * span // len(UNITS) == slot]


def attention(nc, d, keep):
    with ExitStack() as ctx:
        sb = lambda name, shape, dt=F32: ctx.enter_context(nc.sbuf_tensor(name, shape, dt))
        sem = lambda name: ctx.enter_context(nc.semaphore(name))
        pb = lambda name, shape: ctx.enter_context(nc.psum_tensor(name, shape, F32))
        ident, v_all, x_all, gate_row = (keep[n] for n in ("ident", "v_all", "x_all", "gate_row"))

        rows = QK_ROWS + 2
        q_st = [[sb(f"q_st{b}{h}", [rows, T], F32R) for h in range(2)] for b in range(2)]
        k_st = [[sb(f"k_st{b}{h}", [rows, T], F32R) for h in range(2)] for b in range(2)]
        v_h = [sb(f"v_h{h}", [P, TT, DH + 1]) for h in range(2)]
        probs = sb("probs", [P, 4, CH])
        o_t = sb("o_t", [P, 2, CH])
        ident16 = sb("ident16", [P, P], F16)
        mask16 = sb("mask16", [P, P], F16)
        fold = sb("fold", [P, DH + 1])
        max_part = sb("max_part", [P, 2, TT, NCH])
        max_q = sb("max_q", [P, 2, 4])
        neg_hi = sb("neg_hi", [P, 2, 4], F32R)
        neg_cols = sb("neg_cols", [P, 2, 2, 4])
        neg_rows = sb("neg_rows", [16, 2, P], F32R)
        rden = sb("rden", [P, 4])
        out_h = sb("out_h", [P, 4, DH])
        s_bank = pb("s_bank", [P, 2, CH])
        m_bank = pb("m_bank", [P, 2, 2, CH])
        o_bank = pb("o_bank", [P, CH])
        misc = pb("misc", [P, CH])

        s_cst = sem("constants_set2")
        s_zero = sem("o_bank_zeroed")
        s_ld = [[sem(f"stack{b}{h}_loaded") for h in range(2)] for b in range(2)]
        s_vh = sem("v_head_copied")
        s_max = sem("max_scores_done")
        s_red = sem("max_reduced")
        s_mq = sem("max_of_chunk_done")
        s_nh = sem("neg_hi_done")
        s_nc = sem("neg_cols_done")
        s_mt = sem("neg_rows_transposed")
        s_mr = sem("neg_rows_copied")
        s_mrow = [sem(f"neg_rows{c}_placed") for c in range(NCH)]
        s_s = sem("scores_done")
        s_exp = sem("exp_done")
        s_mask = sem("probs_masked")
        s_pv = sem("pv_done")
        s_oe = sem("o_t_copied")
        s_comb = sem("o_folded")
        s_rd = sem("denominator_done")
        s_norm = sem("normalized")
        s_og = sem("output_gated")
        s_x2 = sem("x_added")

        block = ctx.enter_context(nc.Block())
        MASKED = [n for n, (h, c, kt) in enumerate(SLOTS) if kt >= 4 * c]

        @block.sync
        def _(sp):
            parts = d["qk_parts"]

            def load(pair, b, h):
                order = [(0, 0), (0, 1), (1, 0)] if h == 0 else [(0, 1), (0, 0), (1, 0)]
                for r, (qp, kp) in enumerate(order):
                    src = bass.ds((pair * 2 + h) * DH, DH)
                    sp.dma_start(q_st[b][h][r * DH:(r + 1) * DH, :].bitcast(F32), parts[qp, 0, src, :]).then_inc(s_ld[b][h], 16)
                    sp.dma_start(k_st[b][h][r * DH:(r + 1) * DH, :].bitcast(F32), parts[kp, 1, src, :]).then_inc(s_ld[b][h], 16)

            def place_max(pair, b, cq):
                sp.wait_ge(s_mr, pair * NCH + cq + 1)
                for h in range(2):
                    for part in range(2):
                        r = h * 8 + part * 4
                        sp.dma_start(q_st[b][h][QK_ROWS + part:QK_ROWS + part + 1, cq * CH:(cq + 1) * CH].bitcast(F32),
                                     neg_rows[r:r + 4, cq % 2, :].bitcast(F32)).then_inc(s_mrow[cq], 16)

            def step(it, s, more):
                st = 2 * it + s
                place_max(st + 1, 1 - s, 0)
                place_max(st + 1, 1 - s, 1)
                if more:
                    sp.wait_ge(s_pv, st * 80 + pv_until(3))
                    load(st + 2, s, 0)
                place_max(st + 1, 1 - s, 2)
                place_max(st + 1, 1 - s, 3)
                if more:
                    sp.wait_ge(s_pv, st * 80 + pv_until(7))
                    load(st + 2, s, 1)

            for b in range(2):
                for h in range(2):
                    load(b, b, h)
            for cq in range(NCH):
                place_max(0, 0, cq)
            with sp.Fori(0, PAIRS // 2 - 1) as it:
                for s in range(2):
                    step(it, s, True)
            step(PAIRS // 2 - 1, 0, False)
            for c in range(NCH):
                sp.wait_ge(s_mrow[c], PAIRS * 64)

        @block.gpsimd
        def _(pool):
            def copy_v(head, h):
                nc.gpsimd.tensor_copy(v_h[h][:, :, :], v_all[:, :, bass.ds(head, 1), :].rearrange("p t o w -> p t (o w)")
                                      ).then_inc(s_vh, 1)

            nc.gpsimd.memset(ident16[:, :], 0.0).then_inc(s_cst, 1)
            nc.gpsimd.memset(mask16[:, :], 0.0).then_inc(s_cst, 1)
            nc.gpsimd.memset(fold[:, :], 0.0).then_inc(s_cst, 1)
            pool.wait_ge(s_cst, 3)
            nc.gpsimd.affine_select(out=ident16[:, :], in_=ident16[:, :], compare_op=ALU.not_equal, fill=1.0,
                                    base=0, pattern=[[-1, P]], channel_multiplier=1).then_inc(s_cst, 1)
            nc.gpsimd.affine_select(out=mask16[:, :], in_=mask16[:, :], compare_op=ALU.is_ge, fill=MASK,
                                    base=0, pattern=[[-1, P]], channel_multiplier=1).then_inc(s_cst, 1)
            nc.gpsimd.affine_select(out=fold[:, :], in_=fold[:, :], compare_op=ALU.not_equal, fill=1.0,
                                    base=0, pattern=[[-1, DH + 1]], channel_multiplier=1).then_inc(s_cst, 1)
            pool.wait_ge(s_cst, 6)
            nc.gpsimd.affine_select(out=fold[:, :], in_=fold[:, :], compare_op=ALU.not_equal, fill=1.0,
                                    base=-P // 2, pattern=[[-1, DH + 1]], channel_multiplier=1).then_inc(s_cst, 1)
            pool.wait_ge(s_cst, 7)
            for h in range(2):
                copy_v(h, h)

            def step(it, s, more):
                st = 2 * it + s
                for n in MASKED:
                    h, c, kt = SLOTS[n]
                    for j in range(2):
                        blk = 2 * n + j
                        wait_apart(pool, s_exp, st * 80 + blk + 1, s_cst)
                        q0 = first_query(c, kt + j)
                        w = (kt + j - 4 * c) * P + P - q0
                        tile = probs[:, blk % 4, q0:q0 + w]
                        nc.gpsimd.affine_select(out=tile, in_=tile, compare_op=ALU.is_ge, fill=0.0,
                                                base=P - w, pattern=[[1, w]], channel_multiplier=-1).then_inc(s_mask, 1)
                    if kt == 4 * c + 2 and c == NCH - 1 and more:
                        wait_apart(pool, s_pv, st * 80 + pv_until(4 * h + 3), s_cst)
                        copy_v(2 * (st + 1) + h, h)

            with pool.Fori(0, PAIRS // 2 - 1) as it:
                for s in range(2):
                    step(it, s, True)
            step(PAIRS // 2 - 1, 0, True)
            step(PAIRS // 2 - 1, 1, False)

        @block.scalar
        def _(act):
            def copy_o(st, k):
                act.wait_ge(s_pv, st * 80 + pv_until(k))
                if k >= 2:
                    act.wait_ge(s_comb, 8 * st + k - 1)
                nc.scalar.activation(o_t[:, k % 2], o_bank[:, :], ACT.Copy).then_inc(s_oe, 1)

            def step(it, s):
                st = 2 * it + s
                ended = None
                for n, (h, c, kt) in enumerate(SLOTS):
                    for j in range(2):
                        blk = 2 * n + j
                        act.wait_ge(s_s, st * 80 + blk + 1)
                        if blk >= 4:
                            act.wait_ge(s_pv, st * 80 + blk - 3)
                        q0 = first_query(c, kt + j)
                        nc.scalar.activation(probs[:, blk % 4, q0:], s_bank[:, blk % 2, q0:], ACT.Exp,
                                             scale=DH ** -0.5).then_inc(s_exp, 1)
                    if ended is not None:
                        copy_o(st, ended)
                    ended = 4 * h + c if kt == 4 * c + 2 else None
                copy_o(st, ended)
                act.wait_ge(s_comb, 8 * st + 8)

            act.wait_ge(s_zero, 1)
            with act.Fori(0, PAIRS // 2 - 1) as it:
                for s in range(2):
                    step(it, s)
            for s in range(2):
                step(PAIRS // 2 - 1, s)

        @block.vector
        def _(dve):
            def reduce_unit(pair, u):
                i, c, w = UNITS[u]
                dve.wait_ge(s_max, pair * len(UNITS) + u + 1)
                nc.vector.tensor_reduce(max_part[:, :, i, c], m_bank[:, u % 2, :, 0:w], AX.X, ALU.max).then_inc(s_red, 1)

            def max_of_chunk(pair, cq):
                m = pair * NCH + cq
                dve.wait_ge(s_red, pair * len(UNITS) + LAST_OF_CHUNK[cq] + 1)
                nc.vector.tensor_reduce(max_q[:, :, :], max_part[:, :, 4 * cq:4 * cq + 4, 0:cq + 1], AX.X,
                                        ALU.max).then_inc(s_mq, 1)
                dve.wait_ge(s_mq, m + 1)
                nc.vector.tensor_scalar(neg_hi[:, :, :], max_q[:, :, :], -1.0, None, ALU.mult).then_inc(s_nh, 1)
                dve.wait_ge(s_nh, m + 1)
                nc.vector.tensor_copy(neg_cols[:, :, 0], neg_hi[:, :, :]).then_inc(s_nc, 1)
                nc.vector.scalar_tensor_tensor(neg_cols[:, :, 1], max_q[:, :, :], -1.0, neg_hi[:, :, :], ALU.mult,
                                               ALU.subtract).then_inc(s_nc, 1)

            def copy_rows(pair, cq):
                dve.wait_ge(s_mt, pair * NCH + cq + 1)
                if cq >= 2:
                    dve.wait_ge(s_mrow[cq - 2], (pair + 1) * 64)
                nc.vector.tensor_copy(neg_rows[:, cq % 2], misc[0:16, 0:P]).then_inc(s_mr, 1)

            def normalize(st, k, head):
                h, c = divmod(k, 4)
                dve.wait_ge(s_comb, 8 * st + k + 1)
                o = misc[:, 0:4 * (DH + 1)].rearrange("p (i w) -> p i w", i=4)
                nc.vector.reciprocal(rden[:, :], o[:, :, DH]).then_inc(s_rd, 1)
                dve.wait_ge(s_rd, 8 * st + k + 1)
                nc.vector.tensor_tensor(out_h[:, :, :], o[:, :, 0:DH], rden[:, :].unsqueeze(2).to_broadcast([P, 4, DH]),
                                        ALU.mult).then_inc(s_norm, 1)
                dve.wait_ge(s_norm, 8 * st + k + 1)
                cols = bass.ds(head * DH, DH)
                nc.vector.tensor_tensor(out_h[:, :, :], out_h[:, :, :], gate_row[:, 0:1, cols].to_broadcast([P, 4, DH]),
                                        ALU.mult).then_inc(s_og, 1)
                dve.wait_ge(s_og, 8 * st + k + 1)
                nc.vector.tensor_tensor(x_all[:, 4 * c:4 * c + 4, cols], x_all[:, 4 * c:4 * c + 4, cols], out_h[:, :, :],
                                        ALU.add).then_inc(s_x2, 1)
                dve.wait_ge(s_x2, 8 * st + k + 1)

            nc.vector.memset(o_bank[:, :], 0.0).then_inc(s_zero, 1)
            for b in range(2):
                for h in range(2):
                    nc.vector.memset(k_st[b][h][QK_ROWS:QK_ROWS + 2, :].bitcast(F32), 1.0).then_inc(s_zero, 1)
            for u in range(len(UNITS)):
                reduce_unit(0, u)
                if u in LAST_OF_CHUNK:
                    max_of_chunk(0, LAST_OF_CHUNK.index(u))
                    copy_rows(0, LAST_OF_CHUNK.index(u))

            def step(it, s, more):
                st = 2 * it + s
                for what, arg in timeline(more):
                    if what == "unit":
                        reduce_unit(st + 1, arg)
                        if arg in LAST_OF_CHUNK:
                            max_of_chunk(st + 1, LAST_OF_CHUNK.index(arg))
                    elif what == "rows":
                        copy_rows(st + 1, arg)
                    elif what == "fold":
                        normalize(st, arg, 2 * st + arg // 4)
                if more:
                    dve.wait_ge(s_mrow[2], (st + 2) * 64)
                    dve.wait_ge(s_mrow[3], (st + 2) * 64)

            with dve.Fori(0, PAIRS // 2 - 1) as it:
                for s in range(2):
                    step(it, s, True)
            step(PAIRS // 2 - 1, 0, True)
            step(PAIRS // 2 - 1, 1, False)

        @block.tensor
        def _(pe):
            def unit(pair, b, u):
                i, c, w = UNITS[u]
                if u >= 2:
                    pe.wait_ge(s_red, pair * len(UNITS) + u - 1)
                last = None
                diagonal = c == i // 4
                for h in range(2):
                    r = slice(h * DH, (h + 1) * DH)
                    last = nc.tensor.matmul(m_bank[:, u % 2, h, 0:w], q_st[b][h][r, i * P:(i + 1) * P],
                                            k_st[b][h][r, c * CH:c * CH + w], start=True, stop=True)
                if diagonal:
                    for h in range(2):
                        last = nc.tensor.matmul(m_bank[:, u % 2, h, w - P:w], ident16[:, :], mask16[:, :],
                                                start=False, stop=True, skip_group_check=True)
                last.then_inc(s_max, 1)

            def rows(pair, cq):
                pe.wait_ge(s_nc, 2 * (pair * NCH + cq) + 2)
                nc.tensor.transpose(misc[0:16, 0:P], neg_cols[:, :, :, :].rearrange("p h s i -> p (h s i)"),
                                    ident[:, :]).then_inc(s_mt, 1)

            def scores(st, s, n):
                h, c, kt = SLOTS[n]
                for j in range(2):
                    blk = 2 * n + j
                    if blk >= 2:
                        pe.wait_ge(s_exp, st * 80 + blk - 1)
                    q0 = first_query(c, kt + j)
                    nc.tensor.matmul(s_bank[:, blk % 2, q0:], k_st[s][h][:, (kt + j) * P:(kt + j + 1) * P],
                                     q_st[s][h][:, c * CH + q0:(c + 1) * CH], start=True, stop=True).then_inc(s_s, 1)

            def pv(st, n):
                h, c, kt = SLOTS[n]
                k = 4 * h + c
                masked = len([m for m in MASKED if m <= n])
                if kt >= 4 * c:
                    pe.wait_ge(s_mask, st * 2 * len(MASKED) + 2 * masked)
                else:
                    pe.wait_ge(s_exp, st * 80 + 2 * n + 2)
                if kt == 0:
                    if c == 0:
                        pe.wait_ge(s_vh, 2 * st + h + 1)
                    if k:
                        pe.wait_ge(s_oe, 8 * st + k)
                for j in range(2):
                    q0 = first_query(c, kt + j)
                    last = nc.tensor.matmul(o_bank[64 * j:64 * j + DH + 1, q0:], v_h[h][:, kt + j, :],
                                            probs[:, (2 * n + j) % 4, q0:], start=(kt == 0), stop=(kt == 4 * c + 2))
                    last.then_inc(s_pv, 1)

            def fold_o(st, k):
                pe.wait_ge(s_oe, 8 * st + k + 1)
                for i in range(4):
                    last = nc.tensor.matmul(misc[:, i * (DH + 1):(i + 1) * (DH + 1)], o_t[:, k % 2, i * P:(i + 1) * P],
                                            fold[:, :], start=True, stop=True)
                last.then_inc(s_comb, 1)

            pe.wait_ge(s_cst, 7)
            pe.wait_ge(s_zero, 5)
            for h in range(2):
                pe.wait_ge(s_ld[0][h], 96)
            for u in range(len(UNITS)):
                unit(0, 0, u)
                if u in LAST_OF_CHUNK:
                    cq = LAST_OF_CHUNK.index(u)
                    if cq:
                        pe.wait_ge(s_mr, cq)
                    rows(0, cq)
            pe.wait_ge(s_mr, NCH)

            def step(it, s, more):
                st = 2 * it + s
                free = None
                for what, arg in timeline(more):
                    if what == "scores":
                        h, c, kt = SLOTS[arg]
                        if h == 0 and kt == 0:
                            pe.wait_ge(s_mrow[c], (st + 1) * 64)
                        scores(st, s, arg)
                    elif what == "pv":
                        pv(st, arg)
                    elif what == "unit":
                        if arg == 0:
                            for h in range(2):
                                pe.wait_ge(s_ld[1 - s][h], (it + 1 + s) * 96)
                        unit(st + 1, 1 - s, arg)
                    elif what == "rows":
                        if free:
                            pe.wait_ge(*free)
                        rows(st + 1, arg)
                        free = (s_mr, (st + 1) * NCH + arg + 1)
                    elif what == "fold":
                        if free:
                            pe.wait_ge(*free)
                        fold_o(st, arg)
                        free = (s_norm, 8 * st + arg + 1)
                pe.wait_ge(*free)

            with pe.Fori(0, PAIRS // 2 - 1) as it:
                for s in range(2):
                    step(it, s, True)
            step(PAIRS // 2 - 1, 0, True)
            step(PAIRS // 2 - 1, 1, False)


def timeline(more):
    out, due, rows = [], [], []
    for n in range(len(SLOTS) + 1):
        if n < len(SLOTS):
            out.append(("scores", n))
        if more:
            for u in units_of(n):
                out.append(("unit", u))
                if u in LAST_OF_CHUNK:
                    rows.append((n + 1, LAST_OF_CHUNK.index(u)))
        for at, cq in [r for r in rows if r[0] == n]:
            out.append(("rows", cq))
        if n:
            out.append(("pv", n - 1))
            h, c, kt = SLOTS[n - 1]
            for at, k in [x for x in due if x[0] == n]:
                out.append(("fold", k))
            if kt == 4 * c + 2:
                due.append((n + 1, 4 * h + c))
    out.append(("fold", 2 * NCH - 1))
    return out


E_N, TOP = 32, 4
SLOT_TILE = 320
SUBS = [(0, P), (P, P), (2 * P, SLOT_TILE - 2 * P)]
REGION = -(-T // SLOT_TILE) * SLOT_TILE
N_MORE = REGION // SLOT_TILE - 1
CHUNKS = E_N // 2
ALL_SLOTS = E_N * REGION
PAIRS_MAX = CHUNKS + T * TOP // SLOT_TILE
LISTED = CHUNKS + E_N
ROWS = T * TOP
SATURATED = 16.6355


def route(nc, d, keep):
    with ExitStack() as ctx:
        sb = lambda name, shape, dt=F32: ctx.enter_context(nc.sbuf_tensor(name, shape, dt))
        sem = lambda name: ctx.enter_context(nc.semaphore(name))
        pb = lambda name, shape: ctx.enter_context(nc.psum_tensor(name, shape, F32))
        ident, mod_col, x_all, weights, tile_list, n_pairs = (
            keep[n] for n in ("ident", "mod_col", "x_all", "weights", "tile_list", "n_pairs"))

        gate_w = sb("gate_w", [P, KT, E_N])
        stats = sb("stats2", [P, 4, 6])
        meanvar = sb("meanvar2", [P, 4, 2])
        std = sb("std2", [P, 4])
        rstd = sb("rstd2", [P, 4])
        eps_col = sb("eps_col2", [P, 1])
        x_n = sb("x_n2", [P, 2, 4, D])
        h_t = sb("h_t2", [P, 2, KT, CH])
        logits = sb("logits", [P, 4, E_N])
        capped = sb("capped", [P, 4, E_N])
        top_v = sb("top_v", [P, 4, 8])
        top_i = sb("top_i", [P, 4, 8], U32)
        top_f = sb("top_f", [P, 4, 8])
        expert_no = sb("expert_no", [P, E_N])
        region_of = sb("region_of", [P, E_N])
        onehot = sb("onehot", [P, TOP, 4, E_N])
        picked = sb("picked", [P, TOP, 4, E_N])
        row_max = sb("row_max", [P, 4])
        top_logit = sb("top_logit", [P, TOP, 4])
        top_exp = sb("top_exp", [P, TOP, 4])
        top_sum = sb("top_sum", [P, 4])
        top_rec = sb("top_rec", [P, 4])
        mask_h = sb("mask_h", [P, 4, E_N], F16)
        count_h = sb("count_h", [P, 5, E_N], F16)
        before = sb("before", [P, P], F16)
        ones_h = sb("ones_h", [P, P], F16)
        slot_f = sb("slot_f", [P, 4, E_N])
        slot_k = sb("slot_k", [P, TOP, 4])
        slot_i = sb("slot_i", [P, NCH, TOP, 4], I32)
        row_no = sb("row_no", [P, TOP, TT], I32)
        blank = sb("blank", [P, 5 * P], I32)
        zero_rows = sb("zero_rows", [P // 4, D])
        chunk_max = sb("chunk_max", [P, CHUNKS])
        flags = sb("flags", [P, N_MORE, CHUNKS])
        flag_sum = sb("flag_sum", [P, N_MORE * CHUNKS])
        ones_f = sb("ones_f", [P, N_MORE * CHUNKS])
        start_v = sb("start_v", [P, N_MORE, CHUNKS])
        chosen = sb("chosen", [P, N_MORE * CHUNKS])
        prod = sb("prod", [P, N_MORE * CHUNKS])
        number_1 = sb("number_1", [P, 1])
        more_f = sb("more_f", [P, 2])
        more_i = sb("more_i", [P, 2], I32)
        first_i = sb("first_i", [P, 2], I32)
        tp = [pb(f"tp2_{i}", [P, CH]) for i in range(2)]
        lg = [pb(f"lg{i}", [P, 4, E_N]) for i in range(2)]
        pos = [pb(f"pos{i}", [P, 4, E_N]) for i in range(2)]
        tot = pb("tot", [P, E_N])

        s_gw = sem("gate_w_loaded")
        s_cst = sem("constants_set3")
        s_cst2 = sem("constants_set4")
        s_blank = sem("slot_list_blank")
        s_blankz = sem("zero_rows_stored")
        s_st = sem("stats_done2")
        s_mv = sem("meanvar_done2")
        s_std = sem("std_done2")
        s_rs = sem("rstd_done2")
        s_xn = sem("x_n_done2")
        s_xns = [sem(f"x_n_stored{i}") for i in range(2)]
        s_tp = sem("transposed2")
        s_ht = sem("h_t_done2")
        s_lg = sem("logits_done")
        s_d = sem("routing_step")
        s_e = sem("top_exp_done")
        s_mask = sem("mask_done")
        s_pos = sem("ranks_done")
        s_slot = sem("slots_done")
        s_scat = sem("slots_placed")
        chain = sem("vector_chain")
        s_zc = sem("count_zeroed")
        s_tot = sem("counts_done")
        s_list = sem("tile_list_done")
        s_lstore = sem("tile_list_stored")
        s_lload = sem("tile_list_loaded")

        block = ctx.enter_context(nc.Block())

        @block.sync
        def _(sp):
            sp.dma_start(gate_w[:, :, :], d["gate_t"].rearrange("(k p) e -> p k e", p=P)).then_inc(s_gw, 16)
            sp.wait_ge(s_cst, 5)
            n = P * 5
            full = ALL_SLOTS // n
            assert full * n == ALL_SLOTS
            sp.dma_start(d["slots"][0:full * n, :].rearrange("(p f) o -> p (f o)", f=n), blank[0:full, :]).then_inc(s_blank, 16)
            sp.dma_start(d["x_norm"][T:T + P // 4, :], zero_rows[:, :]).then_inc(s_blankz, 16)
            for c in range(NCH):
                b = c % 2
                sp.wait_ge(s_xn, c * 4 + 4)
                sp.dma_start(d["x_norm"][c * CH:(c + 1) * CH, :].rearrange("(t p) n -> p t n", p=P),
                             x_n[:, b]).then_inc(s_xns[b], 16)
            sp.wait_ge(s_list, 2)
            sp.dma_start(d["tiles"][0:CHUNKS, :], first_i[0:CHUNKS, :]).then_inc(s_lstore, 16)
            sp.dma_start(d["tiles"][CHUNKS:LISTED, :], more_i[0:LISTED - CHUNKS, :]).then_inc(s_lstore, 16)
            sp.wait_ge(s_lstore, 32)
            sp.dma_start(tile_list[0:1, :], d["tiles"].rearrange("(o a) b -> o (a b)", o=1)).then_inc(s_lload, 16)
            sp.wait_ge(s_lload, 16)
            sp.wait_ge(s_blankz, 16)
            for b in range(2):
                sp.wait_ge(s_xns[b], 16 * NCH // 2)

        @block.gpsimd
        def _(pool):
            nc.gpsimd.iota(blank[:, :], [[0, 5], [1, P]], base=ROWS, channel_multiplier=0).then_inc(s_cst, 1)
            nc.gpsimd.memset(zero_rows[:, :], 0.0).then_inc(s_cst, 1)
            nc.gpsimd.memset(ones_h[:, :], 1.0).then_inc(s_cst, 1)
            nc.gpsimd.memset(eps_col[:, :], EPS).then_inc(s_cst, 1)
            nc.gpsimd.memset(ones_f[:, :], 1.0).then_inc(s_cst, 1)
            pool.wait_ge(s_cst, 5)
            nc.gpsimd.affine_select(out=before[:, :], in_=ones_h[:, :], compare_op=ALU.is_gt, fill=0.0,
                                    base=0, pattern=[[1, P]], channel_multiplier=-1).then_inc(s_cst2, 1)
            nc.gpsimd.iota(expert_no[:, :], [[1, E_N]], base=0, channel_multiplier=0,
                           allow_small_or_imprecise_dtypes=True).then_inc(s_cst2, 1)
            nc.gpsimd.iota(region_of[:, :], [[REGION, E_N]], base=0, channel_multiplier=0,
                           allow_small_or_imprecise_dtypes=True).then_inc(s_cst2, 1)
            nc.gpsimd.iota(row_no[:, :, :], [[1, TOP], [TOP * P, TT]], base=0, channel_multiplier=TOP).then_inc(s_cst2, 1)
            nc.gpsimd.iota(start_v[:, :, :], [[SLOT_TILE, N_MORE], [2 * REGION, CHUNKS]], base=SLOT_TILE,
                           channel_multiplier=0, allow_small_or_imprecise_dtypes=True).then_inc(s_cst2, 1)
            nc.gpsimd.iota(number_1[:, :], [[0, 1]], base=1, channel_multiplier=1,
                           allow_small_or_imprecise_dtypes=True).then_inc(s_cst2, 1)
            nc.gpsimd.iota(first_i[:, 0:1], [[0, 1]], base=0, channel_multiplier=1).then_inc(s_cst2, 1)
            nc.gpsimd.iota(first_i[:, 1:2], [[0, 1]], base=0, channel_multiplier=2 * REGION).then_inc(s_cst2, 1)
            pool.wait_ge(s_blank, 16)
            for c in range(NCH):
                b = c % 2
                pool.wait_ge(s_slot, c + 1)
                for t in range(4):
                    for k in range(TOP):
                        nc.gpsimd.indirect_dma_start(
                            out=d["slots"], out_offset=bass.IndirectOffsetOnAxis(ap=slot_i[:, c, k, t:t + 1], axis=0),
                            in_=row_no[:, k, 4 * c + t:4 * c + t + 1], in_offset=None).then_inc(s_scat, 16)
            pool.wait_ge(s_scat, 16 * TOP * TT)

        @block.scalar
        def _(act):
            for c in range(NCH):
                b = c % 2
                act.wait_ge(s_mv, c + 1)
                nc.scalar.activation(std[:, :], meanvar[:, :, 1], ACT.Sqrt, bias=eps_col[:, :]).then_inc(s_std, 1)
                for k in range(KT):
                    act.wait_ge(s_tp, c * KT + k + 1)
                    nc.scalar.activation(h_t[:, b, k], tp[k % 2][:, :], ACT.Identity, bias=mod_col[:, 2, k:k + 1],
                                         scale=mod_col[:, 3, k:k + 1]).then_inc(s_ht, 1)
                act.wait_ge(s_d, c * 2 + 1)
                nc.scalar.activation(top_exp[:, :, :], top_logit[:, :, :], ACT.Exp).then_inc(s_e, 1)

        @block.vector
        def _(dve):
            spread_e = lambda ap: ap.unsqueeze(1).to_broadcast([P, 4, E_N])

            def normalize(c, b):
                for t in range(4):
                    nc.vector.bn_stats(stats[:, t], x_all[:, c * 4 + t]
                                       ).then_inc(s_st, 1)
                for t in range(4):
                    dve.wait_ge(s_st, c * 4 + t + 1)
                    last = nc.vector.bn_aggr(meanvar[:, t], stats[:, t])
                last.then_inc(s_mv, 1)
                dve.wait_ge(s_std, c + 1)
                nc.vector.reciprocal(rstd[:, :], std[:, :]).then_inc(s_rs, 1)
                dve.wait_ge(s_rs, c + 1)
                for t in range(4):
                    nc.vector.tensor_scalar(x_n[:, b, t], x_all[:, c * 4 + t],
                                            meanvar[:, t, 0:1], rstd[:, t:t + 1],
                                            ALU.subtract, ALU.mult).then_inc(s_xn, 1)

            def choose(c, b):
                steps = [0]

                def link(ins):
                    steps[0] += 1
                    ins.then_inc(chain, 1)
                    dve.wait_ge(chain, c * LINKS + steps[0])

                dve.wait_ge(s_lg, c + 1)
                link(nc.vector.tensor_copy(logits[:, :, :], lg[b][:, :, :]))
                link(nc.vector.tensor_scalar(capped[:, :, :], logits[:, :, :], SATURATED, None, ALU.min))
                for t in range(4):
                    link(nc.vector.max(top_v[:, t], capped[:, t]))
                    link(nc.vector.max_index(top_i[:, t], top_v[:, t], capped[:, t]))
                link(nc.vector.tensor_copy(top_f[:, :, :], top_i[:, :, :]))
                for k in range(TOP):
                    link(nc.vector.tensor_tensor(onehot[:, k], top_f[:, :, k].unsqueeze(2).to_broadcast([P, 4, E_N]),
                                                 spread_e(expert_no[:, :]), ALU.is_equal))
                with nc.allow_low_precision("ones and zeros"):
                    link(nc.vector.tensor_reduce(mask_h[:, :, :], onehot[:, :, :, :].rearrange("p k t e -> p t e k"),
                                                 AX.X, ALU.add))
                for t in range(3):
                    link(nc.vector.tensor_tensor(count_h[:, t + 1], count_h[:, t], mask_h[:, t], ALU.add))
                nc.vector.tensor_tensor(count_h[:, 4], count_h[:, 3], mask_h[:, 3], ALU.add).then_inc(s_mask, 1)
                dve.wait_ge(s_mask, c + 1)
                link(nc.vector.tensor_reduce(row_max[:, :], logits[:, :, :], AX.X, ALU.max))
                for k in range(TOP):
                    link(nc.vector.tensor_tensor(picked[:, k], onehot[:, k], logits[:, :, :], ALU.mult))
                link(nc.vector.tensor_reduce(top_logit[:, :, :], picked[:, :, :, :], AX.X, ALU.add))
                nc.vector.tensor_tensor(top_logit[:, :, :], top_logit[:, :, :],
                                        row_max[:, :].unsqueeze(1).to_broadcast([P, TOP, 4]), ALU.subtract
                                        ).then_inc(s_d, 1)
                dve.wait_ge(s_d, 2 * c + 1)
                dve.wait_ge(s_pos, c + 1)
                link(nc.vector.tensor_tensor(slot_f[:, :, :], pos[b][:, :, :], spread_e(region_of[:, :]), ALU.add))
                for k in range(TOP):
                    link(nc.vector.tensor_tensor(picked[:, k], onehot[:, k], slot_f[:, :, :], ALU.mult))
                link(nc.vector.tensor_reduce(slot_k[:, :, :], picked[:, :, :, :], AX.X, ALU.add))
                nc.vector.tensor_copy(slot_i[:, c], slot_k[:, :, :]).then_inc(s_slot, 1)
                dve.wait_ge(s_slot, c + 1)
                dve.wait_ge(s_e, c + 1)
                link(nc.vector.tensor_reduce(top_sum[:, :], top_exp[:, :, :].rearrange("p k t -> p t k"), AX.X, ALU.add))
                link(nc.vector.reciprocal(top_rec[:, :], top_sum[:, :]))
                link(nc.vector.tensor_tensor(weights[:, :, 4 * c:4 * c + 4], top_exp[:, :, :],
                                             top_rec[:, :].unsqueeze(1).to_broadcast([P, TOP, 4]), ALU.mult))
                nc.vector.tensor_copy(count_h[:, 0], count_h[:, 4]).then_inc(s_d, 1)
                dve.wait_ge(s_d, 2 * c + 2)
                assert steps[0] == LINKS

            LINKS = 34
            with nc.allow_low_precision("a count of zero"):
                nc.vector.memset(count_h[:, 0], 0.0).then_inc(s_zc, 1)
            dve.wait_ge(s_zc, 1)
            dve.wait_ge(s_gw, 16)
            dve.wait_ge(s_cst2, 8)
            for c in range(NCH):
                b = c % 2
                if c >= 2:
                    dve.wait_ge(s_xns[b], 16 * (c // 2))
                normalize(c, b)
                choose(c, b)

            last = [NCH * LINKS]

            def link(ins):
                last[0] += 1
                ins.then_inc(chain, 1)
                dve.wait_ge(chain, last[0])

            dve.wait_ge(s_tot, 1)
            link(nc.vector.tensor_reduce(chunk_max[:, :], tot[:, :].rearrange("p (c two) -> p c two", two=2), AX.X, ALU.max))
            for r in range(N_MORE):
                link(nc.vector.tensor_scalar(flags[:, r], chunk_max[:, :], float((r + 1) * SLOT_TILE), None, ALU.is_gt))
            flat = flags[:, :, :].rearrange("p r c -> p (r c)")
            link(nc.vector.tensor_tensor_scan(flag_sum[:, :], ones_f[:, :], flat, 0.0, ALU.mult, ALU.add))
            link(nc.vector.tensor_scalar(chosen[:, :], flag_sum[:, :], number_1[:, 0:1], None, ALU.is_equal))
            link(nc.vector.tensor_tensor(chosen[:, :], chosen[:, :], flat, ALU.mult))
            link(nc.vector.tensor_tensor(prod[:, :], chosen[:, :], start_v[:, :, :].rearrange("p r c -> p (r c)"), ALU.mult))
            link(nc.vector.tensor_reduce(more_f[:, 1:2], prod[:, :], AX.X, ALU.add))
            link(nc.vector.tensor_tensor(flags[:, :, :], chosen[:, :].rearrange("p (r c) -> p r c", c=CHUNKS),
                                         expert_no[:, 0:CHUNKS].unsqueeze(1).to_broadcast([P, N_MORE, CHUNKS]), ALU.mult))
            link(nc.vector.tensor_reduce(more_f[:, 0:1], flags[:, :, :], AX.XY, ALU.add))
            nc.vector.tensor_copy(more_i[:, :], more_f[:, :]).then_inc(s_list, 1)
            nc.vector.tensor_scalar(n_pairs[:, 0:1], flag_sum[:, N_MORE * CHUNKS - 1:], float(CHUNKS), None,
                                    ALU.add).then_inc(s_list, 1)
            dve.wait_ge(s_list, 2)

        @block.tensor
        def _(pe):
            pe.wait_ge(s_gw, 16)
            pe.wait_ge(s_cst2, 8)
            for c in range(NCH):
                b = c % 2
                pe.wait_ge(s_xn, c * 4 + 4)
                for k in range(KT):
                    if k >= 2:
                        pe.wait_ge(s_ht, c * KT + k - 1)
                    for t in range(4):
                        last = nc.tensor.transpose(tp[k % 2][:, t * P:(t + 1) * P], x_n[:, b, t, k * P:(k + 1) * P],
                                                   ident[:, :])
                    last.then_inc(s_tp, 1)
                pe.wait_ge(s_ht, (c + 1) * KT)
                for t in range(4):
                    for k in range(KT):
                        last = nc.tensor.matmul(lg[b][:, t], h_t[:, b, k, t * P:(t + 1) * P], gate_w[:, k],
                                                start=(k == 0), stop=(k == KT - 1))
                last.then_inc(s_lg, 1)
                pe.wait_ge(s_mask, c + 1)
                nc.tensor.matmul(pos[b][:, :, :], before[:, :], mask_h[:, :, :], start=True, stop=False)
                nc.tensor.matmul(pos[b][:, :, :], ones_h[:, :], count_h[:, 0:4], start=False, stop=True).then_inc(s_pos, 1)
            pe.wait_ge(s_d, 2 * NCH)
            nc.tensor.matmul(tot[:, :], ones_h[:, :], count_h[:, 4], start=True, stop=True).then_inc(s_tot, 1)


I_BIG, I_SMALL = 192, 128
SMALL_SCALE = 0.05
GU_COLS = 2 * I_BIG
JOBS_GU = [("big", 0, P), ("big", P, P), ("big", 2 * P, P), ("small", 0, P), ("small", P, P)]


def experts(nc, d, keep):
    with ExitStack() as ctx:
        sb = lambda name, shape, dt=F32: ctx.enter_context(nc.sbuf_tensor(name, shape, dt))
        sem = lambda name: ctx.enter_context(nc.semaphore(name))
        pb = lambda name, shape: ctx.enter_context(nc.psum_tensor(name, shape, F32))
        ident, mod_col, tile_list, n_pairs = (keep[n] for n in ("ident", "mod_col", "tile_list", "n_pairs"))
        REST = I_BIG - P

        w_gu = [sb(f"w_gu{b}", [P, KT, GU_COLS]) for b in range(2)]
        w_d = [sb(f"w_d{b}", [P, 2, D]) for b in range(2)]
        c_gu = sb("c_gu", [P, KT, 2 * I_SMALL])
        c_d = sb("c_d", [P, D])
        w_gu_p = [sb(f"w_gu_p{b}", [P, 2, KT, GU_COLS], F32R) for b in range(2)]
        w_d_p = [sb(f"w_d_p{b}", [P, 2, 2, D], F32R) for b in range(2)]
        c_gu_p = sb("c_gu_p", [P, 2, KT, 2 * I_SMALL], F32R)
        c_d_p = sb("c_d_p", [P, 2, D], F32R)
        rows_g = [sb(f"rows_g{b}", [P, 3], I32) for b in range(2)]
        rows_i = [sb(f"rows_i{b}", [P, 3], I32) for b in range(2)]
        toks_i = [sb(f"toks_i{b}", [P, 3], I32) for b in range(2)]
        x_g = [sb(f"x_g{b}", [P, 3, D]) for b in range(2)]
        x_t = sb("x_t", [P, KT, SLOT_TILE])
        x_p = sb("x_p", [P, 2, KT, SLOT_TILE], F32R)
        gated = sb("gated", [P, 3, SLOT_TILE])
        act_t = sb("act_t", [P, 3, SLOT_TILE])
        a_p = sb("a_p", [P, 3, 2, SLOT_TILE], F32R)
        y_sb = [sb(f"y_sb{b}", [P, 3, D]) for b in range(2)]
        gu = [pb(f"gu{j}", [P, CH]) for j in range(5)]
        yb = [pb(f"y{j}", [P, D]) for j in range(2)]
        tp = [pb("tp3", [P, CH]), gu[0]]

        s_rg = [sem(f"gather_rows{b}_loaded") for b in range(2)]
        s_ri = [sem(f"scatter_rows{b}_loaded") for b in range(2)]
        s_wgu = [sem(f"w_gu{b}_loaded") for b in range(2)]
        s_wd = [sem(f"w_d{b}_loaded") for b in range(2)]
        s_c = sem("chunk_loaded")
        s_wgh, s_wgl = sem("w_gu_high"), sem("w_gu_low")
        s_wdh, s_wdl = sem("w_d_high"), sem("w_d_low")
        s_cgh, s_cgl = sem("chunk_gu_high"), sem("chunk_gu_low")
        s_cdh, s_cdl = sem("chunk_d_high"), sem("chunk_d_low")
        s_tok = sem("tokens_done")
        s_xg = [sem(f"x_gathered{b}") for b in range(2)]
        s_tp = sem("x_transposed")
        s_xt = sem("x_t_done")
        s_xh, s_xl = sem("x_high"), sem("x_low")
        s_gu = sem("gate_up_done")
        s_silu = sem("silu_done2")
        s_act = sem("act_done")
        s_ah, s_al = sem("act_high"), sem("act_low")
        s_y = sem("y_done")
        s_yc = sem("y_copied")
        s_ys = [sem(f"y_stored{b}") for b in range(2)]
        one = sem("always_one")

        block = ctx.enter_context(nc.Block())

        def bound(eng):
            return eng.value_load(n_pairs[0:1, 0:1], min_val=CHUNKS, max_val=PAIRS_MAX)

        @block.sync
        def _(sp):
            def entry(it, what, top):
                return sp.value_load(tile_list[0:1, bass.ds(it * 2 + what, 1)], min_val=0, max_val=top)

            def pair_of(it):
                return (entry(it, 0, CHUNKS - 1), entry(it, 1, (E_N - 2) * REGION + REGION - SLOT_TILE))

            def load_rows(pair, b, to, loaded):
                start = pair[1]
                s = start + b * REGION
                n = SLOT_TILE // P
                sp.dma_start(to[b][:, 0:n], d["slots"][bass.ds(s, n * P), :].rearrange("(p j) o -> p (j o)", p=P)
                             ).then_inc(loaded[b], 16)
                sp.dma_start(to[b][0:SLOT_TILE - n * P, n:n + 1], d["slots"][bass.ds(s + n * P, SLOT_TILE - n * P), :]
                             ).then_inc(loaded[b], 16)

            def load_weights(pair, b):
                e = pair[0] * 2 + b
                sp.dma_start(w_gu[b][:, :, :], d["w_gu"][bass.ds(e, 1)].rearrange("o (k p) n -> p (o k) n", p=P)).then_inc(s_wgu[b], 16)
                sp.dma_start(w_d[b][:, 0, :], d["w_d"][bass.ds(e, 1), 0:P].rearrange("o p n -> p (o n)")).then_inc(s_wd[b], 16)
                for half in range(2):
                    sp.dma_start(w_d[b][half * REST:(half + 1) * REST, 1, :],
                                 d["w_d"][bass.ds(e, 1), P:I_BIG].rearrange("o p n -> p (o n)")).then_inc(s_wd[b], 16)

            def load_chunk(pair):
                c = pair[0]
                sp.dma_start(c_gu[:, :, :], d["w_gu_s"][bass.ds(c, 1)].rearrange("o (k p) n -> p (o k) n", p=P)).then_inc(s_c, 16)
                sp.dma_start(c_d[:, :], d["w_d_s"][bass.ds(c, 1)].rearrange("o p n -> p (o n)")).then_inc(s_c, 16)

            n = bound(sp)
            pair = pair_of(0)
            for b in range(2):
                load_rows(pair, b, rows_g, s_rg)
            load_weights(pair, 0)
            load_chunk(pair)
            load_weights(pair, 1)
            for b in range(2):
                load_rows(pair, b, rows_i, s_ri)
            with sp.Fori(0, n) as it:
                pair = pair_of(it + 1)
                for b in range(2):
                    g = it * 2 + b
                    wait_apart(sp, s_wgl, g + 1, one)
                    sp.wait_ge(s_wdl, g + 1)
                    load_weights(pair, b)
                    wait_apart(sp, s_tok, g + 1, one)
                    load_rows(pair, b, rows_g, s_rg)
                    if b == 0:
                        wait_apart(sp, s_cgl, it + 1, one)
                        sp.wait_ge(s_cdl, it + 1)
                        load_chunk(pair)
                    else:
                        for h in range(2):
                            wait_apart(sp, s_ys[h], it * 48 + 48, one)
                            load_rows(pair, h, rows_i, s_ri)
            lists, gate_ups, downs, stored = (sp.to_reg(v) for v in (n * 32 + 32, n * 16 + 16, n * 48 + 48, n * 48))
            wait_apart(sp, s_c, lists, one)
            for b in range(2):
                sp.wait_ge(s_wgu[b], gate_ups)
                sp.wait_ge(s_wd[b], downs)
                sp.wait_ge(s_rg[b], lists)
                sp.wait_ge(s_ri[b], lists)
                sp.wait_ge(s_ys[b], stored)

        @block.gpsimd
        def _(pool):
            def gather(g, b):
                wait_apart(pool, s_tok, g + 1, one)
                for j, (s0, n) in enumerate(SUBS):
                    nc.gpsimd.indirect_dma_start(
                        out=x_g[b][0:n, j, :], out_offset=None, in_=d["x_norm"],
                        in_offset=bass.IndirectOffsetOnAxis(ap=toks_i[b][0:n, j:j + 1], axis=0)).then_inc(s_xg[b], 16)

            pool.sem_inc(one, 1)
            n = bound(pool)
            gather(0, 0)
            with pool.Fori(0, n) as it:
                for b in range(2):
                    g = it * 2 + b
                    gather(g + 1, 1 - b)
                    for j, (s0, m) in enumerate(SUBS):
                        wait_apart(pool, s_yc, g * 3 + j + 1, one)
                        nc.gpsimd.indirect_dma_start(
                            out=d["y_rows"], out_offset=bass.IndirectOffsetOnAxis(ap=rows_i[b][0:m, j:j + 1], axis=0),
                            in_=y_sb[b][0:m, j, :], in_offset=None).then_inc(s_ys[b], 16)

        @block.scalar
        def _(act):
            def weights_high(pair, b):
                act.wait_ge(s_wgu[b], pair * 16 + 16)
                nc.scalar.activation(w_gu_p[b][:, 0], w_gu[b][:, :, :], ACT.Copy).then_inc(s_wgh, 1)
                act.wait_ge(s_wd[b], pair * 48 + 48)
                nc.scalar.activation(w_d_p[b][:, 0], w_d[b][:, :, :], ACT.Copy).then_inc(s_wdh, 1)

            def chunk_gu_high(it):
                act.wait_ge(s_c, it * 32 + 32)
                nc.scalar.activation(c_gu_p[:, 0], c_gu[:, :, :], ACT.Copy).then_inc(s_cgh, 1)

            def modulate(g, k):
                act.wait_ge(s_tp, g * KT + k + 1)
                nc.scalar.activation(x_t[:, k], tp[k % 2][:, 0:SLOT_TILE], ACT.Identity, bias=mod_col[:, 2, k:k + 1],
                                     scale=mod_col[:, 3, k:k + 1]).then_inc(s_xt, 1)

            def x_high(g):
                act.wait_ge(s_xt, g * KT + KT)
                nc.scalar.activation(x_p[:, 0], x_t[:, :, :], ACT.Copy).then_inc(s_xh, 1)

            def gate(g, j):
                act.wait_ge(s_gu, g * 5 + (1, 3, 4)[j])
                rows = slice(0, REST) if j == 1 else slice(0, P)
                nc.scalar.activation(gated[rows, j], gu[(0, 2, 3)[j]][rows, 0:SLOT_TILE], ACT.Silu).then_inc(s_silu, 1)

            def act_high(g, j):
                rows = slice(0, REST) if j == 1 else slice(0, P)
                act.wait_ge(s_act, g * 3 + j + 1)
                nc.scalar.activation(a_p[rows, j, 0], act_t[rows, j], ACT.Copy).then_inc(s_ah, 1)

            n = bound(act)
            weights_high(0, 0)
            chunk_gu_high(0)
            for k in range(KT):
                modulate(0, k)
            x_high(0)
            with act.Fori(0, n) as it:
                for b in range(2):
                    g = it * 2 + b
                    weights_high(it + b, 1 - b)
                    if b == 0:
                        act.wait_ge(s_c, it * 32 + 32)
                        nc.scalar.activation(c_d_p[:, 0], c_d[:, :], ACT.Copy).then_inc(s_cdh, 1)
                    gate(g, 0)
                    act_high(g, 0)
                    gate(g, 1)
                    act_high(g, 1)
                    gate(g, 2)
                    act.wait_ge(s_xl, g + 1)
                    modulate(g + 1, 0)
                    act_high(g, 2)
                    for k in range(1, KT):
                        modulate(g + 1, k)
                    x_high(g + 1)
                    act.wait_ge(s_ri[b], it * 32 + 32)
                    for i, (s0, m) in enumerate(SUBS):
                        act.wait_ge(s_y, g * 3 + i + 1)
                        nc.scalar.activation(y_sb[b][0:m, i, :], yb[i % 2][0:m, :], ACT.Copy).then_inc(s_yc, 1)
                        if i == 0 and b == 1:
                            chunk_gu_high(it + 1)

        @block.vector
        def _(dve):
            def low(part, whole, high, done):
                nc.vector.tensor_tensor(part, whole, high, ALU.subtract).then_inc(done, 1)

            def weights_low(g, b):
                dve.wait_ge(s_wgh, g + 1)
                low(w_gu_p[b][:, 1], w_gu[b][:, :, :], w_gu_p[b][:, 0], s_wgl)
                dve.wait_ge(s_wdh, g + 1)
                low(w_d_p[b][:, 1], w_d[b][:, :, :], w_d_p[b][:, 0], s_wdl)

            def chunk_gu_low(it):
                dve.wait_ge(s_cgh, it + 1)
                low(c_gu_p[:, 1], c_gu[:, :, :], c_gu_p[:, 0], s_cgl)

            def x_low(g):
                dve.wait_ge(s_xh, g + 1)
                low(x_p[:, 1], x_t[:, :, :], x_p[:, 0], s_xl)

            def tokens(pair, b):
                dve.wait_ge(s_rg[b], pair * 32 + 32)
                for j, (s0, n) in enumerate(SUBS):
                    last = nc.vector.tensor_scalar(toks_i[b][0:n, j:j + 1], rows_g[b][0:n, j:j + 1], 2, None,
                                                   ALU.logical_shift_right)
                last.then_inc(s_tok, 1)

            tokens(0, 0)
            tokens(0, 1)
            weights_low(0, 0)
            chunk_gu_low(0)
            x_low(0)
            n = bound(dve)
            with dve.Fori(0, n) as it:
                for b in range(2):
                    g = it * 2 + b
                    weights_low(g + 1, 1 - b)
                    for j in range(3):
                        rows = slice(0, REST) if j == 1 else slice(0, P)
                        dve.wait_ge(s_silu, g * 3 + j + 1)
                        dve.wait_ge(s_gu, g * 5 + (2, 3, 5)[j])
                        if j == 2:
                            nc.vector.scalar_tensor_tensor(act_t[:, 2], gated[:, 2], SMALL_SCALE, gu[4][:, 0:SLOT_TILE],
                                                           ALU.mult, ALU.mult).then_inc(s_act, 1)
                        else:
                            up = gu[1][:, 0:SLOT_TILE] if j == 0 else gu[2][REST:P, 0:SLOT_TILE]
                            nc.vector.tensor_tensor(act_t[rows, j], gated[rows, j], up, ALU.mult).then_inc(s_act, 1)
                        dve.wait_ge(s_ah, g * 3 + j + 1)
                        if j == 1:
                            low(a_p[REST:P, 1, 0], act_t[rows, 1], a_p[rows, 1, 0], s_al)
                        else:
                            low(a_p[:, j, 1], act_t[:, j], a_p[:, j, 0], s_al)
                        if j == 1 and b == 0:
                            dve.wait_ge(s_cdh, it + 1)
                            low(c_d_p[:, 1], c_d[:, :], c_d_p[:, 0], s_cdl)
                    x_low(g + 1)
                    if b == 1:
                        chunk_gu_low(it + 1)
                    dve.wait_ge(s_xg[b], it * 48 + 48)
                    tokens(it + 1, b)

        @block.tensor
        def _(pe):
            def transpose_x(g, b, k):
                if k >= 2:
                    pe.wait_ge(s_xt, g * KT + k - 1)
                for j, (s0, n) in enumerate(SUBS):
                    last = nc.tensor.transpose(tp[k % 2][:, s0:s0 + n], x_g[b][0:n, j, k * P:(k + 1) * P], ident[0:n, 0:n])
                last.then_inc(s_tp, 1)

            n = bound(pe)
            pe.wait_ge(s_xg[0], 48)
            for k in range(KT):
                transpose_x(0, 0, k)
            THREE = ((0, 0), (0, 1), (1, 0))
            with pe.Fori(0, n) as it:
                for b in range(2):
                    g = it * 2 + b
                    pe.wait_ge(s_wgl, g + 1)
                    pe.wait_ge(s_xl, g + 1)
                    for j, (which, c0, cols) in enumerate(JOBS_GU):
                        if j == 3 and b == 0:
                            pe.wait_ge(s_cgl, it + 1)
                        w = w_gu_p[b] if which == "big" else c_gu_p
                        for k in range(KT):
                            for wp, xp in THREE:
                                last = nc.tensor.matmul(gu[j][:, 0:SLOT_TILE], w[:, wp, k, c0:c0 + cols], x_p[:, xp, k],
                                                        start=(k == 0 and (wp, xp) == (0, 0)),
                                                        stop=(k == KT - 1 and (wp, xp) == (1, 0)))
                        last.then_inc(s_gu, 1)
                    pe.wait_ge(s_xg[1 - b], (it + b) * 48 + 48)
                    pe.wait_ge(s_act, g * 3 + 1)
                    for k in range(KT):
                        transpose_x(g + 1, 1 - b, k)
                    pe.wait_ge(s_wdl, g + 1)
                    if b == 0:
                        pe.wait_ge(s_cdl, it + 1)
                    for i, (s0, m) in enumerate(SUBS):
                        if i == 2:
                            pe.wait_ge(s_yc, g * 3 + 1)
                        rows = slice(s0, s0 + m)
                        for j in range(3):
                            if i == 0:
                                pe.wait_ge(s_al, g * 3 + j + 1)
                            w = c_d_p if j == 2 else w_d_p[b][:, :, j]
                            if j == 1:
                                nc.tensor.matmul(yb[i % 2][0:m, :], a_p[:, 1, 0, rows], w[:, 0], start=False, stop=False)
                                nc.tensor.matmul(yb[i % 2][0:m, :], a_p[0:REST, 1, 0, rows], w[0:REST, 1],
                                                 start=False, stop=False)
                            else:
                                for ap, wp in THREE:
                                    last = nc.tensor.matmul(yb[i % 2][0:m, :], a_p[:, j, ap, rows], w[:, wp],
                                                            start=(j == 0 and (ap, wp) == (0, 0)),
                                                            stop=(j == 2 and (ap, wp) == (1, 0)))
                        last.then_inc(s_y, 1)


def combine(nc, d, keep):
    with ExitStack() as ctx:
        sb = lambda name, shape, dt=F32: ctx.enter_context(nc.sbuf_tensor(name, shape, dt))
        sem = lambda name: ctx.enter_context(nc.semaphore(name))
        x_all, gate_row, weights = (keep[n] for n in ("x_all", "gate_row", "weights"))
        BUFS = 4
        y_in = [sb(f"y_in{b}", [P, TOP, D]) for b in range(BUFS)]
        acc = [sb(f"acc{b}", [P, D]) for b in range(2)]
        res = [sb(f"res{b}", [P, D]) for b in range(2)]
        s_in = [sem(f"y_in{b}_loaded") for b in range(BUFS)]
        s_w0 = sem("first_weighed")
        s_acc = sem("weighed")
        s_gate = sem("gated_done")
        s_res = sem("result_done")
        s_out = [sem(f"out{b}_stored") for b in range(2)]
        block = ctx.enter_context(nc.Block())
        y_view = d["y_rows"][0:ROWS, :].rearrange("(t p k) n -> t p k n", p=P, k=TOP)

        @block.sync
        def _(sp):
            for t in range(TT):
                if t >= BUFS:
                    sp.wait_ge(s_acc, 3 * (t - BUFS) + 3)
                sp.dma_start(y_in[t % BUFS][:, :, :], y_view[t]).then_inc(s_in[t % BUFS], 16)

        @block.scalar
        def _(act):
            for t in range(TT):
                act.wait_ge(s_in[t % BUFS], 16 * (t // BUFS) + 16)
                if t >= 2:
                    act.wait_ge(s_gate, t - 1)
                nc.scalar.activation(acc[t % 2][:, :], y_in[t % BUFS][:, 0, :], ACT.Copy,
                                     scale=weights[:, 0, t:t + 1]).then_inc(s_w0, 1)
                if t:
                    act.wait_ge(s_res, t)
                    act.dma_start(d["out"][(t - 1) * P:t * P, :], res[(t - 1) % 2][:, :]).then_inc(s_out[(t - 1) % 2], 16)
            act.wait_ge(s_res, TT)
            act.dma_start(d["out"][(TT - 1) * P:TT * P, :], res[(TT - 1) % 2][:, :]).then_inc(s_out[(TT - 1) % 2], 16)
            for b in range(2):
                act.wait_ge(s_out[b], 16 * TT // 2)

        @block.vector
        def _(dve):
            def finish(t):
                dve.wait_ge(s_gate, t + 1)
                if t >= 2:
                    dve.wait_ge(s_out[t % 2], 16 * (t // 2))
                nc.vector.tensor_tensor(res[t % 2][:, :], acc[t % 2][:, :], x_all[:, t], ALU.add).then_inc(s_res, 1)

            for t in range(TT):
                dve.wait_ge(s_w0, t + 1)
                dve.wait_ge(s_in[t % BUFS], 16 * (t // BUFS) + 16)
                for k in range(1, TOP):
                    if k > 1:
                        dve.wait_ge(s_acc, 3 * t + k - 1)
                    nc.vector.scalar_tensor_tensor(acc[t % 2][:, :], y_in[t % BUFS][:, k], weights[:, k, t:t + 1],
                                                   acc[t % 2][:, :], ALU.mult, ALU.add).then_inc(s_acc, 1)
                if t:
                    finish(t - 1)
            finish(TT - 1)

        @block.gpsimd
        def _(pool):
            for t in range(TT):
                pool.wait_ge(s_acc, 3 * t + 3)
                nc.gpsimd.tensor_tensor(acc[t % 2][:, :], acc[t % 2][:, :], gate_row[:, 1], ALU.mult).then_inc(s_gate, 1)


def adaln_moe_kernel(nc, d):
    scratch = lambda name, shape, dt=F32: nc.dram_tensor(name, shape, dt, kind="Internal").ap()
    d = dict(d)
    d["qk_parts"] = scratch("qk_parts", (2, 2, D, T))
    d["slots"] = scratch("slots", (ALL_SLOTS, 1), I32)
    d["x_norm"] = scratch("x_norm", (T + P // 4, D))
    d["tiles"] = scratch("tiles", (LISTED, 2), I32)
    d["y_rows"] = scratch("y_rows", (ROWS + P, D))
    with ExitStack() as ctx:
        sb = lambda name, shape, dt=F32: ctx.enter_context(nc.sbuf_tensor(name, shape, dt))
        keep = {
            "ident": sb("ident", [P, P]),
            "mod_col": sb("mod_col", [P, 4, KT]),
            "gate_row": sb("gate_row", [P, 2, D]),
            "x_all": sb("x_all", [P, TT, D]),
            "weights": sb("weights", [P, TOP, TT]),
            "tile_list": sb("tile_list", [1, 2 * LISTED], I32),
            "n_pairs": sb("n_pairs", [P, 1], I32),
        }
        with nc.sbuf_tensor("v_all", [P, TT, H, DH + 1], F32) as v_all:
            keep["v_all"] = v_all
            modulation_and_projection(nc, d, keep)
            attention(nc, d, keep)
        route(nc, d, keep)
        experts(nc, d, keep)
        combine(nc, d, keep)


def rotary_tables():
    inv = (np.float32(1.0) / np.float32(10000.0) ** (np.arange(0, DH, 2, dtype=np.float32) / np.float32(DH)))
    angle = np.outer(np.arange(T, dtype=np.float32), inv.astype(np.float32)).astype(np.float32).T
    cos, sin = np.cos(angle).astype(np.float32), np.sin(angle).astype(np.float32)
    return np.concatenate([cos, cos]), np.concatenate([-sin, sin])


def kernel(**inputs):
    import concourse.bacc as bacc
    from concourse.bass_utils import run_bass_kernel_spmd

    a = {n: np.asarray(v) for n, v in inputs.items()}
    cos, sin = rotary_tables()
    bias = a["L0_attn_Wqkv_b"]
    gate_up = lambda g, u: [g[..., :P], u[..., :P]] + ([g[..., P:], u[..., P:]] if g.shape[-1] > P else [])
    arrays = {
        "x": a["L0_attn_x"].reshape(T, D),
        "w_t": a["L0_attn_Wqkv_w"].T,
        "b_qk": bias[:2 * D].reshape(8, P).T,
        "b_v": bias[2 * D:],
        "wmod": a["L0_wmod"],
        "c_col": a["L0_c"].reshape(KT, P).T,
        "cos": cos,
        "sin": sin,
        "gate_t": a["L0_ffn_gate_w"].T,
        "w_gu": np.concatenate(gate_up(a["L0_ffn_Wg"], a["L0_ffn_Wu"]), axis=-1),
        "w_d": a["L0_ffn_Wd"],
        "w_gu_s": np.concatenate(gate_up(a["L0_ffn_cWg"], a["L0_ffn_cWu"]), axis=-1),
        "w_d_s": a["L0_ffn_cWd"],
    }
    arrays = {n: np.ascontiguousarray(v) for n, v in arrays.items()}
    nc = bacc.Bacc("TRN2", target_bir_lowering=False, num_devices=1)
    d = {n: nc.dram_tensor(f"in_{n}", v.shape, mybir.dt.from_np(v.dtype), kind="ExternalInput").ap() for n, v in arrays.items()}
    d["out"] = nc.dram_tensor("out", (T, D), F32, kind="ExternalOutput").ap()
    adaln_moe_kernel(nc, d)
    r = run_bass_kernel_spmd(nc, [{f"in_{n}": v for n, v in arrays.items()}], core_ids=[0])
    return r.results[0]["out"].reshape(1, T, D)
```

```python
from contextlib import ExitStack

import numpy as np
import concourse.bass as bass
from concourse import mybir

F32 = mybir.dt.float32
F32R = mybir.dt.float32r
F16 = mybir.dt.float16
I32 = mybir.dt.int32
U32 = mybir.dt.uint32
ALU = mybir.AluOpType
ACT = mybir.ActivationFunctionType
AX = mybir.AxisListType

P = 128
T, D = 2048, 512
H, DH = 16, 32
KT = D // P
TT = T // P
CH = 512
NCH = T // CH
EPS = 1e-5
GROUPS_1, GROUPS_2 = (0, 1, 2), (3, 4, 5)
SWAP = [(i + DH // 2) % DH for i in range(DH)]


def wait_apart(eng, sem, value, passed):
    value = eng.to_reg(value)
    eng.wait_ge(passed, 1)
    eng.wait_ge(sem, value)


def mod_columns(nc, out, wmod, silu_c, ms=range(KT)):
    for m in ms:
        for k in range(KT):
            last = nc.tensor.matmul(out[:, m:m + 1], wmod[:, k, m * P:(m + 1) * P], silu_c[:, k:k + 1],
                                    start=(k == 0), stop=(k == KT - 1))
    return last


def mod_row(nc, out, wmod, silu_cb):
    for k in range(KT):
        last = nc.tensor.matmul(out[:, :], silu_cb[:, k], wmod[:, k], start=(k == 0), stop=(k == KT - 1))
    return last


def gate_floor(nc, dve, out, gate, scratch, step, before):
    n = [before]

    def link(ins):
        n[0] += 1
        ins.then_inc(step, 1)
        dve.wait_ge(step, n[0])

    link(nc.vector.tensor_scalar(scratch[:, 0], gate, -1.0, 0.25, ALU.mult, ALU.max))
    link(nc.vector.tensor_scalar(scratch[:, 1], gate, 0.25, None, ALU.max))
    link(nc.vector.tensor_tensor(scratch[:, 1], scratch[:, 1], scratch[:, 0], ALU.max))
    link(nc.vector.tensor_scalar(scratch[:, 0], gate, 0.0, 2.0, ALU.is_ge, ALU.mult))
    link(nc.vector.tensor_scalar(scratch[:, 0], scratch[:, 0], -1.0, None, ALU.add))
    link(nc.vector.tensor_tensor(out, scratch[:, 0], scratch[:, 1], ALU.mult))


def modulation_and_projection(nc, d, keep):
    with ExitStack() as ctx:
        sb = lambda name, shape, dt=F32: ctx.enter_context(nc.sbuf_tensor(name, shape, dt))
        sem = lambda name: ctx.enter_context(nc.semaphore(name))
        pb = lambda name: ctx.enter_context(nc.psum_tensor(name, [P, CH], F32))

        wmod = sb("wmod_sb", [P, 3, KT, D])
        c_col = sb("c_col", [P, KT])
        floor_t = sb("floor_t", [P, 2, D])
        w_qkv = sb("w_qkv", [P, KT, 3 * D])
        b_qk = sb("b_qk", [P, 8])
        b_v = sb("b_v", [P, D])
        cos_t = sb("cos_t", [P, T])
        sin_t = sb("sin_t", [P, T])
        x_n = sb("x_n", [P, 4, D])
        stats = sb("stats", [P, 4, 6])
        meanvar = sb("meanvar", [P, 4, 2])
        std = sb("std", [P, 4])
        rstd = sb("rstd", [P, 4])
        h_t = sb("h_t", [P, 2, KT, CH])
        biased = sb("biased", [P, 2, CH])
        swapped = sb("swapped", [P, 2, CH])
        by_cos = sb("by_cos", [P, 2, CH])
        rotated = sb("rotated", [P, 2, CH])
        part_hi = sb("part_hi", [P, 2, CH], F32R)
        part_lo = sb("part_lo", [P, 2, CH], F32R)
        eps_col = sb("eps_col", [P, 1])
        tp = [pb(f"tp{i}") for i in range(2)]
        pj = [pb(f"pj{i}") for i in range(4)]
        pm = [pb(f"pm{i}") for i in range(2)]
        ident, mod_col, gate_row, v_all, x_all, silu_c, silu_cb = (
            keep[n] for n in ("ident", "mod_col", "gate_row", "v_all", "x_all", "silu_c", "silu_cb"))

        s_small = sem("small_loaded")
        s_wmod = [sem(f"wmod{g}_loaded") for g in GROUPS_1]
        s_w = [sem(f"w_{n}_loaded") for n in ("q", "k", "v")]
        s_tab = sem("tables_loaded")
        s_x0 = sem("x_first_loaded")
        s_x = sem("x_rest_loaded")
        s_const = sem("constants_set")
        s_silu = sem("silu_done")
        s_sb = sem("silu_spread")
        s_mod = sem("mod_done")
        s_modc = sem("mod_copied")
        s_flo = sem("gate_floor")
        s_st = sem("stats_done")
        s_mv = sem("meanvar_done")
        s_std = sem("std_done")
        s_rs = sem("rstd_done")
        s_xn = sem("x_n_done")
        s_tp = sem("transposed")
        s_ht = sem("h_t_done")
        s_pj = sem("projected")
        s_bi = sem("biased_done")
        s_v = sem("v_done")
        s_sw = sem("swapped_done")
        s_sw2 = sem("sin_done")
        s_cos = sem("cos_done")
        s_rot = sem("rotated_done")
        s_hi = sem("hi_done")
        s_lo = sem("lo_done")
        s_store = [sem(f"parts{i}_stored") for i in range(2)]

        JOBS = 8

        block = ctx.enter_context(nc.Block())

        @block.sync
        def _(sp):
            sp.dma_start(c_col[:, :], d["c_col"]).then_inc(s_small, 16)
            sp.dma_start(b_qk[:, :], d["b_qk"]).then_inc(s_small, 16)
            sp.dma_start(b_v[:, :], d["b_v"].partition_broadcast(P)).then_inc(s_small, 16)
            wm = d["wmod"].rearrange("(k p) (g n) -> g p k n", p=P, n=D)
            xs = d["x"].rearrange("(c t p) n -> c p t n", p=P, t=4)
            sp.dma_start(x_all[:, 0:4], xs[0]).then_inc(s_x0, 16)
            for g in GROUPS_1[:2]:
                sp.dma_start(wmod[:, g], wm[g]).then_inc(s_wmod[g], 16)
            w_view = d["w_t"].rearrange("(k p) n -> p k n", p=P)
            for n in range(3):
                sp.dma_start(w_qkv[:, :, n * D:(n + 1) * D], w_view[:, :, n * D:(n + 1) * D]).then_inc(s_w[n], 16)
            for r in range(4):
                sp.dma_start(cos_t[DH * r:DH * r + DH, :], d["cos"]).then_inc(s_tab, 16)
                sp.dma_start(sin_t[DH * r:DH * r + DH, :], d["sin"]).then_inc(s_tab, 16)
            for c in range(1, NCH):
                sp.dma_start(x_all[:, 4 * c:4 * c + 4], xs[c]).then_inc(s_x, 16)
            sp.dma_start(wmod[:, 2], wm[2]).then_inc(s_wmod[2], 16)
            with sp.Fori(0, NCH) as c:
                for j in range(JOBS):
                    s, o = divmod(j, KT)
                    rows = slice(o * P, (o + 1) * P)
                    sp.wait_ge(s_hi, c * JOBS + j + 1)
                    sp.dma_start(d["qk_parts"][0, s, rows, bass.ds(c * CH, CH)], part_hi[:, j % 2].bitcast(F32)).then_inc(s_store[j % 2], 16)
                    sp.wait_ge(s_lo, c * JOBS + j + 1)
                    sp.dma_start(d["qk_parts"][1, s, rows, bass.ds(c * CH, CH)], part_lo[:, j % 2].bitcast(F32)).then_inc(s_store[j % 2], 16)
            for b in range(2):
                sp.wait_ge(s_store[b], NCH * JOBS * 16)

        @block.gpsimd
        def _(pool):
            nc.gpsimd.memset(ident[:, :], 0.0).then_inc(s_const, 1)
            pool.wait_ge(s_const, 1)
            nc.gpsimd.affine_select(out=ident[:, :], in_=ident[:, :], compare_op=ALU.not_equal, fill=1.0,
                                    base=0, pattern=[[-1, P]], channel_multiplier=1).then_inc(s_const, 1)
            nc.gpsimd.memset(v_all[:, :, :, DH:DH + 1], 1.0).then_inc(s_const, 1)
            nc.gpsimd.memset(eps_col[:, :], EPS).then_inc(s_const, 1)
            pool.wait_ge(s_silu, 1)
            nc.gpsimd.tensor_copy(silu_cb[:, :, :], silu_c[:, :].unsqueeze(2).to_broadcast([P, KT, P])).then_inc(s_sb, 1)
            pool.wait_ge(s_tab, 16 * 8)
            with pool.Fori(0, NCH) as c:
                for j in range(JOBS):
                    wait_apart(pool, s_bi, c * JOBS + j + 1, s_tab)
                    if j >= 2:
                        pool.wait_ge(s_rot, c * JOBS + j - 1)
                    nc.gpsimd.tensor_tensor(by_cos[:, j % 2], biased[:, j % 2], cos_t[:, bass.ds(c * CH, CH)],
                                            ALU.mult).then_inc(s_cos, 1)
                pool.wait_ge(s_rot, c * JOBS + JOBS)

        @block.scalar
        def _(act):
            act.wait_ge(s_small, 48)
            nc.scalar.activation(silu_c[:, :], c_col[:, :], ACT.Silu).then_inc(s_silu, 1)
            act.wait_ge(s_const, 4)

            def modulate(c, b):
                act.wait_ge(s_mv, c + 1)
                nc.scalar.activation(std[:, :], meanvar[:, :, 1], ACT.Sqrt, bias=eps_col[:, :]).then_inc(s_std, 1)
                for k in range(KT):
                    act.wait_ge(s_tp, c * KT + k + 1)
                    if k == 0:
                        act.wait_ge(s_modc, 2)
                    nc.scalar.activation(h_t[:, b, k], tp[k % 2][:, :], ACT.Identity, bias=mod_col[:, 0, k:k + 1],
                                         scale=mod_col[:, 1, k:k + 1]).then_inc(s_ht, 1)

            def chunk(c, b, last):
                for j in range(JOBS):
                    act.wait_ge(s_pj, c * 12 + j + 1)
                    if j >= 2:
                        act.wait_ge(s_cos, c * JOBS + j - 1)
                        act.wait_ge(s_sw, c * JOBS + j - 1)
                    nc.scalar.activation(biased[:, j % 2], pj[j % 4][:, :], ACT.Identity,
                                         bias=b_qk[:, j:j + 1]).then_inc(s_bi, 1)
                    act.wait_ge(s_rot, c * JOBS + j + 1)
                    if j >= 2:
                        act.wait_ge(s_store[j % 2], (c * (JOBS // 2) + j // 2) * 32)
                    nc.scalar.activation(part_hi[:, j % 2], rotated[:, j % 2], ACT.Copy).then_inc(s_hi, 1)
                if not last:
                    modulate(c + 1, 1 - b)
                for p in range(2):
                    act.wait_ge(s_store[p], (c + 1) * (JOBS * 16))

            modulate(0, 0)
            with act.Fori(0, NCH // 2 - 1) as pair:
                chunk(pair * 2, 0, False)
                chunk(pair * 2 + 1, 1, False)
            chunk(NCH - 2, 0, False)
            chunk(NCH - 1, 1, True)

        @block.vector
        def _(dve):
            def ln(c, first):
                if not first:
                    dve.wait_ge(s_x, (NCH - 1) * 16)
                for t in range(4):
                    nc.vector.bn_stats(stats[:, t], x_all[:, bass.ds(c * 4 + t, 1)].rearrange("p o n -> p (o n)")).then_inc(s_st, 1)
                wait_apart(dve, s_st, c * 4 + 4, s_x0)
                for t in range(4):
                    last = nc.vector.bn_aggr(meanvar[:, t], stats[:, t])
                last.then_inc(s_mv, 1)
                dve.wait_ge(s_std, c + 1)
                nc.vector.reciprocal(rstd[:, :], std[:, :]).then_inc(s_rs, 1)
                dve.wait_ge(s_rs, c + 1)
                for t in range(4):
                    last = nc.vector.tensor_scalar(x_n[:, t], x_all[:, bass.ds(c * 4 + t, 1)].rearrange("p o n -> p (o n)"), meanvar[:, t, 0:1], rstd[:, t:t + 1],
                                                   ALU.subtract, ALU.mult)
                    last.then_inc(s_xn, 1)

            def mod_part(i):
                dve.wait_ge(s_mod, i + 1)
                nc.vector.tensor_scalar(mod_col[:, i], pm[i][:, 0:KT], float(i), None,
                                        ALU.add).then_inc(s_modc, 1)

            def chunk(c, last):
                for j in range(JOBS):
                    n = c * JOBS + j
                    wait_apart(dve, s_bi, n + 1, s_x0)
                    if j >= 2:
                        dve.wait_ge(s_rot, n - 1)
                    nc.vector.stream_shuffle(swapped[:, j % 2], biased[:, j % 2], SWAP).then_inc(s_sw, 1)
                    dve.wait_ge(s_sw, n + 1)
                    nc.vector.tensor_tensor(swapped[:, j % 2], swapped[:, j % 2], sin_t[:, bass.ds(c * CH, CH)],
                                            ALU.mult).then_inc(s_sw2, 1)
                    dve.wait_ge(s_sw2, n + 1)
                    dve.wait_ge(s_cos, n + 1)
                    if j >= 2:
                        dve.wait_ge(s_lo, n - 1)
                        dve.wait_ge(s_hi, n - 1)
                    nc.vector.tensor_tensor(rotated[:, j % 2], by_cos[:, j % 2], swapped[:, j % 2],
                                            ALU.add).then_inc(s_rot, 1)
                    dve.wait_ge(s_hi, n + 1)
                    if j >= 2:
                        dve.wait_ge(s_store[j % 2], (c * (JOBS // 2) + j // 2) * 32)
                    nc.vector.tensor_tensor(part_lo[:, j % 2], rotated[:, j % 2], part_hi[:, j % 2],
                                            ALU.subtract).then_inc(s_lo, 1)
                if not last:
                    ln(c + 1, False)
                for t in range(4):
                    dve.wait_ge(s_pj, c * 12 + JOBS + t + 1)
                    nc.vector.tensor_tensor(v_all[:, bass.ds(c * 4 + t, 1), :, 0:DH].rearrange("p o h w -> p (o h) w"),
                                            pj[t % 4][:, :].rearrange("p (h w) -> p h w", w=DH),
                                            b_v[:, :].rearrange("p (h w) -> p h w", w=DH), ALU.add).then_inc(s_v, 1)

            dve.wait_ge(s_x0, 16)
            ln(0, True)
            mod_part(0)
            mod_part(1)
            dve.wait_ge(s_tab, 16 * 8)
            with dve.Fori(0, NCH // 2 - 1) as pair:
                chunk(pair * 2, False)
                chunk(pair * 2 + 1, False)
            chunk(NCH - 2, False)
            dve.wait_ge(s_mod, 3)
            gate_floor(nc, dve, gate_row[:, 0], pm[0][:, :], floor_t, s_flo, 0)
            chunk(NCH - 1, True)

        @block.tensor
        def _(pe):
            def transposes(c):
                pe.wait_ge(s_xn, c * 4 + 4)
                for k in range(KT):
                    if k >= 2:
                        pe.wait_ge(s_ht, c * KT + k - 1)
                    for t in range(4):
                        last = nc.tensor.transpose(tp[k % 2][:, t * P:(t + 1) * P], x_n[:, t, k * P:(k + 1) * P],
                                                   ident[:, :])
                    last.then_inc(s_tp, 1)

            def chunk(c, b, first, last):
                for j in range(JOBS + 4):
                    if j % 4 == 0:
                        pe.wait_ge(s_w[j // 4], 16)
                    if j >= 4:
                        pe.wait_ge(s_bi, c * JOBS + j - 3)
                    elif not first:
                        pe.wait_ge(s_v, c * 4 - 3 + j)
                    for k in range(KT):
                        if j == 0:
                            pe.wait_ge(s_ht, c * KT + k + 1)
                        if j < JOBS:
                            last_mm = nc.tensor.matmul(pj[j % 4][:, :], w_qkv[:, k, j * P:(j + 1) * P], h_t[:, b, k],
                                                       start=(k == 0), stop=(k == KT - 1))
                        else:
                            t = j - JOBS
                            last_mm = nc.tensor.matmul(pj[j % 4][:, :], h_t[:, b, k, t * P:(t + 1) * P],
                                                       w_qkv[:, k, 2 * D:3 * D], start=(k == 0), stop=(k == KT - 1))
                    last_mm.then_inc(s_pj, 1)
                if not last:
                    transposes(c + 1)

            pe.wait_ge(s_silu, 1)
            pe.wait_ge(s_const, 4)
            for g in GROUPS_1[:2]:
                pe.wait_ge(s_wmod[g], 16)
                mod_columns(nc, pm[g], wmod[:, g], silu_c).then_inc(s_mod, 1)
            transposes(0)
            chunk(0, 0, True, False)
            with pe.Fori(0, NCH // 2 - 1) as pair:
                chunk(pair * 2 + 1, 1, False, False)
                chunk(pair * 2 + 2, 0, False, False)
            pe.wait_ge(s_sb, 1)
            pe.wait_ge(s_wmod[2], 16)
            mod_row(nc, pm[0], wmod[:, 2], silu_cb).then_inc(s_mod, 1)
            chunk(NCH - 1, 1, False, True)


PAIRS = H // 2
BLK = 2 * NCH
QK_ROWS = 3 * DH
MASK = -56576.0


def block_pairs():
    return [(h, c, kt) for h in range(2) for c in range(NCH) for kt in range(0, 4 * c + 4, 2)]


def first_query(c, kt):
    return 0 if c == 0 and kt == 1 else max(0, (kt - 4 * c) * P)


def pv_until(k):
    return 40 * (k // NCH) + 2 * (k % NCH + 1) * (k % NCH + 2)


def max_units():
    return [(i, c, CH if c < i // 4 else (i % 4 + 1) * P) for i in range(TT) for c in range(i // 4 + 1)]


SLOTS = block_pairs()
UNITS = max_units()
LAST_OF_CHUNK = [n for n, (i, c, _) in enumerate(UNITS) if i % 4 == 3 and c == i // 4]
N_S = len(SLOTS)
N_BLK = 2 * N_S
KEEP_P = 8
PV_LAG = 2
FOLD_LAG = 4
UNIT_FROM, UNIT_TO = 5, N_S - 3


def max_items():
    out = []
    for n in range(len(UNITS)):
        out.append(("unit", n))
        out += [("rows", cq) for cq, last in enumerate(LAST_OF_CHUNK) if n == last + 3]
    return out + [("rows", NCH - 1)]


ITEMS = max_items()
N_I = len(ITEMS)
ROWS_ITEM = [ITEMS.index(("rows", cq)) for cq in range(NCH)]


def items_of(slot):
    last = [N_I - 1] if slot == N_S - 1 else []
    span = UNIT_TO - UNIT_FROM + 1
    return [y for y in range(N_I - 1) if UNIT_FROM + y * span // (N_I - 1) == slot] + last


def ended_chunk(slot):
    h, c, kt = SLOTS[slot]
    return NCH * h + c if kt == 4 * c + 2 else None


def attention(nc, d, keep):
    with ExitStack() as ctx:
        sb = lambda name, shape, dt=F32: ctx.enter_context(nc.sbuf_tensor(name, shape, dt))
        sem = lambda name: ctx.enter_context(nc.semaphore(name))
        pb = lambda name, shape: ctx.enter_context(nc.psum_tensor(name, shape, F32))
        ident, v_all, x_all, gate_row, mod_col, silu_c, silu_cb = (
            keep[n] for n in ("ident", "v_all", "x_all", "gate_row", "mod_col", "silu_c", "silu_cb"))

        rows = QK_ROWS + 2
        q_st = [[sb(f"q_st{b}{h}", [rows, T], F32R) for h in range(2)] for b in range(2)]
        k_st = [[sb(f"k_st{b}{h}", [rows, T], F32R) for h in range(2)] for b in range(2)]
        v_h = [sb(f"v_h{h}", [P, TT, DH + 1]) for h in range(2)]
        probs = sb("probs", [P, KEEP_P, CH])
        o_t = sb("o_t", [P, 2, CH])
        wmod = sb("wmod_late", [P, 3, KT, D])
        floor_t = sb("floor_t2", [P, 2, D])
        ident16 = sb("ident16", [P, P], F16)
        mask16 = sb("mask16", [P, P], F16)
        fold = sb("fold", [P, DH + 1])
        max_part = sb("max_part", [P, 2, TT, NCH])
        max_q = sb("max_q", [P, 2, 4])
        neg_hi = sb("neg_hi", [P, 2, 4], F32R)
        neg_cols = sb("neg_cols", [P, 2, 2, 4])
        neg_rows = sb("neg_rows", [16, 2, P], F32R)
        rden = sb("rden", [P, 4])
        out_h = sb("out_h", [P, 4, DH])
        s_bank = pb("s_bank", [P, 2, CH])
        m_bank = pb("m_bank", [P, 2, 2, CH])
        o_bank = pb("o_bank", [P, 2, CH])

        s_cst = sem("constants_set2")
        s_zero = sem("o_bank_zeroed")
        s_lead = [[sem(f"stack{b}{h}_leading_loaded") for h in range(2)] for b in range(2)]
        s_ones = sem("ones_of_k_set")
        s_ld = [[sem(f"stack{b}{h}_loaded") for h in range(2)] for b in range(2)]
        s_vh = sem("v_head_copied")
        s_max = sem("max_scores_done")
        s_red = sem("max_reduced")
        s_mq = sem("max_of_chunk_done")
        s_nh = sem("neg_hi_done")
        s_nc = sem("neg_cols_done")
        s_mrow = [sem(f"neg_rows{c}_placed") for c in range(NCH)]
        s_s = sem("scores_done")
        s_exp = sem("exp_done")
        s_mask = sem("probs_masked")
        s_pv = sem("pv_done")
        s_oe = sem("o_t_copied")
        s_comb = sem("o_folded")
        s_rd = sem("denominator_done")
        s_norm = sem("normalized")
        s_og = sem("output_gated")
        s_x2 = sem("x_added")
        s_wmod = sem("wmod_late_loaded")
        s_mod = sem("mod_done2")
        s_modc = sem("mod_copied2")
        s_flo = sem("gate_floor2")

        block = ctx.enter_context(nc.Block())
        MASKED = [n for n, (h, c, kt) in enumerate(SLOTS) if kt >= 4 * c]

        @block.sync
        def _(sp):
            parts = d["qk_parts"]

            def load(pair, b, h, leading=(True, False)):
                order = [(0, 0), (0, 1), (1, 0)] if h == 0 else [(0, 1), (0, 0), (1, 0)]
                src = bass.ds((pair * 2 + h) * DH, DH)
                for lead in leading:
                    for r, (qp, kp) in enumerate(order):
                        if ((qp, kp) == (0, 0)) == lead:
                            done = (s_lead if lead else s_ld)[b][h]
                            rows = slice(r * DH, (r + 1) * DH)
                            sp.dma_start(q_st[b][h][rows, :].bitcast(F32), parts[qp, 0, src, :]).then_inc(done, 16)
                            sp.dma_start(k_st[b][h][rows, :].bitcast(F32), parts[kp, 1, src, :]).then_inc(done, 16)

            def place_max(pair, b, cq):
                sp.wait_ge(s_red, pair * N_I + ROWS_ITEM[cq] + 1)
                for h in range(2):
                    for part in range(2):
                        r = h * 8 + part * 4
                        sp.dma_start(q_st[b][h][QK_ROWS + part:QK_ROWS + part + 1, cq * CH:(cq + 1) * CH].bitcast(F32),
                                     neg_rows[r:r + 4, cq % 2, :].bitcast(F32)).then_inc(s_mrow[cq], 16)

            def step(it, s, more):
                st = 2 * it + s
                place_max(st + 1, 1 - s, 0)
                place_max(st + 1, 1 - s, 1)
                if more:
                    sp.wait_ge(s_s, st * N_BLK + N_BLK // 2)
                    load(st + 2, s, 0)
                place_max(st + 1, 1 - s, 2)
                place_max(st + 1, 1 - s, 3)
                if more:
                    sp.wait_ge(s_s, st * N_BLK + N_BLK)
                    load(st + 2, s, 1)

            for leading in ((True,), (False,)):
                for h in range(2):
                    load(0, 0, h, leading)
            for h in range(2):
                load(1, 1, h)
            for i, g in enumerate(GROUPS_2):
                sp.dma_start(wmod[:, i], d["wmod"].rearrange("(k p) (g n) -> g p k n", p=P, n=D)[g]).then_inc(s_wmod, 16)
            for cq in range(NCH):
                place_max(0, 0, cq)
            with sp.Fori(0, PAIRS // 2 - 1) as it:
                for s in range(2):
                    step(it, s, True)
            step(PAIRS // 2 - 1, 0, False)
            for c in range(NCH):
                sp.wait_ge(s_mrow[c], PAIRS * 64)

        @block.gpsimd
        def _(pool):
            def copy_v(head, h):
                nc.gpsimd.tensor_copy(v_h[h][:, :, :], v_all[:, :, bass.ds(head, 1), :].rearrange("p t o w -> p t (o w)")
                                      ).then_inc(s_vh, 1)

            nc.gpsimd.memset(ident16[:, :], 0.0).then_inc(s_cst, 1)
            nc.gpsimd.memset(mask16[:, :], 0.0).then_inc(s_cst, 1)
            nc.gpsimd.memset(fold[:, :], 0.0).then_inc(s_cst, 1)
            pool.wait_ge(s_cst, 3)
            nc.gpsimd.affine_select(out=ident16[:, :], in_=ident16[:, :], compare_op=ALU.not_equal, fill=1.0,
                                    base=0, pattern=[[-1, P]], channel_multiplier=1).then_inc(s_cst, 1)
            nc.gpsimd.affine_select(out=mask16[:, :], in_=mask16[:, :], compare_op=ALU.is_ge, fill=MASK,
                                    base=0, pattern=[[-1, P]], channel_multiplier=1).then_inc(s_cst, 1)
            nc.gpsimd.affine_select(out=fold[:, :], in_=fold[:, :], compare_op=ALU.not_equal, fill=1.0,
                                    base=0, pattern=[[-1, DH + 1]], channel_multiplier=1).then_inc(s_cst, 1)
            pool.wait_ge(s_cst, 6)
            nc.gpsimd.affine_select(out=fold[:, :], in_=fold[:, :], compare_op=ALU.not_equal, fill=1.0,
                                    base=-P // 2, pattern=[[-1, DH + 1]], channel_multiplier=1).then_inc(s_cst, 1)
            pool.wait_ge(s_cst, 7)
            for b in range(2):
                for h in range(2):
                    nc.gpsimd.memset(k_st[b][h][QK_ROWS:QK_ROWS + 2, :].bitcast(F32), 1.0).then_inc(s_ones, 1)
            pool.wait_ge(s_ones, 4)
            for h in range(2):
                copy_v(h, h)

            def step(st, first, last):
                for n in MASKED:
                    h, c, kt = SLOTS[n]
                    for j in range(2):
                        blk = 2 * n + j
                        wait_apart(pool, s_exp, st * N_BLK + blk + 1, s_cst)
                        q0 = first_query(c, kt + j)
                        w = (kt + j - 4 * c) * P + P - q0
                        tile = probs[:, blk % KEEP_P, q0:q0 + w]
                        nc.gpsimd.affine_select(out=tile, in_=tile, compare_op=ALU.is_ge, fill=0.0,
                                                base=P - w, pattern=[[1, w]], channel_multiplier=-1).then_inc(s_mask, 1)
                    if c == 0 and kt == 2:
                        if h == 0 and not first:
                            wait_apart(pool, s_pv, st * N_BLK, s_cst)
                            copy_v(2 * st + 1, 1)
                        if h == 1 and not last:
                            wait_apart(pool, s_pv, st * N_BLK + N_BLK // 2, s_cst)
                            copy_v(2 * st + 2, 0)

            step(0, True, False)
            with pool.Fori(0, PAIRS // 2 - 1) as it:
                for s in range(2):
                    step(2 * it + 1 + s, False, False)
            step(PAIRS - 1, False, True)

        @block.scalar
        def _(act):
            def copy_o(st, k, first):
                act.wait_ge(s_pv, st * N_BLK + pv_until(k))
                if not (first and k < 2):
                    act.wait_ge(s_comb, 8 * st + k - 1)
                nc.scalar.activation(o_t[:, k % 2], o_bank[:, k % 2], ACT.Copy).then_inc(s_oe, 1)

            def step(st, first, last):
                for n in range(N_S):
                    h, c, kt = SLOTS[n]
                    for j in range(2):
                        blk = 2 * n + j
                        act.wait_ge(s_s, st * N_BLK + blk + 1)
                        if not (first and blk < KEEP_P):
                            act.wait_ge(s_pv, st * N_BLK + blk - KEEP_P + 1)
                        q0 = first_query(c, kt + j)
                        nc.scalar.activation(probs[:, blk % KEEP_P, q0:], s_bank[:, blk % 2, q0:], ACT.Exp,
                                             scale=DH ** -0.5).then_inc(s_exp, 1)
                    if n >= PV_LAG and ended_chunk(n - PV_LAG) is not None:
                        copy_o(st, ended_chunk(n - PV_LAG), first)
                    if n == PV_LAG - 1 and not first:
                        copy_o(st - 1, 2 * NCH - 1, False)
                if last:
                    copy_o(st, 2 * NCH - 1, first)

            act.wait_ge(s_zero, 1)
            step(0, True, False)
            with act.Fori(0, PAIRS // 2 - 1) as it:
                for s in range(2):
                    step(2 * it + 1 + s, False, False)
            step(PAIRS - 1, False, True)

        @block.vector
        def _(dve):
            def reduce_unit(pair, y, u):
                i, c, w = UNITS[u]
                dve.wait_ge(s_max, pair * N_I + y + 1)
                nc.vector.tensor_reduce(max_part[:, :, i, c], m_bank[:, y % 2, :, 0:w], AX.X, ALU.max).then_inc(s_red, 1)

            def max_of_chunk(pair, cq):
                m = pair * NCH + cq
                dve.wait_ge(s_red, pair * N_I + ITEMS.index(("unit", LAST_OF_CHUNK[cq])) + 1)
                nc.vector.tensor_reduce(max_q[:, :, :], max_part[:, :, 4 * cq:4 * cq + 4, 0:cq + 1], AX.X,
                                        ALU.max).then_inc(s_mq, 1)
                dve.wait_ge(s_mq, m + 1)
                nc.vector.tensor_scalar(neg_hi[:, :, :], max_q[:, :, :], -1.0, None, ALU.mult).then_inc(s_nh, 1)
                dve.wait_ge(s_nh, m + 1)
                nc.vector.tensor_copy(neg_cols[:, :, 0], neg_hi[:, :, :]).then_inc(s_nc, 1)
                nc.vector.scalar_tensor_tensor(neg_cols[:, :, 1], max_q[:, :, :], -1.0, neg_hi[:, :, :], ALU.mult,
                                               ALU.subtract).then_inc(s_nc, 1)

            def copy_rows(pair, y, cq, first):
                dve.wait_ge(s_max, pair * N_I + y + 1)
                if cq >= 2:
                    dve.wait_ge(s_mrow[cq - 2], (pair + 1) * 64)
                elif not first:
                    dve.wait_ge(s_mrow[cq + 2], pair * 64)
                nc.vector.tensor_copy(neg_rows[:, cq % 2], m_bank[0:16, y % 2, 0, 0:P]).then_inc(s_red, 1)

            def item(pair, y, first):
                what, arg = ITEMS[y]
                if what == "rows":
                    copy_rows(pair, y, arg, first)
                else:
                    reduce_unit(pair, y, arg)
                    if arg in LAST_OF_CHUNK:
                        max_of_chunk(pair, LAST_OF_CHUNK.index(arg))

            def normalize(st, k, head):
                h, c = divmod(k, 4)
                dve.wait_ge(s_comb, 8 * st + k + 1)
                o = o_bank[:, k % 2, 0:4 * (DH + 1)].rearrange("p (i w) -> p i w", i=4)
                nc.vector.reciprocal(rden[:, :], o[:, :, DH]).then_inc(s_rd, 1)
                dve.wait_ge(s_rd, 8 * st + k + 1)
                nc.vector.tensor_tensor(out_h[:, :, :], o[:, :, 0:DH], rden[:, :].unsqueeze(2).to_broadcast([P, 4, DH]),
                                        ALU.mult).then_inc(s_norm, 1)
                dve.wait_ge(s_norm, 8 * st + k + 1)
                cols = bass.ds(head * DH, DH)
                nc.vector.tensor_tensor(out_h[:, :, :], out_h[:, :, :], gate_row[:, 0:1, cols].to_broadcast([P, 4, DH]),
                                        ALU.mult).then_inc(s_og, 1)
                dve.wait_ge(s_og, 8 * st + k + 1)
                nc.vector.tensor_tensor(x_all[:, 4 * c:4 * c + 4, cols], x_all[:, 4 * c:4 * c + 4, cols], out_h[:, :, :],
                                        ALU.add).then_inc(s_x2, 1)
                dve.wait_ge(s_x2, 8 * st + k + 1)

            nc.vector.memset(o_bank[:, :, :], 0.0).then_inc(s_zero, 1)
            for y in range(N_I):
                item(0, y, True)
            for i in range(2):
                dve.wait_ge(s_mod, i + 1)
                nc.vector.tensor_scalar(mod_col[:, 2 + i], s_bank[:, i, 0:KT], float(i), None, ALU.add).then_inc(s_modc, 1)
            dve.wait_ge(s_mod, 3)
            gate_floor(nc, dve, gate_row[:, 1], o_bank[:, 1], floor_t, s_flo, 0)

            def step(st, first, last):
                for what, arg in timeline(first, last):
                    if what == "item":
                        item(st + 1, arg, False)
                    elif what == "fold":
                        normalize(st, arg, 2 * st + arg // NCH)
                    elif what == "fold before":
                        normalize(st - 1, arg, 2 * st - 2 + arg // NCH)

            step(0, True, False)
            with dve.Fori(0, PAIRS // 2 - 1) as it:
                for s in range(2):
                    step(2 * it + 1 + s, False, False)
            step(PAIRS - 1, False, True)

        @block.tensor
        def _(pe):
            def unit(pair, b, y, u):
                i, c, w = UNITS[u]
                last = None
                diagonal = c == i // 4
                for h in range(2):
                    r = slice(h * DH, (h + 1) * DH)
                    last = nc.tensor.matmul(m_bank[:, y % 2, h, 0:w], q_st[b][h][r, i * P:(i + 1) * P],
                                            k_st[b][h][r, c * CH:c * CH + w], start=True, stop=True)
                if diagonal:
                    for h in range(2):
                        last = nc.tensor.matmul(m_bank[:, y % 2, h, w - P:w], ident16[:, :], mask16[:, :],
                                                start=False, stop=True, skip_group_check=True)
                last.then_inc(s_max, 1)

            def item(pair, b, y, first):
                if not (first and y < 2):
                    pe.wait_ge(s_red, pair * N_I + y - 1)
                what, arg = ITEMS[y]
                if what == "unit":
                    unit(pair, b, y, arg)
                else:
                    pe.wait_ge(s_nc, 2 * (pair * NCH + arg) + 2)
                    nc.tensor.transpose(m_bank[0:16, y % 2, 0, 0:P], neg_cols[:, :, :, :].rearrange("p h s i -> p (h s i)"),
                                        ident[:, :]).then_inc(s_max, 1)

            def scores(st, s, n, first):
                h, c, kt = SLOTS[n]
                for j in range(2):
                    blk = 2 * n + j
                    if not (first and blk < 2):
                        pe.wait_ge(s_exp, st * N_BLK + blk - 1)
                    q0 = first_query(c, kt + j)
                    nc.tensor.matmul(s_bank[:, blk % 2, q0:], k_st[s][h][:, (kt + j) * P:(kt + j + 1) * P],
                                     q_st[s][h][:, c * CH + q0:(c + 1) * CH], start=True, stop=True).then_inc(s_s, 1)

            def pv(st, n, first):
                h, c, kt = SLOTS[n]
                k = NCH * h + c
                masked = len([m for m in MASKED if m <= n])
                if kt >= 4 * c:
                    pe.wait_ge(s_mask, st * 2 * len(MASKED) + 2 * masked)
                else:
                    pe.wait_ge(s_exp, st * N_BLK + 2 * n + 2)
                if kt == 0:
                    if c == 0:
                        pe.wait_ge(s_vh, 2 * st + h + 1)
                    if not (first and k < 2):
                        pe.wait_ge(s_norm, 8 * st + k - 1)
                    elif k == 1:
                        pe.wait_ge(s_flo, 6)
                for j in range(2):
                    q0 = first_query(c, kt + j)
                    last = nc.tensor.matmul(o_bank[64 * j:64 * j + DH + 1, k % 2, q0:], v_h[h][:, kt + j, :],
                                            probs[:, (2 * n + j) % KEEP_P, q0:], start=(kt == 0), stop=(kt == 4 * c + 2))
                    last.then_inc(s_pv, 1)

            def fold_o(st, k):
                pe.wait_ge(s_oe, 8 * st + k + 1)
                for i in range(4):
                    last = nc.tensor.matmul(o_bank[:, k % 2, i * (DH + 1):(i + 1) * (DH + 1)], o_t[:, k % 2, i * P:(i + 1) * P],
                                            fold[:, :], start=True, stop=True)
                last.then_inc(s_comb, 1)

            pe.wait_ge(s_cst, 7)
            for h in range(2):
                pe.wait_ge(s_lead[0][h], 32)
            late = [(i, m) for i in range(2) for m in range(KT)]
            for y in range(N_I):
                if y == N_I - 1:
                    pe.wait_ge(s_zero, 1)
                    mod_row(nc, o_bank[:, 1], wmod[:, 2], silu_cb).then_inc(s_mod, 1)
                item(0, 0, y, True)
                if y >= N_I // 2 and y % 2 == 0 and late:
                    i, m = late.pop(0)
                    pe.wait_ge(s_wmod, 48)
                    last = mod_columns(nc, s_bank[:, i], wmod[:, i], silu_c, [m])
                    if m == KT - 1:
                        last.then_inc(s_mod, 1)
            pe.wait_ge(s_modc, 2)
            pe.wait_ge(s_ones, 4)

            def step(st, s, first, last, loaded, loaded_next):
                for what, arg in timeline(first, last):
                    if what == "scores":
                        h, c, kt = SLOTS[arg]
                        if h == 0 and kt == 0:
                            pe.wait_ge(s_mrow[c], (st + 1) * 64)
                        if c == 0 and kt == 0:
                            pe.wait_ge(s_ld[s][h], loaded * 64)
                        scores(st, s, arg, first)
                    elif what == "pv":
                        pv(st, arg, first)
                    elif what == "pv before":
                        pv(st - 1, arg, False)
                    elif what == "item":
                        if arg == 0:
                            for h in range(2):
                                pe.wait_ge(s_lead[1 - s][h], loaded_next * 32)
                        item(st + 1, 1 - s, arg, False)
                    elif what == "fold":
                        fold_o(st, arg)
                    elif what == "fold before":
                        fold_o(st - 1, arg)

            step(0, 0, True, False, 1, 1)
            with pe.Fori(0, PAIRS // 2 - 1) as it:
                step(2 * it + 1, 1, False, False, it + 1, it + 2)
                step(2 * it + 2, 0, False, False, it + 2, it + 2)
            step(PAIRS - 1, 1, False, True, PAIRS // 2, None)


def timeline(first, last):
    out = []
    for n in range(N_S + FOLD_LAG if last else N_S):
        if n < N_S:
            out.append(("scores", n))
        if not last:
            out += [("item", y) for y in items_of(n)]
        if n < FOLD_LAG:
            k = ended_chunk(n - FOLD_LAG)
            if not first and k is not None:
                out.append(("fold before", k))
        elif ended_chunk(n - FOLD_LAG) is not None:
            out.append(("fold", ended_chunk(n - FOLD_LAG)))
        if n < PV_LAG:
            if not first:
                out.append(("pv before", N_S + n - PV_LAG))
        elif n - PV_LAG < N_S:
            out.append(("pv", n - PV_LAG))
    return out


E_N, TOP = 32, 4
SLOT_TILE = 320
SUBS = [(0, P), (P, P), (2 * P, SLOT_TILE - 2 * P)]
REGION = -(-T // SLOT_TILE) * SLOT_TILE
N_MORE = REGION // SLOT_TILE - 1
CHUNKS = E_N // 2
ALL_SLOTS = E_N * REGION
PAIRS_MAX = CHUNKS + T * TOP // SLOT_TILE
LISTED = CHUNKS + E_N
ROWS = T * TOP
I_BIG, I_SMALL = 192, 128
I_REST = I_BIG - P
GU_COLS = 2 * I_BIG
SATURATED = 16.6355


def weight_buffers(nc, ctx):
    sb = lambda name, shape: ctx.enter_context(nc.sbuf_tensor(name, shape, F32))
    sem = lambda name: ctx.enter_context(nc.semaphore(name))
    return {
        "w_gu": [sb(f"w_gu{b}", [P, KT, GU_COLS]) for b in range(2)],
        "w_d": [sb(f"w_d{b}", [P, 2, D]) for b in range(2)],
        "c_gu": sb("c_gu", [P, KT, 2 * I_SMALL]),
        "c_d": sb("c_d", [P, D]),
        "w_gu_loaded": [sem(f"w_gu{b}_loaded") for b in range(2)],
        "w_d_loaded": [sem(f"w_d{b}_loaded") for b in range(2)],
        "chunk_loaded": sem("chunk_loaded"),
    }


def load_expert(eng, d, keep, e, b):
    eng.dma_start(keep["w_gu"][b][:, :, :], d["w_gu"][bass.ds(e, 1)].rearrange("o (k p) n -> p (o k) n", p=P)
                  ).then_inc(keep["w_gu_loaded"][b], 16)
    w_d, loaded = keep["w_d"][b], keep["w_d_loaded"][b]
    eng.dma_start(w_d[:, 0, :], d["w_d"][bass.ds(e, 1), 0:P].rearrange("o p n -> p (o n)")).then_inc(loaded, 16)
    for rows in (slice(0, I_REST), slice(I_REST, 2 * I_REST)):
        eng.dma_start(w_d[rows, 1, :], d["w_d"][bass.ds(e, 1), P:I_BIG].rearrange("o p n -> p (o n)")).then_inc(loaded, 16)


def load_chunk(eng, d, keep, c):
    eng.dma_start(keep["c_gu"][:, :, :], d["w_gu_s"][bass.ds(c, 1)].rearrange("o (k p) n -> p (o k) n", p=P)
                  ).then_inc(keep["chunk_loaded"], 16)
    eng.dma_start(keep["c_d"][:, :], d["w_d_s"][bass.ds(c, 1)].rearrange("o p n -> p (o n)")
                  ).then_inc(keep["chunk_loaded"], 16)


def route(nc, d, keep):
    with ExitStack() as ctx:
        sb = lambda name, shape, dt=F32: ctx.enter_context(nc.sbuf_tensor(name, shape, dt))
        sem = lambda name: ctx.enter_context(nc.semaphore(name))
        pb = lambda name, shape: ctx.enter_context(nc.psum_tensor(name, shape, F32))
        ident, mod_col, x_all, weights, tile_list, n_pairs = (
            keep[n] for n in ("ident", "mod_col", "x_all", "weights", "tile_list", "n_pairs"))

        gate_w = sb("gate_w", [P, KT, E_N])
        stats = sb("stats2", [P, 4, 6])
        meanvar = sb("meanvar2", [P, 4, 2])
        std = sb("std2", [P, 4])
        rstd = sb("rstd2", [P, 4])
        eps_col = sb("eps_col2", [P, 1])
        x_n = sb("x_n2", [P, 2, 4, D])
        h_t = sb("h_t2", [P, 2, KT, CH])
        logits = sb("logits", [P, 4, E_N])
        capped = sb("capped", [P, 4, E_N])
        top_v = sb("top_v", [P, 4, 8])
        top_i = sb("top_i", [P, 4, 8], U32)
        top_f = sb("top_f", [P, 4, 8])
        expert_no = sb("expert_no", [P, E_N])
        region_of = sb("region_of", [P, E_N])
        onehot = sb("onehot", [P, TOP, 4, E_N])
        picked = sb("picked", [P, TOP, 4, E_N])
        row_max = sb("row_max", [P, 4])
        top_logit = sb("top_logit", [P, TOP, 4])
        top_exp = sb("top_exp", [P, TOP, 4])
        top_sum = sb("top_sum", [P, 4])
        top_rec = sb("top_rec", [P, 4])
        mask_h = sb("mask_h", [P, 4, E_N], F16)
        count_h = sb("count_h", [P, E_N], F16)
        count_c = sb("count_c", [P, E_N], F16)
        before = sb("before", [P, P], F16)
        ones_h = sb("ones_h", [P, P], F16)
        slot_f = sb("slot_f", [P, 4, E_N])
        slot_k = sb("slot_k", [P, TOP, 4])
        slot_i = sb("slot_i", [P, NCH, TOP, 4], I32)
        row_no = sb("row_no", [P, TOP, TT], I32)
        blank = sb("blank", [P, 5 * P], I32)
        zero_rows = sb("zero_rows", [P // 4, D])
        chunk_max = sb("chunk_max", [P, CHUNKS])
        flags = sb("flags", [P, N_MORE, CHUNKS])
        flag_sum = sb("flag_sum", [P, N_MORE * CHUNKS])
        ones_f = sb("ones_f", [P, N_MORE * CHUNKS])
        start_v = sb("start_v", [P, N_MORE, CHUNKS])
        chosen = sb("chosen", [P, N_MORE * CHUNKS])
        prod = sb("prod", [P, N_MORE * CHUNKS])
        number_1 = sb("number_1", [P, 1])
        more_f = sb("more_f", [P, 2])
        more_i = sb("more_i", [P, 2], I32)
        first_i = sb("first_i", [P, 2], I32)
        tp = [pb(f"tp2_{i}", [P, CH]) for i in range(2)]
        lg = [pb(f"lg{i}", [P, 4, E_N]) for i in range(2)]
        pos = pb("pos", [P, 2, 4, E_N])
        tot = lg[0][:, 0]

        s_gw = sem("gate_w_loaded")
        s_cst = sem("constants_set3")
        s_cst2 = sem("constants_set4")
        s_blank = sem("slot_list_blank")
        s_blankz = sem("zero_rows_stored")
        s_st = sem("stats_done2")
        s_mv = sem("meanvar_done2")
        s_std = sem("std_done2")
        s_rs = sem("rstd_done2")
        s_xn = sem("x_n_done2")
        s_xns = [sem(f"x_n_stored{i}") for i in range(2)]
        s_tp = sem("transposed2")
        s_ht = sem("h_t_done2")
        s_lg = sem("logits_done")
        s_d = sem("routing_step")
        s_e = sem("top_exp_done")
        s_mask = sem("mask_done")
        s_pos = sem("ranks_done")
        s_slot = sem("slots_done")
        s_scat = sem("slots_placed")
        chain = sem("vector_chain")
        s_zc = sem("count_zeroed")
        s_tot = sem("counts_done")
        s_list = sem("tile_list_done")
        s_lstore = sem("tile_list_stored")
        s_lload = sem("tile_list_loaded")

        block = ctx.enter_context(nc.Block())

        @block.sync
        def _(sp):
            sp.dma_start(gate_w[:, :, :], d["gate_t"].rearrange("(k p) e -> p k e", p=P)).then_inc(s_gw, 16)
            for b in range(2):
                load_expert(sp, d, keep, b, b)
                if b == 0:
                    load_chunk(sp, d, keep, 0)
            sp.wait_ge(s_cst, 5)
            n = P * 5
            full = ALL_SLOTS // n
            assert full * n == ALL_SLOTS
            sp.dma_start(d["slots"][0:full * n, :].rearrange("(p f) o -> p (f o)", f=n), blank[0:full, :]).then_inc(s_blank, 16)
            sp.dma_start(d["x_norm"][T:T + P // 4, :], zero_rows[:, :]).then_inc(s_blankz, 16)
            for c in range(NCH):
                b = c % 2
                sp.wait_ge(s_xn, c * 4 + 4)
                sp.dma_start(d["x_norm"][c * CH:(c + 1) * CH, :].rearrange("(t p) n -> p t n", p=P),
                             x_n[:, b]).then_inc(s_xns[b], 16)
            sp.wait_ge(s_list, 2)
            sp.dma_start(d["tiles"][0:CHUNKS, :], first_i[0:CHUNKS, :]).then_inc(s_lstore, 16)
            sp.dma_start(d["tiles"][CHUNKS:LISTED, :], more_i[0:LISTED - CHUNKS, :]).then_inc(s_lstore, 16)
            sp.wait_ge(s_lstore, 32)
            sp.dma_start(tile_list[0:1, :], d["tiles"].rearrange("(o a) b -> o (a b)", o=1)).then_inc(s_lload, 16)
            sp.wait_ge(s_lload, 16)
            sp.wait_ge(s_blankz, 16)
            for b in range(2):
                sp.wait_ge(s_xns[b], 16 * NCH // 2)

        @block.gpsimd
        def _(pool):
            nc.gpsimd.iota(blank[:, :], [[0, 5], [1, P]], base=ROWS, channel_multiplier=0).then_inc(s_cst, 1)
            nc.gpsimd.memset(zero_rows[:, :], 0.0).then_inc(s_cst, 1)
            nc.gpsimd.memset(ones_h[:, :], 1.0).then_inc(s_cst, 1)
            nc.gpsimd.memset(eps_col[:, :], EPS).then_inc(s_cst, 1)
            nc.gpsimd.memset(ones_f[:, :], 1.0).then_inc(s_cst, 1)
            pool.wait_ge(s_cst, 5)
            nc.gpsimd.affine_select(out=before[:, :], in_=ones_h[:, :], compare_op=ALU.is_gt, fill=0.0,
                                    base=0, pattern=[[1, P]], channel_multiplier=-1).then_inc(s_cst2, 1)
            nc.gpsimd.iota(expert_no[:, :], [[1, E_N]], base=0, channel_multiplier=0,
                           allow_small_or_imprecise_dtypes=True).then_inc(s_cst2, 1)
            nc.gpsimd.iota(region_of[:, :], [[REGION, E_N]], base=0, channel_multiplier=0,
                           allow_small_or_imprecise_dtypes=True).then_inc(s_cst2, 1)
            nc.gpsimd.iota(row_no[:, :, :], [[1, TOP], [TOP * P, TT]], base=0, channel_multiplier=TOP).then_inc(s_cst2, 1)
            nc.gpsimd.iota(start_v[:, :, :], [[SLOT_TILE, N_MORE], [2 * REGION, CHUNKS]], base=SLOT_TILE,
                           channel_multiplier=0, allow_small_or_imprecise_dtypes=True).then_inc(s_cst2, 1)
            nc.gpsimd.iota(number_1[:, :], [[0, 1]], base=1, channel_multiplier=1,
                           allow_small_or_imprecise_dtypes=True).then_inc(s_cst2, 1)
            nc.gpsimd.iota(first_i[:, 0:1], [[0, 1]], base=0, channel_multiplier=1).then_inc(s_cst2, 1)
            nc.gpsimd.iota(first_i[:, 1:2], [[0, 1]], base=0, channel_multiplier=2 * REGION).then_inc(s_cst2, 1)
            pool.wait_ge(s_blank, 16)
            for c in range(NCH):
                b = c % 2
                pool.wait_ge(s_slot, c + 1)
                for t in range(4):
                    for k in range(TOP):
                        nc.gpsimd.indirect_dma_start(
                            out=d["slots"], out_offset=bass.IndirectOffsetOnAxis(ap=slot_i[:, c, k, t:t + 1], axis=0),
                            in_=row_no[:, k, 4 * c + t:4 * c + t + 1], in_offset=None).then_inc(s_scat, 16)
            pool.wait_ge(s_scat, 16 * TOP * TT)

        @block.scalar
        def _(act):
            def modulate(c, b):
                act.wait_ge(s_mv, c + 1)
                nc.scalar.activation(std[:, :], meanvar[:, :, 1], ACT.Sqrt, bias=eps_col[:, :]).then_inc(s_std, 1)
                for k in range(KT):
                    act.wait_ge(s_tp, c * KT + k + 1)
                    nc.scalar.activation(h_t[:, b, k], tp[k % 2][:, :], ACT.Identity, bias=mod_col[:, 2, k:k + 1],
                                         scale=mod_col[:, 3, k:k + 1]).then_inc(s_ht, 1)

            act.wait_ge(s_cst, 5)
            modulate(0, 0)
            for c in range(NCH):
                if c + 1 < NCH:
                    modulate(c + 1, (c + 1) % 2)
                act.wait_ge(s_d, c * 2 + 1)
                nc.scalar.activation(top_exp[:, :, :], top_logit[:, :, :], ACT.Exp).then_inc(s_e, 1)

        @block.vector
        def _(dve):
            spread_e = lambda ap: ap.unsqueeze(1).to_broadcast([P, 4, E_N])

            def normalize(c, b):
                for t in range(4):
                    nc.vector.bn_stats(stats[:, t], x_all[:, c * 4 + t]
                                       ).then_inc(s_st, 1)
                dve.wait_ge(s_st, c * 4 + 4)
                for t in range(4):
                    last = nc.vector.bn_aggr(meanvar[:, t], stats[:, t])
                last.then_inc(s_mv, 1)
                dve.wait_ge(s_std, c + 1)
                nc.vector.reciprocal(rstd[:, :], std[:, :]).then_inc(s_rs, 1)
                dve.wait_ge(s_rs, c + 1)
                for t in range(4):
                    nc.vector.tensor_scalar(x_n[:, b, t], x_all[:, c * 4 + t],
                                            meanvar[:, t, 0:1], rstd[:, t:t + 1],
                                            ALU.subtract, ALU.mult).then_inc(s_xn, 1)

            def choose(c, b):
                steps = [0]

                def link(ins, wait=True):
                    steps[0] += 1
                    ins.then_inc(chain, 1)
                    if wait:
                        dve.wait_ge(chain, c * LINKS + steps[0])

                spread_k = lambda ap: ap.unsqueeze(1).to_broadcast([P, TOP, 4, E_N])
                dve.wait_ge(s_lg, c + 1)
                if c == 0:
                    dve.wait_ge(s_cst2, 8)
                link(nc.vector.tensor_copy(logits[:, :, :], lg[b][:, :, :]), False)
                link(nc.vector.tensor_scalar(capped[:, :, :], lg[b][:, :, :], SATURATED, None, ALU.min))
                for t in range(4):
                    link(nc.vector.max(top_v[:, t], capped[:, t]), t == 3)
                for t in range(4):
                    link(nc.vector.max_index(top_i[:, t], top_v[:, t], capped[:, t]), t == 3)
                link(nc.vector.tensor_copy(top_f[:, :, :], top_i[:, :, :]))
                link(nc.vector.tensor_tensor(onehot[:, :, :, :],
                                             top_f[:, :, 0:TOP].rearrange("p t k -> p k t").unsqueeze(3).to_broadcast([P, TOP, 4, E_N]),
                                             expert_no[:, :].unsqueeze(1).unsqueeze(1).to_broadcast([P, TOP, 4, E_N]),
                                             ALU.is_equal))
                with nc.allow_low_precision("ones and zeros"):
                    nc.vector.tensor_reduce(mask_h[:, :, :], onehot[:, :, :, :].rearrange("p k t e -> p t e k"),
                                            AX.X, ALU.add).then_inc(s_mask, 1)
                link(nc.vector.tensor_reduce(row_max[:, :], logits[:, :, :], AX.X, ALU.max), False)
                link(nc.vector.tensor_tensor(picked[:, :, :, :], onehot[:, :, :, :], spread_k(logits[:, :, :]), ALU.mult))
                link(nc.vector.tensor_reduce(top_logit[:, :, :], picked[:, :, :, :], AX.X, ALU.add))
                nc.vector.tensor_tensor(top_logit[:, :, :], top_logit[:, :, :],
                                        row_max[:, :].unsqueeze(1).to_broadcast([P, TOP, 4]), ALU.subtract
                                        ).then_inc(s_d, 1)
                dve.wait_ge(s_d, 2 * c + 1)
                dve.wait_ge(s_pos, c + 1)
                link(nc.vector.tensor_tensor(slot_f[:, :, :], pos[:, b], spread_e(region_of[:, :]), ALU.add))
                link(nc.vector.tensor_tensor(picked[:, :, :, :], onehot[:, :, :, :], spread_k(slot_f[:, :, :]), ALU.mult))
                link(nc.vector.tensor_reduce(slot_k[:, :, :], picked[:, :, :, :], AX.X, ALU.add))
                nc.vector.tensor_copy(slot_i[:, c], slot_k[:, :, :]).then_inc(s_slot, 1)
                with nc.allow_low_precision("whole numbers up to the number of tiles"):
                    link(nc.vector.tensor_reduce(count_c[:, :], mask_h[:, :, :].rearrange("p t e -> p e t"), AX.X, ALU.add))
                nc.vector.tensor_tensor(count_h[:, :], count_h[:, :], count_c[:, :], ALU.add).then_inc(s_d, 1)
                dve.wait_ge(s_d, 2 * c + 2)
                dve.wait_ge(s_e, c + 1)
                link(nc.vector.tensor_reduce(top_sum[:, :], top_exp[:, :, :].rearrange("p k t -> p t k"), AX.X, ALU.add))
                link(nc.vector.reciprocal(top_rec[:, :], top_sum[:, :]))
                link(nc.vector.tensor_tensor(weights[:, :, 4 * c:4 * c + 4], top_exp[:, :, :],
                                             top_rec[:, :].unsqueeze(1).to_broadcast([P, TOP, 4]), ALU.mult))
                assert steps[0] == LINKS

            LINKS = 22
            with nc.allow_low_precision("a count of zero"):
                nc.vector.memset(count_h[:, :], 0.0).then_inc(s_zc, 1)
            dve.wait_ge(s_zc, 1)
            normalize(0, 0)
            for c in range(NCH):
                if c + 1 < NCH:
                    if c >= 1:
                        dve.wait_ge(s_xns[(c + 1) % 2], 16 * ((c + 1) // 2))
                    normalize(c + 1, (c + 1) % 2)
                choose(c, c % 2)

            last = [NCH * LINKS]

            def link(ins):
                last[0] += 1
                ins.then_inc(chain, 1)
                dve.wait_ge(chain, last[0])

            dve.wait_ge(s_tot, 1)
            link(nc.vector.tensor_reduce(chunk_max[:, :], tot.rearrange("p (c two) -> p c two", two=2), AX.X, ALU.max))
            for r in range(N_MORE):
                link(nc.vector.tensor_scalar(flags[:, r], chunk_max[:, :], float((r + 1) * SLOT_TILE), None, ALU.is_gt))
            flat = flags[:, :, :].rearrange("p r c -> p (r c)")
            link(nc.vector.tensor_tensor_scan(flag_sum[:, :], ones_f[:, :], flat, 0.0, ALU.mult, ALU.add))
            link(nc.vector.tensor_scalar(chosen[:, :], flag_sum[:, :], number_1[:, 0:1], None, ALU.is_equal))
            link(nc.vector.tensor_tensor(chosen[:, :], chosen[:, :], flat, ALU.mult))
            link(nc.vector.tensor_tensor(prod[:, :], chosen[:, :], start_v[:, :, :].rearrange("p r c -> p (r c)"), ALU.mult))
            link(nc.vector.tensor_reduce(more_f[:, 1:2], prod[:, :], AX.X, ALU.add))
            link(nc.vector.tensor_tensor(flags[:, :, :], chosen[:, :].rearrange("p (r c) -> p r c", c=CHUNKS),
                                         expert_no[:, 0:CHUNKS].unsqueeze(1).to_broadcast([P, N_MORE, CHUNKS]), ALU.mult))
            link(nc.vector.tensor_reduce(more_f[:, 0:1], flags[:, :, :], AX.XY, ALU.add))
            nc.vector.tensor_copy(more_i[:, :], more_f[:, :]).then_inc(s_list, 1)
            nc.vector.tensor_scalar(n_pairs[:, 0:1], flag_sum[:, N_MORE * CHUNKS - 1:], float(CHUNKS), None,
                                    ALU.add).then_inc(s_list, 1)
            dve.wait_ge(s_list, 2)

        @block.tensor
        def _(pe):
            pe.wait_ge(s_gw, 16)
            pe.wait_ge(s_cst2, 8)
            def route_logits(c, b):
                pe.wait_ge(s_xn, c * 4 + 4)
                for k in range(KT):
                    if k >= 2:
                        pe.wait_ge(s_ht, c * KT + k - 1)
                    for t in range(4):
                        last = nc.tensor.transpose(tp[k % 2][:, t * P:(t + 1) * P], x_n[:, b, t, k * P:(k + 1) * P],
                                                   ident[:, :])
                    last.then_inc(s_tp, 1)
                pe.wait_ge(s_ht, (c + 1) * KT)
                for t in range(4):
                    for k in range(KT):
                        last = nc.tensor.matmul(lg[b][:, t], h_t[:, b, k, t * P:(t + 1) * P], gate_w[:, k],
                                                start=(k == 0), stop=(k == KT - 1))
                last.then_inc(s_lg, 1)

            route_logits(0, 0)
            for c in range(NCH):
                b = c % 2
                pe.wait_ge(s_mask, c + 1)
                nc.tensor.matmul(pos[:, b], before[:, :], mask_h[:, :, :], start=True, stop=False)
                for t in range(3):
                    nc.tensor.matmul(pos[:, b, t + 1:4], ones_h[:, :], mask_h[:, t:t + 1].to_broadcast([P, 3 - t, E_N]),
                                     start=False, stop=False)
                if c:
                    pe.wait_ge(s_d, 2 * c)
                nc.tensor.matmul(pos[:, b], ones_h[:, :], count_h[:, :].unsqueeze(1).to_broadcast([P, 4, E_N]),
                                 start=False, stop=True).then_inc(s_pos, 1)
                if c + 1 < NCH:
                    route_logits(c + 1, 1 - b)
            pe.wait_ge(s_d, 2 * NCH)
            nc.tensor.matmul(tot, ones_h[:, :], count_h[:, :], start=True, stop=True).then_inc(s_tot, 1)


SMALL_SCALE = 0.05
JOBS_GU = [("big", 0, P), ("big", P, P), ("big", 2 * P, P), ("small", 0, P), ("small", P, P)]


def experts(nc, d, keep):
    with ExitStack() as ctx:
        sb = lambda name, shape, dt=F32: ctx.enter_context(nc.sbuf_tensor(name, shape, dt))
        sem = lambda name: ctx.enter_context(nc.semaphore(name))
        pb = lambda name, shape: ctx.enter_context(nc.psum_tensor(name, shape, F32))
        ident, mod_col, tile_list, n_pairs = (keep[n] for n in ("ident", "mod_col", "tile_list", "n_pairs"))
        w_gu, w_d, c_gu, c_d, s_wgu, s_wd, s_c = (
            keep[n] for n in ("w_gu", "w_d", "c_gu", "c_d", "w_gu_loaded", "w_d_loaded", "chunk_loaded"))

        w_gu_p = [sb(f"w_gu_p{b}", [P, 2, KT, GU_COLS], F32R) for b in range(2)]
        w_d_p = [sb(f"w_d_p{b}", [P, 2, 2, D], F32R) for b in range(2)]
        c_gu_p = sb("c_gu_p", [P, 2, KT, 2 * I_SMALL], F32R)
        c_d_p = sb("c_d_p", [P, 2, D], F32R)
        rows_g = [sb(f"rows_g{b}", [P, 3], I32) for b in range(2)]
        rows_i = [sb(f"rows_i{b}", [P, 3], I32) for b in range(2)]
        toks_i = [sb(f"toks_i{b}", [P, 3], I32) for b in range(2)]
        x_g = [sb(f"x_g{b}", [P, 3, D]) for b in range(2)]
        x_t = sb("x_t", [P, KT, SLOT_TILE])
        x_p = sb("x_p", [P, 2, KT, SLOT_TILE], F32R)
        gated = sb("gated", [P, 3, SLOT_TILE])
        act_t = sb("act_t", [P, 3, SLOT_TILE])
        a_p = sb("a_p", [P, 3, 2, SLOT_TILE], F32R)
        y_sb = [sb(f"y_sb{b}", [P, 3, D]) for b in range(2)]
        gu = [pb(f"gu{j}", [P, CH]) for j in range(5)]
        tp = [pb("tp3", [P, CH]), gu[0]]
        yb = [gu[1]] + [pb(f"y{j}", [P, D]) for j in range(2)]

        s_rg = [sem(f"gather_rows{b}_loaded") for b in range(2)]
        s_ri = [sem(f"scatter_rows{b}_loaded") for b in range(2)]
        s_wgh, s_wgl = sem("w_gu_high"), sem("w_gu_low")
        s_wdh, s_wdl = sem("w_d_high"), sem("w_d_low")
        s_cgh, s_cgl = sem("chunk_gu_high"), sem("chunk_gu_low")
        s_cdh, s_cdl = sem("chunk_d_high"), sem("chunk_d_low")
        s_tok = sem("tokens_done")
        s_xg = [sem(f"x_gathered{b}") for b in range(2)]
        s_tp = sem("x_transposed")
        s_xt = [sem("x_t_even_done"), sem("x_t_odd_done")]
        s_xh, s_xl = sem("x_high"), sem("x_low")
        s_gu = sem("gate_up_done")
        s_silu = sem("silu_done2")
        s_act = sem("act_done")
        s_ah, s_al = sem("act_high"), sem("act_low")
        s_y = sem("y_done")
        s_yc = sem("y_copied")
        s_ys = [sem(f"y_stored{b}") for b in range(2)]
        one = sem("always_one")

        block = ctx.enter_context(nc.Block())

        def bound(eng):
            return eng.value_load(n_pairs[0:1, 0:1], min_val=CHUNKS, max_val=PAIRS_MAX)

        @block.sync
        def _(sp):
            def entry(it, what, top):
                return sp.value_load(tile_list[0:1, bass.ds(it * 2 + what, 1)], min_val=0, max_val=top)

            def pair_of(it):
                return (entry(it, 0, CHUNKS - 1), entry(it, 1, (E_N - 2) * REGION + REGION - SLOT_TILE))

            def load_rows(pair, b, to, loaded):
                start = pair[1]
                s = start + b * REGION
                n = SLOT_TILE // P
                sp.dma_start(to[b][:, 0:n], d["slots"][bass.ds(s, n * P), :].rearrange("(p j) o -> p (j o)", p=P)
                             ).then_inc(loaded[b], 16)
                sp.dma_start(to[b][0:SLOT_TILE - n * P, n:n + 1], d["slots"][bass.ds(s + n * P, SLOT_TILE - n * P), :]
                             ).then_inc(loaded[b], 16)

            n = bound(sp)
            pair = pair_of(0)
            for b in range(2):
                load_rows(pair, b, rows_g, s_rg)
            for b in range(2):
                load_rows(pair, b, rows_i, s_ri)
            with sp.Fori(0, n) as it:
                pair = pair_of(it + 1)
                for b in range(2):
                    g = it * 2 + b
                    wait_apart(sp, s_wgl, g + 1, one)
                    sp.wait_ge(s_wdl, g + 1)
                    load_expert(sp, d, keep, pair[0] * 2 + b, b)
                    wait_apart(sp, s_tok, g + 1, one)
                    load_rows(pair, b, rows_g, s_rg)
                    if b == 0:
                        wait_apart(sp, s_cgl, it + 1, one)
                        sp.wait_ge(s_cdl, it + 1)
                        load_chunk(sp, d, keep, pair[0])
                    else:
                        for h in range(2):
                            wait_apart(sp, s_ys[h], it * 48 + 48, one)
                            load_rows(pair, h, rows_i, s_ri)
            lists, gate_ups, downs, stored = (sp.to_reg(v) for v in (n * 32 + 32, n * 16 + 16, n * 48 + 48, n * 48))
            wait_apart(sp, s_c, lists, one)
            for b in range(2):
                sp.wait_ge(s_wgu[b], gate_ups)
                sp.wait_ge(s_wd[b], downs)
                sp.wait_ge(s_rg[b], lists)
                sp.wait_ge(s_ri[b], lists)
                sp.wait_ge(s_ys[b], stored)

        @block.gpsimd
        def _(pool):
            def gather(g, b):
                wait_apart(pool, s_tok, g + 1, one)
                for j, (s0, n) in enumerate(SUBS):
                    nc.gpsimd.indirect_dma_start(
                        out=x_g[b][0:n, j, :], out_offset=None, in_=d["x_norm"],
                        in_offset=bass.IndirectOffsetOnAxis(ap=toks_i[b][0:n, j:j + 1], axis=0)).then_inc(s_xg[b], 16)

            pool.sem_inc(one, 1)
            n = bound(pool)
            gather(0, 0)
            with pool.Fori(0, n) as it:
                for b in range(2):
                    g = it * 2 + b
                    gather(g + 1, 1 - b)
                    for j, (s0, m) in enumerate(SUBS):
                        wait_apart(pool, s_yc, g * 3 + j + 1, one)
                        nc.gpsimd.indirect_dma_start(
                            out=d["y_rows"], out_offset=bass.IndirectOffsetOnAxis(ap=rows_i[b][0:m, j:j + 1], axis=0),
                            in_=y_sb[b][0:m, j, :], in_offset=None).then_inc(s_ys[b], 16)

        @block.scalar
        def _(act):
            def weights_high(pair, b):
                act.wait_ge(s_wgu[b], pair * 16 + 16)
                nc.scalar.activation(w_gu_p[b][:, 0], w_gu[b][:, :, :], ACT.Copy).then_inc(s_wgh, 1)
                act.wait_ge(s_wd[b], pair * 48 + 48)
                nc.scalar.activation(w_d_p[b][:, 0], w_d[b][:, :, :], ACT.Copy).then_inc(s_wdh, 1)

            def chunk_gu_high(it):
                act.wait_ge(s_c, it * 32 + 32)
                nc.scalar.activation(c_gu_p[:, 0], c_gu[:, :, :], ACT.Copy).then_inc(s_cgh, 1)

            def modulate(g, k):
                act.wait_ge(s_tp, g * KT + k + 1)
                nc.scalar.activation(x_t[:, k], tp[k % 2][:, 0:SLOT_TILE], ACT.Identity, bias=mod_col[:, 2, k:k + 1],
                                     scale=mod_col[:, 3, k:k + 1]).then_inc(s_xt[0], 1)

            def x_high(g, half):
                for odd in range(2):
                    act.wait_ge(s_xt[odd], g * 2 + half + 1)
                ks = slice(2 * half, 2 * half + 2)
                nc.scalar.activation(x_p[:, 0, ks], x_t[:, ks], ACT.Copy).then_inc(s_xh, 1)

            def gate(g, j):
                act.wait_ge(s_gu, g * 5 + (1, 3, 4)[j])
                rows = slice(0, I_REST) if j == 1 else slice(0, P)
                nc.scalar.activation(gated[rows, j], gu[(0, 2, 3)[j]][rows, 0:SLOT_TILE], ACT.Silu).then_inc(s_silu, 1)

            def act_high(g, j):
                rows = slice(0, I_REST) if j == 1 else slice(0, P)
                act.wait_ge(s_act, g * 3 + j + 1)
                nc.scalar.activation(a_p[rows, j, 0], act_t[rows, j], ACT.Copy).then_inc(s_ah, 1)

            n = bound(act)
            weights_high(0, 0)
            chunk_gu_high(0)
            for half in range(2):
                modulate(0, 2 * half)
                x_high(0, half)
            with act.Fori(0, n) as it:
                for b in range(2):
                    g = it * 2 + b
                    weights_high(it + b, 1 - b)
                    if b == 0:
                        act.wait_ge(s_c, it * 32 + 32)
                        nc.scalar.activation(c_d_p[:, 0], c_d[:, :], ACT.Copy).then_inc(s_cdh, 1)
                    gate(g, 0)
                    act_high(g, 0)
                    gate(g, 1)
                    act_high(g, 1)
                    gate(g, 2)
                    act.wait_ge(s_xl, g * 2 + 2)
                    modulate(g + 1, 0)
                    act_high(g, 2)
                    x_high(g + 1, 0)
                    modulate(g + 1, 2)
                    act.wait_ge(s_ri[b], it * 32 + 32)
                    for i, (s0, m) in enumerate(SUBS):
                        act.wait_ge(s_y, g * 3 + i + 1)
                        nc.scalar.activation(y_sb[b][0:m, i, :], yb[i][0:m, :], ACT.Copy).then_inc(s_yc, 1)
                        if i == 0:
                            x_high(g + 1, 1)
                            if b == 1:
                                chunk_gu_high(it + 1)

        @block.vector
        def _(dve):
            def low(part, whole, high, done):
                nc.vector.tensor_tensor(part, whole, high, ALU.subtract).then_inc(done, 1)

            def weights_low(g, b):
                dve.wait_ge(s_wgh, g + 1)
                low(w_gu_p[b][:, 1], w_gu[b][:, :, :], w_gu_p[b][:, 0], s_wgl)
                dve.wait_ge(s_wdh, g + 1)
                low(w_d_p[b][:, 1], w_d[b][:, :, :], w_d_p[b][:, 0], s_wdl)

            def chunk_gu_low(it):
                dve.wait_ge(s_cgh, it + 1)
                low(c_gu_p[:, 1], c_gu[:, :, :], c_gu_p[:, 0], s_cgl)

            def modulate(g, k):
                dve.wait_ge(s_tp, g * KT + k + 1)
                nc.vector.tensor_scalar(x_t[:, k], tp[k % 2][:, 0:SLOT_TILE], mod_col[:, 3, k:k + 1], mod_col[:, 2, k:k + 1],
                                        ALU.mult, ALU.add).then_inc(s_xt[1], 1)

            def x_low(g, half):
                dve.wait_ge(s_xh, g * 2 + half + 1)
                ks = slice(2 * half, 2 * half + 2)
                low(x_p[:, 1, ks], x_t[:, ks], x_p[:, 0, ks], s_xl)

            def tokens(pair, b):
                dve.wait_ge(s_rg[b], pair * 32 + 32)
                for j, (s0, n) in enumerate(SUBS):
                    last = nc.vector.tensor_scalar(toks_i[b][0:n, j:j + 1], rows_g[b][0:n, j:j + 1], 2, None,
                                                   ALU.logical_shift_right)
                last.then_inc(s_tok, 1)

            tokens(0, 0)
            tokens(0, 1)
            weights_low(0, 0)
            chunk_gu_low(0)
            for half in range(2):
                modulate(0, 2 * half + 1)
                x_low(0, half)
            n = bound(dve)
            with dve.Fori(0, n) as it:
                for b in range(2):
                    g = it * 2 + b
                    weights_low(g + 1, 1 - b)
                    for j in range(3):
                        rows = slice(0, I_REST) if j == 1 else slice(0, P)
                        dve.wait_ge(s_silu, g * 3 + j + 1)
                        dve.wait_ge(s_gu, g * 5 + (2, 3, 5)[j])
                        if j == 2:
                            nc.vector.scalar_tensor_tensor(act_t[:, 2], gated[:, 2], SMALL_SCALE, gu[4][:, 0:SLOT_TILE],
                                                           ALU.mult, ALU.mult).then_inc(s_act, 1)
                        else:
                            up = gu[1][:, 0:SLOT_TILE] if j == 0 else gu[2][I_REST:P, 0:SLOT_TILE]
                            nc.vector.tensor_tensor(act_t[rows, j], gated[rows, j], up, ALU.mult).then_inc(s_act, 1)
                        if j == 2:
                            modulate(g + 1, 1)
                        dve.wait_ge(s_ah, g * 3 + j + 1)
                        if j == 1:
                            low(a_p[I_REST:P, 1, 0], act_t[rows, 1], a_p[rows, 1, 0], s_al)
                        else:
                            low(a_p[:, j, 1], act_t[:, j], a_p[:, j, 0], s_al)
                        if j == 1 and b == 0:
                            dve.wait_ge(s_cdh, it + 1)
                            low(c_d_p[:, 1], c_d[:, :], c_d_p[:, 0], s_cdl)
                    x_low(g + 1, 0)
                    modulate(g + 1, 3)
                    x_low(g + 1, 1)
                    if b == 1:
                        chunk_gu_low(it + 1)
                    dve.wait_ge(s_xg[b], it * 48 + 48)
                    tokens(it + 1, b)

        @block.tensor
        def _(pe):
            def transpose_x(g, b, k):
                if k >= 2:
                    pe.wait_ge(s_xt[k % 2], g * 2 + 1)
                for j, (s0, n) in enumerate(SUBS):
                    last = nc.tensor.transpose(tp[k % 2][:, s0:s0 + n], x_g[b][0:n, j, k * P:(k + 1) * P], ident[0:n, 0:n])
                last.then_inc(s_tp, 1)

            n = bound(pe)
            pe.wait_ge(s_xg[0], 48)
            for k in range(KT):
                transpose_x(0, 0, k)
            THREE = ((0, 0), (0, 1), (1, 0))
            with pe.Fori(0, n) as it:
                for b in range(2):
                    g = it * 2 + b
                    pe.wait_ge(s_wgl, g + 1)
                    pe.wait_ge(s_xl, g * 2 + 2)
                    for j, (which, c0, cols) in enumerate(JOBS_GU):
                        if j == 3 and b == 0:
                            pe.wait_ge(s_cgl, it + 1)
                        w = w_gu_p[b] if which == "big" else c_gu_p
                        for k in range(KT):
                            for wp, xp in THREE:
                                last = nc.tensor.matmul(gu[j][:, 0:SLOT_TILE], w[:, wp, k, c0:c0 + cols], x_p[:, xp, k],
                                                        start=(k == 0 and (wp, xp) == (0, 0)),
                                                        stop=(k == KT - 1 and (wp, xp) == (1, 0)))
                        last.then_inc(s_gu, 1)
                    pe.wait_ge(s_xg[1 - b], (it + b) * 48 + 48)
                    pe.wait_ge(s_act, g * 3 + 1)
                    transpose_x(g + 1, 1 - b, 0)
                    transpose_x(g + 1, 1 - b, 1)
                    pe.wait_ge(s_wdl, g + 1)
                    for i, (s0, m) in enumerate(SUBS):
                        rows = slice(s0, s0 + m)
                        for j in range(3):
                            if i == 0:
                                if j:
                                    transpose_x(g + 1, 1 - b, j + 1)
                                pe.wait_ge(s_al, g * 3 + j + 1)
                                if j == 2 and b == 0:
                                    pe.wait_ge(s_cdl, it + 1)
                            w = c_d_p if j == 2 else w_d_p[b][:, :, j]
                            if j == 1:
                                nc.tensor.matmul(yb[i][0:m, :], a_p[:, 1, 0, rows], w[:, 0], start=False, stop=False)
                                nc.tensor.matmul(yb[i][0:m, :], a_p[0:I_REST, 1, 0, rows], w[0:I_REST, 1],
                                                 start=False, stop=False)
                            else:
                                for ap, wp in THREE:
                                    last = nc.tensor.matmul(yb[i][0:m, :], a_p[:, j, ap, rows], w[:, wp],
                                                            start=(j == 0 and (ap, wp) == (0, 0)),
                                                            stop=(j == 2 and (ap, wp) == (1, 0)))
                        last.then_inc(s_y, 1)


def combine(nc, d, keep):
    with ExitStack() as ctx:
        sb = lambda name, shape, dt=F32: ctx.enter_context(nc.sbuf_tensor(name, shape, dt))
        sem = lambda name: ctx.enter_context(nc.semaphore(name))
        x_all, gate_row, weights = (keep[n] for n in ("x_all", "gate_row", "weights"))
        BUFS = 4
        y_in = [sb(f"y_in{b}", [P, TOP, D]) for b in range(BUFS)]
        acc = [sb(f"acc{b}", [P, D]) for b in range(2)]
        res = [sb(f"res{b}", [P, D]) for b in range(2)]
        s_in = [sem(f"y_in{b}_loaded") for b in range(BUFS)]
        s_w0 = sem("first_weighed")
        s_acc = sem("weighed")
        s_gate = sem("gated_done")
        s_res = sem("result_done")
        s_out = [sem(f"out{b}_stored") for b in range(2)]
        block = ctx.enter_context(nc.Block())
        y_view = d["y_rows"][0:ROWS, :].rearrange("(t p k) n -> t p k n", p=P, k=TOP)

        @block.sync
        def _(sp):
            for t in range(TT):
                if t >= BUFS:
                    sp.wait_ge(s_acc, 3 * (t - BUFS) + 3)
                sp.dma_start(y_in[t % BUFS][:, :, :], y_view[t]).then_inc(s_in[t % BUFS], 16)

        @block.scalar
        def _(act):
            for t in range(TT):
                act.wait_ge(s_in[t % BUFS], 16 * (t // BUFS) + 16)
                if t >= 2:
                    act.wait_ge(s_gate, t - 1)
                nc.scalar.activation(acc[t % 2][:, :], y_in[t % BUFS][:, 0, :], ACT.Copy,
                                     scale=weights[:, 0, t:t + 1]).then_inc(s_w0, 1)
                if t:
                    act.wait_ge(s_res, t)
                    act.dma_start(d["out"][(t - 1) * P:t * P, :], res[(t - 1) % 2][:, :]).then_inc(s_out[(t - 1) % 2], 16)
            act.wait_ge(s_res, TT)
            act.dma_start(d["out"][(TT - 1) * P:TT * P, :], res[(TT - 1) % 2][:, :]).then_inc(s_out[(TT - 1) % 2], 16)
            for b in range(2):
                act.wait_ge(s_out[b], 16 * TT // 2)

        @block.vector
        def _(dve):
            def finish(t):
                dve.wait_ge(s_gate, t + 1)
                if t >= 2:
                    dve.wait_ge(s_out[t % 2], 16 * (t // 2))
                nc.vector.tensor_tensor(res[t % 2][:, :], acc[t % 2][:, :], x_all[:, t], ALU.add).then_inc(s_res, 1)

            for t in range(TT):
                dve.wait_ge(s_w0, t + 1)
                dve.wait_ge(s_in[t % BUFS], 16 * (t // BUFS) + 16)
                for k in range(1, TOP):
                    if k > 1:
                        dve.wait_ge(s_acc, 3 * t + k - 1)
                    nc.vector.scalar_tensor_tensor(acc[t % 2][:, :], y_in[t % BUFS][:, k], weights[:, k, t:t + 1],
                                                   acc[t % 2][:, :], ALU.mult, ALU.add).then_inc(s_acc, 1)
                if t:
                    finish(t - 1)
            finish(TT - 1)

        @block.gpsimd
        def _(pool):
            for t in range(TT):
                pool.wait_ge(s_acc, 3 * t + 3)
                nc.gpsimd.tensor_tensor(acc[t % 2][:, :], acc[t % 2][:, :], gate_row[:, 1], ALU.mult).then_inc(s_gate, 1)


def adaln_moe_kernel(nc, d):
    scratch = lambda name, shape, dt=F32: nc.dram_tensor(name, shape, dt, kind="Internal").ap()
    d = dict(d)
    d["qk_parts"] = scratch("qk_parts", (2, 2, D, T))
    d["slots"] = scratch("slots", (ALL_SLOTS, 1), I32)
    d["x_norm"] = scratch("x_norm", (T + P // 4, D))
    d["tiles"] = scratch("tiles", (LISTED, 2), I32)
    d["y_rows"] = scratch("y_rows", (ROWS + P, D))
    with ExitStack() as ctx:
        sb = lambda name, shape, dt=F32: ctx.enter_context(nc.sbuf_tensor(name, shape, dt))
        keep = {
            "ident": sb("ident", [P, P]),
            "mod_col": sb("mod_col", [P, 4, KT]),
            "gate_row": sb("gate_row", [P, 2, D]),
            "silu_c": sb("silu_c", [P, KT]),
            "silu_cb": sb("silu_cb", [P, KT, P]),
            "x_all": sb("x_all", [P, TT, D]),
            "weights": sb("weights", [P, TOP, TT]),
            "tile_list": sb("tile_list", [1, 2 * LISTED], I32),
            "n_pairs": sb("n_pairs", [P, 1], I32),
        }
        with ExitStack() as early:
            v_all = early.enter_context(nc.sbuf_tensor("v_all", [P, TT, H, DH + 1], F32))
            keep["v_all"] = v_all
            modulation_and_projection(nc, d, keep)
            attention(nc, d, keep)
        keep.update(weight_buffers(nc, ctx))
        route(nc, d, keep)
        experts(nc, d, keep)
        combine(nc, d, keep)


def rotary_tables():
    inv = (np.float32(1.0) / np.float32(10000.0) ** (np.arange(0, DH, 2, dtype=np.float32) / np.float32(DH)))
    angle = np.outer(np.arange(T, dtype=np.float32), inv.astype(np.float32)).astype(np.float32).T
    cos, sin = np.cos(angle).astype(np.float32), np.sin(angle).astype(np.float32)
    return np.concatenate([cos, cos]), np.concatenate([-sin, sin])


def kernel(**inputs):
    import concourse.bacc as bacc
    from concourse.bass_utils import run_bass_kernel_spmd

    a = {n: np.asarray(v) for n, v in inputs.items()}
    cos, sin = rotary_tables()
    bias = a["L0_attn_Wqkv_b"]
    gate_up = lambda g, u: [g[..., :P], u[..., :P]] + ([g[..., P:], u[..., P:]] if g.shape[-1] > P else [])
    arrays = {
        "x": a["L0_attn_x"].reshape(T, D),
        "w_t": a["L0_attn_Wqkv_w"].T,
        "b_qk": bias[:2 * D].reshape(8, P).T,
        "b_v": bias[2 * D:],
        "wmod": a["L0_wmod"],
        "c_col": a["L0_c"].reshape(KT, P).T,
        "cos": cos,
        "sin": sin,
        "gate_t": a["L0_ffn_gate_w"].T,
        "w_gu": np.concatenate(gate_up(a["L0_ffn_Wg"], a["L0_ffn_Wu"]), axis=-1),
        "w_d": a["L0_ffn_Wd"],
        "w_gu_s": np.concatenate(gate_up(a["L0_ffn_cWg"], a["L0_ffn_cWu"]), axis=-1),
        "w_d_s": a["L0_ffn_cWd"],
    }
    arrays = {n: np.ascontiguousarray(v) for n, v in arrays.items()}
    nc = bacc.Bacc("TRN2", target_bir_lowering=False, num_devices=1)
    d = {n: nc.dram_tensor(f"in_{n}", v.shape, mybir.dt.from_np(v.dtype), kind="ExternalInput").ap() for n, v in arrays.items()}
    d["out"] = nc.dram_tensor("out", (T, D), F32, kind="ExternalOutput").ap()
    adaln_moe_kernel(nc, d)
    r = run_bass_kernel_spmd(nc, [{f"in_{n}": v for n, v in arrays.items()}], core_ids=[0])
    return r.results[0]["out"].reshape(1, T, D)
```
